# Optimizing a Trainium2 kernel written in Bass

```python
import numpy as np
import jax
import jax.numpy as jnp

def _softmax(x, axis=-1):
    return jax.nn.softmax(x, axis=axis)

def _gelu(x):
    return jax.nn.gelu(x, approximate=True)

def _silu(x):
    return jax.nn.silu(x)

def _sigmoid(x):
    return jax.nn.sigmoid(x)

def _layernorm(x, axis=-1, eps=1e-05):
    m = jnp.mean(x, axis=axis, keepdims=True)
    v = jnp.var(x, axis=axis, keepdims=True)
    return (x - m) / jnp.sqrt(v + eps)

def _scatter_add(tgt, idx, src, axis=0):
    return tgt.at[idx].add(src)

def _segment_sum(src, seg, n):
    return jax.ops.segment_sum(src, seg, n)
kernel_name = 'mk_sandwich_d2_jaxref_r8_b87965'

def setup_inputs(seed: int=0):
    np.random.seed(seed)
    _w = jnp.asarray

    def _L0_attn_setup():
        import jax, jax.numpy as jnp
        import numpy as np
        B, N, D = (2, 256, 128)
        H, WS = (16, 128)
        DH = D // H
        HALF = WS // 2
        key = jax.random.key(seed)
        ks = jax.random.split(key, 5)
        return {'x': jax.random.normal(ks[0], (B, N, D), dtype=jnp.float32), 'Wqkv': jax.random.normal(ks[1], (D, 3 * D), dtype=jnp.float32) * 0.02, 'bqkv': jax.random.normal(ks[2], (3 * D,), dtype=jnp.float32) * 0.02, 'Wout': jax.random.normal(ks[3], (D, D), dtype=jnp.float32) * 0.02, 'bout': jax.random.normal(ks[4], (D,), dtype=jnp.float32) * 0.02}
    _L0_attn_in = _L0_attn_setup()

    def _L0_ffn_setup():
        import jax, jax.numpy as jnp
        import numpy as np
        D_MODEL = 128
        D1, D2 = (32, 32)
        F1, F2 = (64, 64)
        E = 64
        TOP_K = 2

        def kmoe(x_flat, W_router, A, B, scale, bias, d_in1, d_in2, d_out1, d_out2, top_k):
            logits = x_flat @ W_router.T
            vals, idx = jax.lax.top_k(logits, top_k)
            probs = jax.nn.softmax(vals, axis=-1)
            xs = x_flat.reshape(-1, d_in1, d_in2)
            Ag = A[idx]
            Bg = B[idx]
            Y = jnp.einsum('nkoi,nij,nkpj->nkop', Ag, xs, Bg)
            out = jnp.einsum('nkop,nk->nop', Y, probs).reshape(-1, d_out1 * d_out2)
            return out * scale + bias
        key = jax.random.key(seed)
        ks = jax.random.split(key, 12)
        s = 0.02
        return {'x': jax.random.normal(ks[0], (4, 256, D_MODEL), dtype=jnp.float32), 'W_up': jax.random.normal(ks[1], (E, D1 * D2), dtype=jnp.float32) * s, 'A_up': jax.random.normal(ks[2], (E, F1, D1), dtype=jnp.float32) * s, 'B_up': jax.random.normal(ks[3], (E, F2, D2), dtype=jnp.float32) * s, 'scale_up': jnp.ones((1,), dtype=jnp.float32), 'bias_up': jnp.zeros((F1 * F2,), dtype=jnp.float32), 'W_down': jax.random.normal(ks[4], (E, F1 * F2), dtype=jnp.float32) * s, 'A_down': jax.random.normal(ks[5], (E, D1, F1), dtype=jnp.float32) * s, 'B_down': jax.random.normal(ks[6], (E, D2, F2), dtype=jnp.float32) * s, 'scale_down': jnp.ones((1,), dtype=jnp.float32), 'bias_down': jnp.zeros((D1 * D2,), dtype=jnp.float32)}
    _L0_ffn_in = _L0_ffn_setup()

    def _L1_attn_setup():
        import jax, jax.numpy as jnp
        import numpy as np
        from jax import lax
        DIM = 128
        INNER = 256
        STATE = 64
        B, T = (4, 256)
        DECAY = 0.95
        INPUT_FACTOR = 0.05
        LN_EPS = 1e-05

        def _layernorm(x, g, b):
            mu = jnp.mean(x, axis=-1, keepdims=True)
            var = jnp.mean(jnp.square(x - mu), axis=-1, keepdims=True)
            return (x - mu) * lax.rsqrt(var + LN_EPS) * g + b
        key = jax.random.key(seed)
        ks = jax.random.split(key, 8)
        s = 0.02
        return {'x': jax.random.normal(ks[0], (B, T, DIM), jnp.float32), 'W_in': jax.random.normal(ks[1], (2 * INNER, DIM), jnp.float32) * s, 'conv_w': jax.random.normal(ks[2], (INNER, 1, 4), jnp.float32) * s, 'conv_b': jax.random.normal(ks[3], (INNER,), jnp.float32) * s, 'W_B': jax.random.normal(ks[4], (STATE, INNER), jnp.float32) * s, 'W_C': jax.random.normal(ks[5], (INNER, STATE), jnp.float32) * s, 'D_param': jax.random.normal(ks[6], (INNER,), jnp.float32) * s, 'W_out': jax.random.normal(ks[7], (DIM, INNER), jnp.float32) * s, 'ln_gamma': jnp.ones((DIM,), jnp.float32), 'ln_beta': jnp.zeros((DIM,), jnp.float32)}
    _L1_attn_in = _L1_attn_setup()

    def _L1_ffn_setup():
        import jax, jax.numpy as jnp
        import numpy as np
        T, Z, D_DIM = (8, 256, 128)
        N_EXP, P_SLOT, H = (64, 32, 128)
        LN_EPS = 1e-05
        key = jax.random.key(seed)
        k = jax.random.split(key, 5)
        s = 0.02
        return {'x': jax.random.normal(k[0], (T, Z, D_DIM), dtype=jnp.float32), 'phi_w': jax.random.normal(k[1], (N_EXP * P_SLOT, D_DIM), dtype=jnp.float32) * s, 'phi_b': jax.random.normal(k[2], (N_EXP * P_SLOT,), dtype=jnp.float32) * s, 'expert_w': jax.random.normal(k[3], (N_EXP, D_DIM, H), dtype=jnp.float32) * s, 'expert_b': jax.random.normal(k[4], (N_EXP, H), dtype=jnp.float32) * s}
    _L1_ffn_in = _L1_ffn_setup()
    _d = {'L0_attn_x': _L0_attn_in['x'], 'L0_attn_Wqkv': _L0_attn_in['Wqkv'], 'L0_attn_bqkv': _L0_attn_in['bqkv'], 'L0_attn_Wout': _L0_attn_in['Wout'], 'L0_attn_bout': _L0_attn_in['bout'], 'L0_ffn_W_up': _L0_ffn_in['W_up'], 'L0_ffn_A_up': _L0_ffn_in['A_up'], 'L0_ffn_B_up': _L0_ffn_in['B_up'], 'L0_ffn_scale_up': _L0_ffn_in['scale_up'], 'L0_ffn_bias_up': _L0_ffn_in['bias_up'], 'L0_ffn_W_down': _L0_ffn_in['W_down'], 'L0_ffn_A_down': _L0_ffn_in['A_down'], 'L0_ffn_B_down': _L0_ffn_in['B_down'], 'L0_ffn_scale_down': _L0_ffn_in['scale_down'], 'L0_ffn_bias_down': _L0_ffn_in['bias_down'], 'L1_attn_W_in': _L1_attn_in['W_in'], 'L1_attn_conv_w': _L1_attn_in['conv_w'], 'L1_attn_conv_b': _L1_attn_in['conv_b'], 'L1_attn_W_B': _L1_attn_in['W_B'], 'L1_attn_W_C': _L1_attn_in['W_C'], 'L1_attn_D_param': _L1_attn_in['D_param'], 'L1_attn_W_out': _L1_attn_in['W_out'], 'L1_attn_ln_gamma': _L1_attn_in['ln_gamma'], 'L1_attn_ln_beta': _L1_attn_in['ln_beta'], 'L1_ffn_phi_w': _L1_ffn_in['phi_w'], 'L1_ffn_phi_b': _L1_ffn_in['phi_b'], 'L1_ffn_expert_w': _L1_ffn_in['expert_w'], 'L1_ffn_expert_b': _L1_ffn_in['expert_b']}
    _x0 = _d['L0_attn_x']
    _d['L0_attn_x'] = jax.random.normal(jax.random.fold_in(jax.random.key(seed), 1), (1, 2048, 128), dtype=_x0.dtype)
    del _x0
    return _d

def reference(L0_attn_x, L0_attn_Wqkv, L0_attn_bqkv, L0_attn_Wout, L0_attn_bout, L0_ffn_W_up, L0_ffn_A_up, L0_ffn_B_up, L0_ffn_scale_up, L0_ffn_bias_up, L0_ffn_W_down, L0_ffn_A_down, L0_ffn_B_down, L0_ffn_scale_down, L0_ffn_bias_down, L1_attn_W_in, L1_attn_conv_w, L1_attn_conv_b, L1_attn_W_B, L1_attn_W_C, L1_attn_D_param, L1_attn_W_out, L1_attn_ln_gamma, L1_attn_ln_beta, L1_ffn_phi_w, L1_ffn_phi_b, L1_ffn_expert_w, L1_ffn_expert_b):

    def _L0_attn_ref(x, Wqkv, bqkv, Wout, bout):
        import jax, jax.numpy as jnp
        import numpy as np
        B, N, D = (2, 256, 128)
        H, WS = (16, 128)
        DH = D // H
        HALF = WS // 2
        b, n, d = x.shape
        scale = DH ** (-0.5)
        qkv = x @ Wqkv + bqkv
        q, k, v = jnp.split(qkv, 3, axis=-1)

        def heads(t):
            return t.reshape(b, n, H, DH).transpose(0, 2, 1, 3)
        q, k, v = (heads(q), heads(k), heads(v))
        scores = jnp.einsum('bhid,bhjd->bhij', q, k) * scale
        idx = jnp.arange(n)
        band = jnp.abs(idx[:, None] - idx[None, :]) <= HALF
        neg = jnp.asarray(jnp.finfo(scores.dtype).min, scores.dtype)
        scores = jnp.where(band[None, None], scores, neg)
        attn = jax.nn.softmax(scores, axis=-1)
        out = jnp.einsum('bhij,bhjd->bhid', attn, v)
        out = out.transpose(0, 2, 1, 3).reshape(b, n, d)
        return out @ Wout + bout

    def _L0_ffn_ref(x, W_up, A_up, B_up, scale_up, bias_up, W_down, A_down, B_down, scale_down, bias_down):
        import jax, jax.numpy as jnp
        import numpy as np
        D_MODEL = 128
        D1, D2 = (32, 32)
        F1, F2 = (64, 64)
        E = 64
        TOP_K = 2

        def kmoe(x_flat, W_router, A, B, scale, bias, d_in1, d_in2, d_out1, d_out2, top_k):
            logits = x_flat @ W_router.T
            vals, idx = jax.lax.top_k(logits, top_k)
            probs = jax.nn.softmax(vals, axis=-1)
            xs = x_flat.reshape(-1, d_in1, d_in2)
            Ag = A[idx]
            Bg = B[idx]
            Y = jnp.einsum('nkoi,nij,nkpj->nkop', Ag, xs, Bg)
            out = jnp.einsum('nkop,nk->nop', Y, probs).reshape(-1, d_out1 * d_out2)
            return out * scale + bias
        orig_shape = x.shape
        x_flat = x.reshape(-1, D1 * D2)
        h = kmoe(x_flat, W_up, A_up, B_up, scale_up, bias_up, D1, D2, F1, F2, TOP_K)
        h = jax.nn.gelu(h, approximate=False)
        y = kmoe(h, W_down, A_down, B_down, scale_down, bias_down, F1, F2, D1, D2, TOP_K)
        return y.reshape(*orig_shape[:-1], D_MODEL)

    def _L1_attn_ref(x, W_in, conv_w, conv_b, W_B, W_C, D_param, W_out, ln_gamma, ln_beta):
        import jax, jax.numpy as jnp
        import numpy as np
        from jax import lax
        DIM = 128
        INNER = 256
        STATE = 64
        B, T = (4, 256)
        DECAY = 0.95
        INPUT_FACTOR = 0.05
        LN_EPS = 1e-05

        def _layernorm(x, g, b):
            mu = jnp.mean(x, axis=-1, keepdims=True)
            var = jnp.mean(jnp.square(x - mu), axis=-1, keepdims=True)
            return (x - mu) * lax.rsqrt(var + LN_EPS) * g + b
        Bn, Tn, Dn = x.shape
        x_proj = jnp.einsum('btd,ed->bte', x, W_in)
        x_input, x_gate = jnp.split(x_proj, 2, axis=-1)
        xc = lax.conv_general_dilated(x_input.transpose(0, 2, 1), conv_w, window_strides=(1,), padding=[(3, 0)], feature_group_count=INNER) + conv_b[None, :, None]
        u = jax.nn.silu(xc).transpose(0, 2, 1)
        Bu = jnp.einsum('btc,sc->bts', u, W_B)

        def step(h, bu_t):
            h = DECAY * h + INPUT_FACTOR * bu_t
            return (h, h)
        h0 = jnp.zeros((Bn, STATE), x.dtype)
        _, hs = lax.scan(step, h0, Bu.transpose(1, 0, 2))
        hs = hs.transpose(1, 0, 2)
        y = jnp.einsum('bts,cs->btc', hs, W_C) + D_param * u
        y = y * jax.nn.silu(x_gate)
        y = jnp.einsum('btc,dc->btd', y, W_out)
        return _layernorm(y + x, ln_gamma, ln_beta)

    def _L1_ffn_ref(x, phi_w, phi_b, expert_w, expert_b):
        import jax, jax.numpy as jnp
        import numpy as np
        T, Z, D_DIM = (8, 256, 128)
        N_EXP, P_SLOT, H = (64, 32, 128)
        LN_EPS = 1e-05
        t, z, d = x.shape
        n = expert_w.shape[0]
        p = phi_w.shape[0] // n
        logits = (jnp.einsum('tzd,ed->tze', x, phi_w) + phi_b).reshape(t, z, n, p)
        D = jax.nn.softmax(logits, axis=3)
        C = jax.nn.softmax(logits, axis=2)
        X_tilde = jnp.einsum('tznp,tzd->npd', D, x)
        X_tilde = jnp.clip(X_tilde, -33000.0, 65000.0)
        mu = jnp.mean(X_tilde, axis=-1, keepdims=True)
        var = jnp.mean(jnp.square(X_tilde - mu), axis=-1, keepdims=True)
        X_tilde = (X_tilde - mu) * jax.lax.rsqrt(var + LN_EPS)
        X_tilde = jnp.tanh(X_tilde)
        Y_tilde = jnp.einsum('npd,ndH->npH', X_tilde, expert_w) + expert_b[:, None, :]
        Y = jnp.einsum('tznp,npH->tzH', C, Y_tilde)
        return Y
    x = L0_attn_x
    x = x + _layernorm(_L0_attn_ref(_layernorm(x, axis=-1), L0_attn_Wqkv, L0_attn_bqkv, L0_attn_Wout, L0_attn_bout), axis=-1)
    x = x + _layernorm(_L0_ffn_ref(_layernorm(x, axis=-1), L0_ffn_W_up, L0_ffn_A_up, L0_ffn_B_up, L0_ffn_scale_up, L0_ffn_bias_up, L0_ffn_W_down, L0_ffn_A_down, L0_ffn_B_down, L0_ffn_scale_down, L0_ffn_bias_down), axis=-1)
    x = x + _layernorm(_L1_attn_ref(_layernorm(x, axis=-1), L1_attn_W_in, L1_attn_conv_w, L1_attn_conv_b, L1_attn_W_B, L1_attn_W_C, L1_attn_D_param, L1_attn_W_out, L1_attn_ln_gamma, L1_attn_ln_beta), axis=-1)
    x = x + _layernorm(_L1_ffn_ref(_layernorm(x, axis=-1), L1_ffn_phi_w, L1_ffn_phi_b, L1_ffn_expert_w, L1_ffn_expert_b), axis=-1)
    return x

_drawn_inputs = setup_inputs


def setup_inputs(seed=0):
    import zlib

    import numpy as np

    out = dict(_drawn_inputs(seed))
    spreads = {'L0_ffn_bias_up': (0.0, 0.8),
     'L0_ffn_bias_down': (0.0, 0.1),
     'L1_attn_ln_gamma': (1.0, 0.2),
     'L1_attn_ln_beta': (0.0, 0.1)}
    factors = {'L0_ffn_W_up': 8.0,
     'L0_ffn_A_up': 8.0,
     'L0_ffn_B_up': 8.0,
     'L0_ffn_W_down': 8.0,
     'L0_ffn_A_down': 8.0,
     'L0_ffn_B_down': 8.0,
     'L1_attn_W_in': 8.0,
     'L1_attn_conv_w': 8.0,
     'L1_attn_conv_b': 8.0,
     'L1_attn_W_B': 8.0,
     'L1_attn_W_C': 8.0,
     'L1_attn_D_param': 8.0,
     'L1_attn_W_out': 8.0,
     'L1_ffn_phi_w': 4.661,
     'L1_ffn_phi_b': 27.973}
    for name, (base, spread) in spreads.items():
        noise = np.random.default_rng([zlib.crc32(name.encode()), seed]).standard_normal(out[name].shape)
        drawn = base * np.exp(spread * noise) if base else spread * noise
        out[name] = jnp.asarray(drawn.astype(out[name].dtype))
    for name, factor in factors.items():
        out[name] = (out[name] * factor).astype(out[name].dtype)
    return out
```

```python
from contextlib import ExitStack

import concourse.bass as bass
from concourse import mybir

F32 = mybir.dt.float32
BF16 = mybir.dt.bfloat16
I32 = mybir.dt.int32
U32 = mybir.dt.uint32
ALU = mybir.AluOpType
ACT = mybir.ActivationFunctionType
AX_X = mybir.AxisListType.X

P = 128
NEG = -1.0e30
EPS = 1e-5


class Count:

    def __init__(self, sem):
        self.sem, self.n = sem, 0

    def up(self, ins):
        ins.then_inc(self.sem, 1)
        self.n += 1
        return self.n

    def settle(self, eng):
        eng.wait_ge(self.sem, self.n)


class Alloc:

    def __init__(self, nc, ctx, tag, cleared=None):
        self.nc, self.ctx, self.tag, self.cleared = nc, ctx, tag, cleared

    def sb(self, name, shape, dt=F32):
        return self.ctx.enter_context(self.nc.sbuf_tensor(f"{self.tag}_{name}", shape, dt))

    def ps(self, name, shape, dt=F32):
        return self.ctx.enter_context(self.nc.psum_tensor(f"{self.tag}_{name}", shape, dt))

    def sem(self, name):
        if self.cleared is not None:
            self.cleared.append(self.nc.alloc_semaphore(name=f"{self.tag}_{name}"))
            return self.cleared[-1]
        return self.ctx.enter_context(self.nc.semaphore(f"{self.tag}_{name}"))


class Norm:

    def __init__(self, nc, a, name, nt):
        self.nc, self.nt = nc, nt
        self.stats = a.sb(f"{name}_stats", [P, nt, 6])
        self.tmp = a.sb(f"{name}_tmp", [P, 8, nt])
        self.chain = Count(a.sem(f"{name}_chain"))
        self.var_ready = a.sem(f"{name}_var")
        self.std_ready = a.sem(f"{name}_std")

    def tile_stats(self, t, src):
        self.chain.up(self.nc.vector.bn_stats(self.stats[:, t, :], src))

    def finish(self, dve, t0=0, t1=None, mark=0):
        t1 = self.nt if t1 is None else t1
        v, tmp, st = self.nc.vector, self.tmp, self.stats
        col = lambda k: tmp[:, k, t0:t1]
        self.chain.settle(dve)
        me, mo, se, so = (st[:, t0:t1, k] for k in (1, 4, 2, 5))
        v.tensor_tensor(col(0), me, mo, ALU.add)
        v.tensor_tensor(col(1), me, mo, ALU.subtract)
        self.chain.up(v.tensor_tensor(col(3), se, so, ALU.add))
        self.chain.settle(dve)
        v.tensor_scalar(col(2), col(0), 0.5, None, ALU.mult)
        self.chain.up(v.scalar_tensor_tensor(out=col(4), in0=col(1), scalar=0.25, in1=col(1), op0=ALU.mult, op1=ALU.mult))
        self.chain.up(v.tensor_scalar(col(3), col(3), 1.0 / P, EPS, ALU.mult, ALU.add))
        self.chain.settle(dve)
        v.tensor_tensor(col(5), col(3), col(4), ALU.add).then_inc(self.var_ready, 1)
        dve.wait_ge(self.std_ready, mark + 1)
        self.chain.up(v.reciprocal(col(6), col(7)))
        self.chain.settle(dve)

    def root(self, act, t0=0, t1=None, mark=0):
        t1 = self.nt if t1 is None else t1
        act.wait_ge(self.var_ready, mark + 1)
        self.nc.scalar.activation(self.tmp[:, 7, t0:t1], self.tmp[:, 5, t0:t1], ACT.Sqrt).then_inc(self.std_ready, 1)

    def scale(self, t, dst, src):
        return self.nc.vector.tensor_scalar(dst, src, self.tmp[:, 2, t:t + 1], self.tmp[:, 6, t:t + 1],
                                            ALU.subtract, ALU.mult)


def attention(nc, x, c, d):
    H, DH, T = 16, 8, 2048
    NT = T // P
    NG, GH = 4, 4
    NP = H // 2
    NS = NT + 1
    TERMS_Q, TERMS_K = "hhmmhl", "hmhmlh"
    scale = DH ** -0.5

    with ExitStack() as ctx:
        used = []
        a = Alloc(nc, ctx, "at", used)
        qs = a.sb("q_stack", [P, NP, NS * P], BF16)
        ks = a.sb("k_stack", [P, NP, (NT + 2) * P], BF16)
        v9 = a.sb("v_and_one", [P, NT + 2, H, DH + 1])
        a_t = a.sb("attn_t", [P, NS * P])
        wout = a.sb("wout", [P, P])
        bout = a.sb("bout", [P, P])
        ln_y = Norm(nc, a, "ln_y", NT)
        stacked = a.sem("stacked")
        psum = a.ps("psum", [P, 8, 512])

        with ExitStack() as ctx0:
            b = Alloc(nc, ctx0, "pr", used)
            xn = b.sb("xn", [P, NT, P])
            xt = b.sb("xt", [P, T])
            wqkv = b.sb("wqkv", [P, 3 * P])
            bqk = b.sb("bqk", [P, 2])
            bq_s = b.sb("bq_scaled", [P, 1])
            bv = b.sb("bv", [P, P])
            full = b.sb("full", [P, 2, T])
            rest = b.sb("rest", [P, 2, T])
            part = {k: b.sb(f"part_{k}", [P, 2, T], BF16) for k in "hml"}
            flags = b.sb("flags", [16, NP * P], BF16)
            ln = Norm(nc, b, "ln_x", NT)
            loaded = b.sem("loaded")
            x_loaded = b.sem("x_loaded")
            filled = b.sem("filled")
            xn_ready = b.sem("xn_ready")
            tp_done = b.sem("tp_done")
            xt_ready = b.sem("xt_ready")
            proj_done = b.sem("proj_done")
            full_ready = b.sem("full_ready")
            hi_ready = b.sem("hi_ready")
            split_done = b.sem("split_done")
            v_ready = b.sem("v_ready")
            bq_ready = b.sem("bq_ready")
            dch = Count(b.sem("dve_chain"))
            NL = 6
            scratch = nc.dram_tensor("parts_scratch", [3, 2, P, T], BF16).ap()
            bounced = b.sem("bounced")
            with nc.Block() as block:
                @block.sync
                def _(sp):
                    sp.dma_start(x[:, :, :], d["x"].rearrange("(t p) c -> p t c", p=P)).then_inc(x_loaded, 16)
                    sp.dma_start(wqkv[:, :], d["wqkv"]).then_inc(loaded, 16)
                    sp.dma_start(bqk[:, :], d["bqkv"][0:2 * P].rearrange("(k p) -> p k", p=P), allow_slow_non_contiguous=True).then_inc(loaded, 16)
                    sp.dma_start(bv[:, :], d["bqkv"][2 * P:].rearrange("(a n) -> a n", a=1).broadcast_to([P, P])).then_inc(loaded, 16)
                    sp.dma_start(wout[:, :], d["wout"]).then_inc(loaded, 16)
                    sp.dma_start(bout[:, :], d["bout"].rearrange("(a n) -> a n", a=1).broadcast_to([P, P])).then_inc(loaded, 16)
                    sp.dma_start(c["ident"][:, :], d["ident"]).then_inc(loaded, 16)
                    sp.wait_ge(filled, 2)
                    for half in range(2):
                        for edge in (0, NT + 1):
                            sp.dma_start(ks[64 * half + 48:64 * half + 64, :, edge * P:(edge + 1) * P],
                                         flags[:, :].rearrange("r (j n) -> r j n", j=NP)).then_inc(stacked, 16)
                    for ch in range(2):
                        cols = slice(1024 * ch, 1024 * ch + 1024)
                        sp.wait_ge(split_done, 4 * ch + 4)
                        for k, kept in part.items():
                            sp.dma_start(scratch["hml".index(k), :, :, cols].rearrange("w p n -> p w n"), kept[:, :, cols]).then_inc(bounced, 16)
                        sp.wait_ge(bounced, 48 * ch + 48)
                        for which, (stack, terms, pad) in enumerate(((qs, TERMS_Q, 64), (ks, TERMS_K, P))):
                            for n, k in enumerate(terms):
                                rows = scratch["hml".index(k), which].rearrange("(j h r) n -> h r j n", j=NP, h=2)
                                for half in range(2):
                                    r0 = 64 * half + 8 * n
                                    sp.dma_start(stack[r0:r0 + 8, :, pad + 1024 * ch:pad + 1024 * ch + 1024], rows[half][:, :, cols])\
                                        .then_inc(stacked, 16)

                @block.gpsimd
                def _(g):
                    nc.gpsimd.memset(flags[:, :], NEG)
                    nc.gpsimd.memset(ks[:, :, :], 0.0)
                    nc.gpsimd.memset(qs[:, :, :], 1.0).then_inc(filled, 2)
                    nc.gpsimd.memset(v9[:, :, :, :], 1.0).then_inc(filled, 1)
                    ch = Count(b.sem("pool_chain"))
                    nc.gpsimd.memset(c["identb"][:, :], 0.0)
                    nc.gpsimd.memset(c["mask"][:, :, :], 0.0)
                    ch.up(nc.gpsimd.memset(c["sel"][:, :, :], 0.0))
                    ch.settle(g)
                    ch.up(nc.gpsimd.affine_select(out=c["identb"][:, :], in_=c["identb"][:, :], compare_op=ALU.not_equal,
                                                  fill=1.0, base=0, pattern=[[-1, P]], channel_multiplier=1))
                    ch.up(nc.gpsimd.affine_select(out=c["mask"][:, :, :], in_=c["mask"][:, :, :], compare_op=ALU.is_ge,
                                                  fill=NEG, base=0, pattern=[[0, 2], [1, 256]], channel_multiplier=-1))
                    ch.settle(g)
                    ch.up(nc.gpsimd.affine_select(out=c["mask"][:, :, :], in_=c["mask"][:, :, :], compare_op=ALU.is_ge,
                                                  fill=NEG, base=P, pattern=[[0, 2], [-1, 256]], channel_multiplier=1))
                    for k in range(3):
                        ch.settle(g)
                        ch.up(nc.gpsimd.affine_select(out=c["sel"][:, :, :], in_=c["sel"][:, :, :], compare_op=ALU.not_equal,
                                                      fill=1.0, base=-H * k, pattern=[[-1, H], [0, P]], channel_multiplier=1))

                @block.vector
                def _(dve):
                    dve.wait_ge(x_loaded, 16)
                    for t in range(NT):
                        ln.tile_stats(t, x[:, t, :])
                    ln.finish(dve)
                    for t in range(NT):
                        ln.scale(t, xn[:, t, :], x[:, t, :]).then_inc(xn_ready, 1)
                    dve.wait_ge(loaded, 16 * NL)
                    nc.vector.tensor_scalar(bq_s[:, :], bqk[:, 0:1], scale, None, ALU.mult).then_inc(bq_ready, 1)
                    dve.wait_ge(filled, 3)
                    for ch in range(4):
                        cols = slice(512 * ch, 512 * ch + 512)
                        dve.wait_ge(proj_done, ch + 1)
                        nc.vector.tensor_tensor(v9[:, 1 + 4 * ch:5 + 4 * ch, :, 0:DH],
                                                psum[:, 4 + ch % 2, :].rearrange("p (t h d) -> p t h d", t=4, h=H),
                                                bv[:, :].rearrange("p (h d) -> p h d", h=H).unsqueeze(1).broadcast_to([P, 4, H, DH]),
                                                ALU.add).then_inc(v_ready, 1)
                        for w in range(2):
                            dve.wait_ge(hi_ready, 2 * ch + w + 1)
                            dch.up(nc.vector.tensor_tensor(rest[:, w, cols], full[:, w, cols], part["h"][:, w, cols], ALU.subtract))
                            dch.settle(dve)
                            dch.up(nc.vector.tensor_copy(part["m"][:, w, cols], rest[:, w, cols]))
                            dch.settle(dve)
                            nc.vector.tensor_tensor(part["l"][:, w, cols], rest[:, w, cols], part["m"][:, w, cols],
                                                    ALU.subtract).then_inc(split_done, 1)

                @block.scalar
                def _(act):
                    ln.root(act)
                    act.wait_ge(bq_ready, 1)
                    for ch in range(4):
                        act.wait_ge(tp_done, ch + 1)
                        nc.scalar.copy(xt[:, 512 * ch:512 * ch + 512], psum[:, ch % 2, :]).then_inc(xt_ready, 1)
                    for ch in range(4):
                        cols = slice(512 * ch, 512 * ch + 512)
                        act.wait_ge(proj_done, ch + 1)
                        nc.scalar.activation(full[:, 0, cols], psum[:, 2, :], ACT.Identity, bias=bq_s[:, 0:1], scale=scale).then_inc(full_ready, 1)
                        nc.scalar.activation(full[:, 1, cols], psum[:, 3, :], ACT.Identity, bias=bqk[:, 1:2], scale=1.0).then_inc(full_ready, 1)
                        for w in range(2):
                            act.wait_ge(full_ready, 2 * ch + w + 1)
                            nc.scalar.copy(part["h"][:, w, cols], full[:, w, cols]).then_inc(hi_ready, 1)

                @block.tensor
                def _(pe):
                    pe.wait_ge(loaded, 16 * NL)
                    for ch in range(4):
                        pe.wait_ge(xn_ready, 4 * ch + 4)
                        if ch >= 2:
                            pe.wait_ge(xt_ready, ch - 1)
                        for t in range(4):
                            last = nc.tensor.transpose(psum[:, ch % 2, P * t:P * t + P], xn[:, 4 * ch + t, :], c["ident"][:, :])
                        last.then_inc(tp_done, 1)
                    for ch in range(4):
                        pe.wait_ge(xt_ready, ch + 1)
                        if ch >= 1:
                            pe.wait_ge(full_ready, 2 * ch)
                        if ch >= 2:
                            pe.wait_ge(v_ready, ch - 1)
                        for w in range(2):
                            nc.tensor.matmul(psum[:, 2 + w, :], wqkv[:, w * P:w * P + P], xt[:, 512 * ch:512 * ch + 512], start=True, stop=True)
                        for t in range(4):
                            last = nc.tensor.matmul(psum[:, 4 + ch % 2, P * t:P * t + P], xt[:, 512 * ch + P * t:512 * ch + P * t + P],
                                                    wqkv[:, 2 * P:3 * P], start=True, stop=True)
                        last.then_inc(proj_done, 1)
        n_stacked = 16 * (2 * 24 + 4)

        with ExitStack() as ctx1:
            b = Alloc(nc, ctx1, "sc", used)
            kw = b.sb("k_window", [P, 2, NP, 2 * P], BF16)
            qw = b.sb("q_window", [P, 2, NP, P], BF16)
            negm = b.sb("neg_max", [P, H])
            nrest = b.sb("neg_max_rest", [P, H])
            nm3 = b.sb("neg_max_parts", [P, P], BF16)
            m_t = b.sb("neg_max_t", [P, 2, P], BF16)
            e = b.sb("exp", [P, 2, GH, 2, P])
            rec = b.sb("rec", [P, H])
            attn = b.sb("attn", [P, H, DH])
            vw = b.sb("v_window", [P, 2, 2, H, 32])
            o_sb = b.sb("values_t", [P, NG, P])
            y = b.sb("y", [P, NT, P])
            win, n_done, max_done, nm_ready, mtp, mt = (b.sem(s) for s in ("window", "nat_done", "max_done", "nm_ready", "mt_psum", "mt_ready"))
            t_done, exp_done, sel_done, pv_done = (b.sem(s) for s in ("t_done", "exp_done", "sel_done", "pv_done"))
            vwin, otp, o_done = (b.sem(s) for s in ("v_window", "values_psum", "values_sbuf"))
            norm_done, atp, at_done = (b.sem(s) for s in ("norm_done", "at_psum", "at_done"))
            proj, y_ready = b.sem("proj"), b.sem("y_ready")
            dch = b.sem("dve_chain")
            rch = b.sem("rec_chain")
            cleared = b.sem("cleared")
            sel_begun = b.sem("sel_begun")
            SN, ST, PV, MISC = 0, 4, 6, 7
            misc_bf = psum[:, MISC, 0:64].bitcast(BF16)

            def steps(eng, body):
                body(0, 0)
                with eng.Fori(0, (NS - 3) // 2) as i:
                    body(2 * i + 1, 1)
                    body(2 * i + 2, 0)
                body(NS - 2, 1)
                body(NS - 1, 0)

            with nc.Block() as block:
                @block.tensor
                def _(pe):
                    def natural(w, wp, g):
                        first = isinstance(w, int) and 4 * w + g < 2
                        if g == 0:
                            pe.wait_ge(win, w + 1)
                        if not first:
                            pe.wait_ge(max_done, 4 * w + g - 1)
                        for r in range(2):
                            nc.tensor.matmul(psum[:, SN + 2 * (g % 2) + r, :], c["identb"][:, :], c["mask"][:, :, :].rearrange("p a b -> p (a b)"),
                                             start=True, stop=False)
                        for u in range(2):
                            for r in range(2):
                                rows = slice(64 * r, 64 * r + 64)
                                last = nc.tensor.matmul(psum[:, SN + 2 * (g % 2) + r, 256 * u:256 * u + 256], qw[rows, wp, 2 * g + u, :],
                                                        kw[rows, wp, 2 * g + u, :], start=False, stop=(u == 1))
                        last.then_inc(n_done, 1)

                    def transposed(s, sp, g):
                        if g == 0:
                            pe.wait_ge(mt, s + 1)
                        if not (isinstance(s, int) and 4 * s + g < 1):
                            pe.wait_ge(exp_done, 4 * s + g)
                        for r in range(2):
                            for u in range(2):
                                nc.tensor.matmul(psum[:, ST + r, 256 * u:256 * u + 256].rearrange("p (j q) -> p j q", j=2), c["sel"][:, 4 * g + 2 * u + r, :],
                                                 m_t[:, sp, :].unsqueeze(1).broadcast_to([P, 2, P]), start=(u == 0), stop=False)
                        for u in range(2):
                            for j in range(2):
                                for r in range(2):
                                    rows = slice(64 * r, 64 * r + 64)
                                    last = nc.tensor.matmul(psum[:, ST + r, 256 * u + P * j:256 * u + P * j + P], kw[rows, sp, 2 * g + u, P * j:P * j + P],
                                                            qw[rows, sp, 2 * g + u, :], start=False, stop=(u == 1 and j == 1))
                        last.then_inc(t_done, 1)

                    def values(s, sp, g):
                        if g == 0:
                            pe.wait_ge(vwin, s + 1)
                            if not (isinstance(s, int) and s == 0):
                                pe.wait_ge(o_done, s)
                        pe.wait_ge(sel_done, 4 * s + g + 1)
                        for k in range(GH):
                            h = GH * g + 2 * (k % 2) + k // 2
                            for j in range(2):
                                last = nc.tensor.matmul(psum[32 * k:32 * k + 32, PV, P * g:P * g + P], vw[:, sp, j, h, :], e[:, g % 2, k, j, :],
                                                        start=(j == 0), stop=(j == 1))
                        last.then_inc(pv_done, 1)

                    def maxima_t(w):
                        pe.wait_ge(nm_ready, w + 1)
                        if not (isinstance(w, int) and w < 2):
                            pe.wait_ge(at_done, w - 1)
                        nc.tensor.transpose(misc_bf, nm3[:, :], c["identb"][:, :]).then_inc(mtp, 1)

                    def values_nat(s):
                        pe.wait_ge(o_done, s + 1)
                        for g in range(NG):
                            last = nc.tensor.transpose(psum[:, MISC, P * g:P * g + P], o_sb[:, g, :], c["ident"][:, :])
                        last.then_inc(otp, 1)

                    def attn_t(s):
                        pe.wait_ge(norm_done, s + 1)
                        nc.tensor.transpose(psum[:, MISC, 0:P], attn[:, :, :].rearrange("p h d -> p (h d)"), c["ident"][:, :]).then_inc(atp, 1)

                    def body(s, sp):
                        more = not (isinstance(s, int) and s == NS - 1)
                        late = not (isinstance(s, int) and s == 0)
                        nat = (lambda g: natural(s + 1, 1 - sp, g)) if more else (lambda g: None)
                        nat(0)
                        transposed(s, sp, 0)
                        if late:
                            values_nat(s - 1)
                        nat(1)
                        transposed(s, sp, 1)
                        values(s, sp, 0)
                        nat(2)
                        if late:
                            attn_t(s - 1)
                        nat(3)
                        transposed(s, sp, 2)
                        values(s, sp, 1)
                        transposed(s, sp, 3)
                        values(s, sp, 2)
                        if more:
                            maxima_t(s + 1)
                        values(s, sp, 3)

                    pe.wait_ge(stacked, n_stacked)
                    for g in range(NG):
                        natural(0, 0, g)
                    maxima_t(0)
                    steps(pe, body)
                    values_nat(NS - 1)
                    attn_t(NS - 1)
                    pe.wait_ge(at_done, NS)
                    for t in range(NT):
                        if t % 4 == 0 and t >= 8:
                            pe.wait_ge(y_ready, t - 4)
                        last = nc.tensor.matmul(psum[:, SN + (t // 4) % 2, P * (t % 4):P * (t % 4) + P], a_t[:, 64 + P * t:64 + P * t + P], wout[:, :],
                                                start=True, stop=True)
                        if t % 4 == 3:
                            last.then_inc(proj, 1)

                @block.vector
                def _(dve):
                    def window(w, wp):
                        nc.vector.tensor_copy(kw[:, wp, :, :], ks[:, :, bass.ds(w * P, 2 * P)])
                        nc.vector.tensor_copy(qw[:, wp, :, :], qs[:, :, bass.ds(w * P, P)]).then_inc(win, 1)

                    def window_v(w, wp):
                        nc.vector.tensor_copy(vw[:, wp, :, :, 0:DH + 1], v9[:, bass.ds(w, 2), :, :]).then_inc(vwin, 1)

                    def maxima(w, g):
                        dve.wait_ge(n_done, 4 * w + g + 1)
                        nc.vector.tensor_reduce(negm[:, GH * g:GH * g + GH].rearrange("p (u r) -> p r u", r=2),
                                                psum[:, SN + 2 * (g % 2):SN + 2 * (g % 2) + 2, :].rearrange("p r (u k) -> p r u k", u=2),
                                                AX_X, ALU.max, negate=True).then_inc(max_done, 1)

                    def parts(w):
                        dve.wait_ge(max_done, 4 * w + 4)
                        if not (isinstance(w, int) and w == 0):
                            dve.wait_ge(mtp, w)
                        nc.vector.tensor_copy(nm3[:, 0:H], negm[:, :]).then_inc(dch, 1)
                        dve.wait_ge(dch, 4 * w + 1)
                        nc.vector.tensor_tensor(nrest[:, :], negm[:, :], nm3[:, 0:H], ALU.subtract).then_inc(dch, 1)
                        dve.wait_ge(dch, 4 * w + 2)
                        nc.vector.tensor_copy(nm3[:, H:2 * H], nrest[:, :]).then_inc(dch, 1)
                        dve.wait_ge(dch, 4 * w + 3)
                        nc.vector.tensor_tensor(nm3[:, 2 * H:3 * H], nrest[:, :], nm3[:, H:2 * H], ALU.subtract).then_inc(nm_ready, 1)
                        dve.sem_inc(dch, 1)

                    def maxima_t(w, wp):
                        dve.wait_ge(mtp, w + 1)
                        if not (isinstance(w, int) and w < 2):
                            dve.wait_ge(t_done, 4 * w - 4)
                        nc.vector.tensor_copy(m_t[:, wp, :], misc_bf).then_inc(mt, 1)

                    def norm(s):
                        dve.wait_ge(otp, s + 1)
                        if not (isinstance(s, int) and s == 0):
                            dve.wait_ge(atp, s)
                        nat = psum[:, MISC, :].rearrange("p (g r u m) -> p g r u m", g=NG, r=2, u=2)
                        rv = rec[:, :].rearrange("p (g u r) -> p g r u", g=NG, u=2)
                        av = attn[:, :, :].rearrange("p (g u r) d -> p g r u d", g=NG, u=2)
                        nc.vector.reciprocal(rv, nat[:, :, :, :, DH]).then_inc(rch, 1)
                        dve.wait_ge(rch, s + 1)
                        for r in range(2):
                            last = nc.vector.tensor_tensor(av[:, :, r], nat[:, :, r, :, 0:DH], rv[:, :, r].unsqueeze(3).broadcast_to([P, NG, 2, DH]), ALU.mult)
                        last.then_inc(norm_done, 1)

                    def body(s, sp):
                        last = isinstance(s, int) and s == NS - 1
                        if not last:
                            maxima(s + 1, 0)
                        if not (isinstance(s, int) and s == 0):
                            norm(s - 1)
                        if last:
                            return
                        dve.wait_ge(pv_done, 4 * s) if not (isinstance(s, int) and s == 0) else None
                        window_v(s + 1, 1 - sp)
                        for g in range(1, NG):
                            maxima(s + 1, g)
                        parts(s + 1)
                        if not (isinstance(s, int) and s == NS - 2):
                            dve.wait_ge(t_done, 4 * s + 4)
                            window(s + 2, sp)
                        maxima_t(s + 1, 1 - sp)

                    nc.vector.memset(vw[:, :, :, :, :], 0.0)
                    nc.vector.memset(nm3[:, :], 0.0).then_inc(cleared, 1)
                    dve.wait_ge(cleared, 1)
                    dve.wait_ge(stacked, n_stacked)
                    window(0, 0)
                    window(1, 1)
                    window_v(0, 0)
                    for g in range(NG):
                        maxima(0, g)
                    parts(0)
                    maxima_t(0, 0)
                    steps(dve, body)
                    norm(NS - 1)
                    ych = Count(b.sem("y_chain"))
                    for t in range(NT):
                        if t % 4 == 0:
                            dve.wait_ge(proj, t // 4 + 1)
                        nc.vector.tensor_tensor(y[:, t, :], psum[:, SN + (t // 4) % 2, P * (t % 4):P * (t % 4) + P], bout[:, :], ALU.add).then_inc(y_ready, 1)
                        dve.wait_ge(y_ready, t + 1)
                        ln_y.tile_stats(t, y[:, t, :])
                    ln_y.finish(dve)
                    for t in range(NT):
                        ych.up(ln_y.scale(t, y[:, t, :], y[:, t, :]))
                    for t in range(NT):
                        dve.wait_ge(ych.sem, t + 1)
                        nc.vector.tensor_tensor(x[:, t, :], x[:, t, :], y[:, t, :], ALU.add)

                @block.scalar
                def _(act):
                    def exps(s, g):
                        act.wait_ge(t_done, 4 * s + g + 1)
                        if not (isinstance(s, int) and 4 * s + g < 2):
                            act.wait_ge(pv_done, 4 * s + g - 1)
                        nc.scalar.activation(e[:, g % 2, :, :, :].rearrange("p h j q -> p (h j q)"),
                                             psum[:, ST:ST + 2, :].rearrange("p b n -> p (b n)"), ACT.Exp).then_inc(exp_done, 1)

                    def attn_t(s):
                        act.wait_ge(atp, s + 1)
                        nc.scalar.copy(a_t[:, bass.ds(s * P, P)], psum[:, MISC, 0:P]).then_inc(at_done, 1)

                    def values_out(s):
                        act.wait_ge(pv_done, 4 * s + 4)
                        if not (isinstance(s, int) and s == 0):
                            act.wait_ge(otp, s)
                        nc.scalar.copy(o_sb[:, :, :].rearrange("p g q -> p (g q)"), psum[:, PV, :]).then_inc(o_done, 1)

                    def body(s, sp):
                        late = not (isinstance(s, int) and s == 0)
                        if late:
                            values_out(s - 1)
                        exps(s, 0)
                        exps(s, 1)
                        if late:
                            attn_t(s - 1)
                        exps(s, 2)
                        exps(s, 3)

                    steps(act, body)
                    values_out(NS - 1)
                    attn_t(NS - 1)
                    ln_y.root(act)

                @block.gpsimd
                def _(pool):
                    def body(s, sp):
                        for g in range(NG):
                            pool.wait_ge(exp_done, 4 * s + g + 1)
                            pool.sem_inc(sel_begun, 1)
                            nc.gpsimd.affine_select(out=e[:, g % 2, :, 0, :], in_=e[:, g % 2, :, 0, :], compare_op=ALU.is_ge,
                                                    fill=0.0, base=0, pattern=[[0, GH], [-1, P]], channel_multiplier=1)
                            nc.gpsimd.affine_select(out=e[:, g % 2, :, 1, :], in_=e[:, g % 2, :, 1, :], compare_op=ALU.is_ge,
                                                    fill=0.0, base=0, pattern=[[0, GH], [1, P]], channel_multiplier=-1).then_inc(sel_done, 1)
                    steps(pool, body)
        nc.clear_and_free_semaphores(used)
        nc.all_engine_barrier()


def kmoe(nc, x, c, d):
    T, R, E = 256, 8, 64
    D1, F1 = 32, 64
    NT = 16
    G = 4
    NGR = T // G
    with ExitStack() as ctx:
        a = Alloc(nc, ctx, "ff")
        psum = a.ps("psum", [P, 8, 512])
        xt = a.sb("xt", [P, T * R])
        wup = a.sb("w_up", [P, R, E])
        bup = a.sb("b_up", [P, E, F1])
        aup = a.sb("a_up", [P, E, F1])
        wdn = a.sb("w_down", [F1, F1, E])
        bdn = a.sb("b_down", [P, E, D1])
        adn = a.sb("a_down", [P, E, D1])
        bias_up = a.sb("bias_up", [F1, F1])
        bias_dn = a.sb("bias_down", [D1, D1])
        scales = a.sb("scales", [F1, 2])
        pb = [a.sb(f"probs_{n}", [F1, 2, T]) for n in ("up", "down")]
        words = [a.sb(f"words_{n}", [1, T // 2], I32) for n in ("up", "down")]
        h = a.sb("h", [F1, T, F1])
        lg = a.sb("logits", [P, 2, E])
        mx = a.sb("top_values", [P, 2, 8])
        ix = a.sb("top_index", [P, 2, 8], U32)
        ef = a.sb("experts", [P, 2, 2])
        wv = a.sb("word_part", [P, 2])
        dv = a.sb("gap", [P, 2])
        ev = a.sb("gap_exp", [P, 2])
        pr = a.sb("probs", [P, 2, 2])
        dg = a.sb("probs_diag", [P, 2, 2, P])
        loaded = a.sem("loaded")
        wup_loaded = a.sem("wup_loaded")
        down_loaded = a.sem("down_loaded")
        zeroed = a.sem("zeroed")
        rch = Count(a.sem("route_chain"))
        gap_ready, exp_ready, diag_ready, route_mm, routed = (a.sem(s) for s in ("gap_ready", "exp_ready", "diag_ready", "route_mm", "routed"))

        def route_dve(dve, n, src):
            v = nc.vector
            for t in range(2):
                rch.up(v.tensor_copy(lg[:, t, :], src(t)))
            rch.settle(dve)
            for t in range(2):
                rch.up(v.max(mx[:, t, :], lg[:, t, :]))
            rch.settle(dve)
            for t in range(2):
                v.max_index(ix[:, t, :], mx[:, t, :], lg[:, t, :])
            rch.up(v.tensor_tensor(dv[:, :], mx[:, :, 1], mx[:, :, 0], ALU.subtract))
            rch.settle(dve)
            v.tensor_copy(ef[:, :, :], ix[:, :, 0:2]).then_inc(gap_ready, 1)
            dve.wait_ge(gap_ready, n + 1)
            rch.up(v.scalar_tensor_tensor(out=wv[:, :], in0=ef[:, :, 1], scalar=64.0, in1=ef[:, :, 0], op0=ALU.mult, op1=ALU.add))
            dve.wait_ge(exp_ready, n + 1)
            rch.up(v.tensor_scalar(dv[:, :], ev[:, :], 1.0, None, ALU.add))
            rch.settle(dve)
            rch.up(v.reciprocal(pr[:, :, 0], dv[:, :]))
            rch.settle(dve)
            rch.up(v.tensor_tensor(pr[:, :, 1], ev[:, :], pr[:, :, 0], ALU.mult))
            rch.settle(dve)
            for t in range(2):
                for k in range(2):
                    last = v.tensor_scalar(dg[:, k, t, :], c["ident"][:, :], pr[:, t, k:k + 1], None, ALU.mult)
            last.then_inc(diag_ready, 1)
            dve.wait_ge(route_mm, n + 1)
            v.tensor_copy(words[n][:, :], psum[0:1, 7, 0:T // 2])
            v.tensor_copy(pb[n][:, :, :].rearrange("p k t -> p (k t)"), psum[0:F1, 6, :]).then_inc(routed, 1)

        def route_act(act, n):
            act.wait_ge(gap_ready, n + 1)
            nc.scalar.activation(ev[:, :], dv[:, :], ACT.Exp).then_inc(exp_ready, 1)

        def route_pe(pe, n):
            pe.wait_ge(diag_ready, n + 1)
            for t in range(2):
                nc.tensor.matmul(psum[0:1, 7, E * t:E * t + E], wv[:, t:t + 1], c["pair"][:, :], start=True, stop=True)
            nc.tensor.matmul(psum[0:F1, 6, :], c["ones"][:, 0:F1], dg[:, :, :, :].rearrange("p k t n -> p (k t n)"), start=True, stop=True).then_inc(route_mm, 1)

        with ExitStack() as ctx0:
            b = Alloc(nc, ctx0, "f0")
            xn = b.sb("xn", [P, NT, P])
            ln = Norm(nc, b, "ln", NT)
            xn_ready, tp_done, xt_ready, lg_done = (b.sem(s) for s in ("xn_ready", "tp_done", "xt_ready", "lg_done"))
            with nc.Block() as block:
                @block.sync
                def _(sp):
                    sp.dma_start(wup[:, :, :], d["w_up"]).then_inc(wup_loaded, 16)
                    for q in range(4):
                        sp.dma_start(bup[32 * q:32 * q + 32, :, :], d["b_up"]).then_inc(loaded, 16)
                    sp.wait_ge(zeroed, 1)
                    sp.dma_start(aup[0:D1, :, :], d["a_up"]).then_inc(loaded, 16)
                    sp.dma_start(bias_up[:, :], d["bias_up"]).then_inc(loaded, 16)
                    sp.dma_start(bias_dn[:, :], d["bias_down"]).then_inc(loaded, 16)
                    sp.dma_start(scales[:, 0:1], d["scale_up"].broadcast_to([F1, 1])).then_inc(loaded, 16)
                    sp.dma_start(scales[:, 1:2], d["scale_down"].broadcast_to([F1, 1])).then_inc(loaded, 16)
                    sp.dma_start(wdn[:, :, :], d["w_down"]).then_inc(down_loaded, 16)
                    sp.dma_start(bdn[0:F1, :, :], d["b_down"]).then_inc(down_loaded, 16)
                    sp.dma_start(adn[0:F1, :, :], d["a_down"]).then_inc(down_loaded, 16)

                @block.gpsimd
                def _(g):
                    nc.gpsimd.memset(aup[:, :, :], 0.0)
                    nc.gpsimd.memset(bdn[:, :, :], 0.0)
                    nc.gpsimd.memset(adn[:, :, :], 0.0)
                    nc.gpsimd.memset(c["ones"][:, :], 1.0).then_inc(zeroed, 1)
                    ch = Count(b.sem("pool_chain"))
                    ch.up(nc.gpsimd.memset(c["pair"][:, :], 0.0))
                    for odd, weight in enumerate((1.0, 4096.0)):
                        ch.settle(g)
                        ch.up(nc.gpsimd.affine_select(out=c["pair"][:, :], in_=c["pair"][:, :], compare_op=ALU.not_equal,
                                                      fill=weight, base=-odd, pattern=[[-2, E]], channel_multiplier=1))
                    c["pair_ready"] = (ch.sem, ch.n)

                @block.vector
                def _(dve):
                    for t in range(NT):
                        ln.tile_stats(t, x[:, t, :])
                    ln.finish(dve)
                    for t in range(NT):
                        ln.scale(t, xn[:, t, :], x[:, t, :]).then_inc(xn_ready, 1)
                    dve.wait_ge(lg_done, 1)
                    route_dve(dve, 0, lambda t: psum[:, 4, E * t:E * t + E])

                @block.scalar
                def _(act):
                    ln.root(act)
                    for ch in range(4):
                        act.wait_ge(tp_done, ch + 1)
                        nc.scalar.copy(xt[:, 512 * ch:512 * ch + 512], psum[:, ch, :]).then_inc(xt_ready, 1)
                    route_act(act, 0)

                @block.tensor
                def _(pe):
                    for ch in range(4):
                        pe.wait_ge(xn_ready, 4 * ch + 4)
                        for t in range(4):
                            last = nc.tensor.transpose(psum[:, ch, P * t:P * t + P], xn[:, 4 * ch + t, :], c["ident"][:, :])
                        last.then_inc(tp_done, 1)
                    pe.wait_ge(wup_loaded, 16)
                    pe.wait_ge(xt_ready, 4)
                    rows = xt[:, :].rearrange("p (t r) -> p r t", r=R)
                    for t in range(2):
                        for r in range(R):
                            last = nc.tensor.matmul(psum[:, 4, E * t:E * t + E], rows[:, r, P * t:P * t + P], wup[:, r, :], start=(r == 0), stop=(r == R - 1))
                    last.then_inc(lg_done, 1)
                    pe.wait_ge(*c["pair_ready"])
                    route_pe(pe, 0)

        def steps(eng, body, n):
            with eng.Fori(0, n // 2 - 1) as i:
                body(2 * i, 0)
                body(2 * i + 1, 1)
            body(n - 2, 0)
            body(n - 1, 1)

        def fetch(pe, raw, kept, n, i, par, width):
            pe.load(raw, words[n][0:1, bass.ds(i * 2, 2)])
            bits = width.bit_length() - 1
            mask = (E - 1) << bits
            out = []
            for w in range(2):
                word = pe.snap(raw[w])
                for k in range(4):
                    shift = 6 * k - bits
                    v = pe.snap(((word << -shift) if shift < 0 else (word >> shift)) & mask)
                    pe.reg_mov(kept[par][4 * w + k], v)
                    out.append(v)
            return out

        def again(pe, kept, par, width):
            mask = (E - 1) * width
            return [pe.snap(pe.snap(kept[par][n]) & mask) for n in range(2 * G)]

        with ExitStack() as ctx1:
            b = Alloc(nc, ctx1, "f1")
            xg = b.sb("x_group", [P, 2, G, R, 4])
            z = b.sb("z", [P, 2, G, 2, F1])
            quarter = b.sem("quarter")
            mid_clear = b.sem("mid_clear")
            clear, xg_ready, z_done, z_ready, h_done, hb_ready, g_done = (b.sem(s) for s in (
                "clear", "xg_ready", "z_psum", "z_ready", "h_psum", "h_biased", "gelu_done"))
            with nc.Block() as block:
                @block.gpsimd
                def _(g):
                    nc.gpsimd.memset(xg[:, :, :, :, :], 0.0).then_inc(clear, 1)
                    g.wait_ge(clear, 1)

                    def body(i, par):
                        if not (isinstance(i, int) and i < 2):
                            g.wait_ge(z_done, i - 1)
                        for q in range(4):
                            rows = slice(32 * q, 32 * q + 32)
                            if not (isinstance(i, int) and 4 * i + q == 0):
                                g.wait_ge(quarter, 4 * i + q)
                            nc.gpsimd.tensor_copy(xg[rows, par, :, :, q], xt[rows, bass.ds(i * (G * R), G * R)].rearrange("p (t r) -> p t r", t=G))\
                                .then_inc(quarter, 1)
                        g.wait_ge(quarter, 4 * i + 4)
                        g.sem_inc(xg_ready, 1)
                    body(0, 0)
                    body(1, 1)
                    with g.Fori(1, NGR // 2) as i:
                        body(2 * i, 0)
                        body(2 * i + 1, 1)

                @block.tensor
                def _(pe):
                    raw = [pe.alloc_register(f"up_word{k}") for k in range(2)]
                    kept = [[pe.alloc_register(f"up_offset{par}_{k}") for k in range(2 * G)] for par in range(2)]
                    bf = bup[:, :, :].rearrange("p e n -> p (e n)")
                    af = aup[:, :, :].rearrange("p e n -> p (e n)")

                    def first(i, par):
                        off = fetch(pe, raw, kept, 0, i, par, F1)
                        pe.wait_ge(xg_ready, i + 1)
                        if not (isinstance(i, int) and i < 2):
                            pe.wait_ge(z_ready, i - 1)
                        for t in range(G):
                            for k in range(2):
                                last = nc.tensor.matmul(psum[0:D1, par, F1 * (2 * t + k):F1 * (2 * t + k) + F1],
                                                        xg[:, par, t, :, :].rearrange("p r q -> p (r q)"), bf[:, bass.ds(off[2 * t + k], F1)], start=True, stop=True)
                        last.then_inc(z_done, 1)

                    def second(i, par, later):
                        off = again(pe, kept, par, F1)
                        pe.wait_ge(z_ready, i + 1)
                        if later:
                            pe.wait_ge(hb_ready, i - 1)
                        for t in range(G):
                            for k in range(2):
                                last = nc.tensor.matmul(psum[0:F1, 2 + par, F1 * t:F1 * t + F1], z[:, par, t, k, :], af[:, bass.ds(off[2 * t + k], F1)],
                                                        start=(k == 0), stop=(k == 1))
                        last.then_inc(h_done, 1)

                    pe.wait_ge(loaded, 16 * 9)
                    pe.wait_ge(clear, 1)
                    pe.wait_ge(mid_clear, 1)
                    first(0, 0)
                    first(1, 1)
                    second(0, 0, False)
                    first(2, 0)
                    second(1, 1, False)
                    with pe.Fori(1, NGR // 2 - 1) as i:
                        first(2 * i + 1, 1)
                        second(2 * i, 0, True)
                        first(2 * i + 2, 0)
                        second(2 * i + 1, 1, True)
                    first(NGR - 1, 1)
                    second(NGR - 2, 0, True)
                    second(NGR - 1, 1, True)

                @block.vector
                def _(dve):
                    nc.vector.memset(z[:, :, :, :, :], 0.0).then_inc(mid_clear, 1)
                    dve.wait_ge(mid_clear, 1)

                    def weigh(i, par, later):
                        dve.wait_ge(z_done, i + 1)
                        if later:
                            dve.wait_ge(h_done, i - 1)
                        nc.vector.tensor_tensor(z[0:D1, par, :, :, :], psum[0:D1, par, :].rearrange("p (t k n) -> p t k n", t=G, k=2),
                                                pb[0][0:D1, :, bass.ds(i * G, G)].rearrange("p k t -> p t k").unsqueeze(3).broadcast_to([D1, G, 2, F1]),
                                                ALU.mult).then_inc(z_ready, 1)

                    def bias(i, par):
                        dve.wait_ge(h_done, i + 1)
                        nc.vector.scalar_tensor_tensor(out=h[:, bass.ds(i * G, G), :], in0=psum[0:F1, 2 + par, 0:G * F1].rearrange("p (t n) -> p t n", t=G),
                                                       scalar=scales[:, 0:1], in1=bias_up[:, :].unsqueeze(1).broadcast_to([F1, G, F1]),
                                                       op0=ALU.mult, op1=ALU.add).then_inc(hb_ready, 1)
                    weigh(0, 0, False)
                    weigh(1, 1, False)
                    bias(0, 0)
                    weigh(2, 0, True)
                    bias(1, 1)
                    with dve.Fori(1, NGR // 2 - 1) as i:
                        weigh(2 * i + 1, 1, True)
                        bias(2 * i, 0)
                        weigh(2 * i + 2, 0, True)
                        bias(2 * i + 1, 1)
                    weigh(NGR - 1, 1, True)
                    bias(NGR - 2, 0)
                    bias(NGR - 1, 1)

                @block.scalar
                def _(act):
                    with act.Fori(0, NGR // 2) as i:
                        act.wait_ge(hb_ready, 2 * i + 2)
                        part = h[:, bass.ds(i * (2 * G), 2 * G), :].rearrange("p t n -> p (t n)")
                        nc.scalar.activation(part, part, ACT.Gelu).then_inc(g_done, 1)

        with ExitStack() as ctx2:
            b = Alloc(nc, ctx2, "f2")
            mid_clear = b.sem("mid_clear")
            hg = b.sb("h_group", [P, 2, G, F1])
            vs = b.sb("v", [P, 2, G, 2, D1])
            yb = b.sb("y_t", [D1, T, D1])
            lgt = b.sb("logits_t", [E, T])
            y = b.sb("y", [P, NT, P])
            ln = Norm(nc, b, "ln", NT)
            lg_done, lgt_ready, lg_nat = (b.sem(s) for s in ("lgt_psum", "lgt_ready", "lg_nat"))
            clear, hg_ready, v_done, v_ready, y_done, y_ready, nat_done = (b.sem(s) for s in (
                "clear", "hg_ready", "v_psum", "v_ready", "y_psum", "y_ready", "nat_done"))
            ych = Count(b.sem("y_chain"))
            with nc.Block() as block:
                @block.gpsimd
                def _(g):
                    nc.gpsimd.memset(hg[:, :, :, :], 0.0).then_inc(clear, 1)
                    g.wait_ge(clear, 1)

                    def body(i, par):
                        if not (isinstance(i, int) and i < 2):
                            g.wait_ge(v_done, i - 1)
                        nc.gpsimd.tensor_copy(hg[0:F1, par, :, :], h[:, bass.ds(i * G, G), :]).then_inc(hg_ready, 1)
                    body(0, 0)
                    body(1, 1)
                    with g.Fori(1, NGR // 2) as i:
                        body(2 * i, 0)
                        body(2 * i + 1, 1)

                @block.tensor
                def _(pe):
                    pe.wait_ge(down_loaded, 48)
                    for o in range(F1):
                        last = nc.tensor.matmul(psum[0:E, 4, 0:T], wdn[:, o, :], h[:, :, o], start=(o == 0), stop=(o == F1 - 1))
                    last.then_inc(lg_done, 1)
                    pe.wait_ge(lgt_ready, 1)
                    for t in range(2):
                        last = nc.tensor.transpose(psum[:, 5, E * t:E * t + E], lgt[:, P * t:P * t + P], c["ident"][0:E, 0:E])
                    last.then_inc(lg_nat, 1)
                    route_pe(pe, 1)
                    raw = [pe.alloc_register(f"dn_word{k}") for k in range(2)]
                    kept = [[pe.alloc_register(f"dn_offset{par}_{k}") for k in range(2 * G)] for par in range(2)]
                    bf = bdn[:, :, :].rearrange("p e n -> p (e n)")
                    af = adn[:, :, :].rearrange("p e n -> p (e n)")

                    def first(i, par):
                        off = fetch(pe, raw, kept, 1, i, par, D1)
                        pe.wait_ge(hg_ready, i + 1)
                        if not (isinstance(i, int) and i < 2):
                            pe.wait_ge(v_ready, i - 1)
                        for t in range(G):
                            for k in range(2):
                                last = nc.tensor.matmul(psum[0:F1, par, D1 * (2 * t + k):D1 * (2 * t + k) + D1], hg[:, par, t, :], bf[:, bass.ds(off[2 * t + k], D1)],
                                                        start=True, stop=True)
                        last.then_inc(v_done, 1)

                    def second(i, par, later):
                        off = again(pe, kept, par, D1)
                        pe.wait_ge(v_ready, i + 1)
                        if later:
                            pe.wait_ge(y_ready, i - 1)
                        for t in range(G):
                            for k in range(2):
                                last = nc.tensor.matmul(psum[0:D1, 2 + par, D1 * t:D1 * t + D1], vs[:, par, t, k, :], af[:, bass.ds(off[2 * t + k], D1)],
                                                        start=(k == 0), stop=(k == 1))
                        last.then_inc(y_done, 1)

                    pe.wait_ge(routed, 2)
                    pe.wait_ge(clear, 1)
                    pe.wait_ge(mid_clear, 1)
                    first(0, 0)
                    first(1, 1)
                    second(0, 0, False)
                    first(2, 0)
                    second(1, 1, False)
                    with pe.Fori(1, NGR // 2 - 1) as i:
                        first(2 * i + 1, 1)
                        second(2 * i, 0, True)
                        first(2 * i + 2, 0)
                        second(2 * i + 1, 1, True)
                    first(NGR - 1, 1)
                    second(NGR - 2, 0, True)
                    second(NGR - 1, 1, True)
                    pe.wait_ge(y_ready, NGR)
                    quarters = yb[:, :, :].rearrange("b t (r q) -> b q (t r)", q=4)
                    for t in range(NT):
                        for q in range(4):
                            last = nc.tensor.transpose(psum[:, 4 + t // 4, P * (t % 4) + 32 * q:P * (t % 4) + 32 * q + 32], quarters[:, q, P * t:P * t + P],
                                                       c["ident"][0:D1, 0:D1])
                        if t % 4 == 3:
                            last.then_inc(nat_done, 1)

                @block.vector
                def _(dve):
                    nc.vector.memset(vs[:, :, :, :, :], 0.0).then_inc(mid_clear, 1)
                    dve.wait_ge(mid_clear, 1)
                    dve.wait_ge(lg_nat, 1)
                    route_dve(dve, 1, lambda t: psum[:, 5, E * t:E * t + E])

                    def weigh(i, par, later):
                        dve.wait_ge(v_done, i + 1)
                        if later:
                            dve.wait_ge(y_done, i - 1)
                        nc.vector.tensor_tensor(vs[0:F1, par, :, :, :], psum[0:F1, par, 0:2 * G * D1].rearrange("p (t k n) -> p t k n", t=G, k=2),
                                                pb[1][:, :, bass.ds(i * G, G)].rearrange("p k t -> p t k").unsqueeze(3).broadcast_to([F1, G, 2, D1]),
                                                ALU.mult).then_inc(v_ready, 1)

                    def bias(i, par):
                        dve.wait_ge(y_done, i + 1)
                        nc.vector.scalar_tensor_tensor(out=yb[:, bass.ds(i * G, G), :], in0=psum[0:D1, 2 + par, 0:G * D1].rearrange("p (t n) -> p t n", t=G),
                                                       scalar=scales[0:D1, 1:2], in1=bias_dn[:, :].unsqueeze(1).broadcast_to([D1, G, D1]),
                                                       op0=ALU.mult, op1=ALU.add).then_inc(y_ready, 1)
                    dve.wait_ge(routed, 2)
                    weigh(0, 0, False)
                    weigh(1, 1, False)
                    bias(0, 0)
                    weigh(2, 0, True)
                    bias(1, 1)
                    with dve.Fori(1, NGR // 2 - 1) as i:
                        weigh(2 * i + 1, 1, True)
                        bias(2 * i, 0)
                        weigh(2 * i + 2, 0, True)
                        bias(2 * i + 1, 1)
                    weigh(NGR - 1, 1, True)
                    bias(NGR - 2, 0)
                    bias(NGR - 1, 1)
                    tile = lambda t: psum[:, 4 + t // 4, P * (t % 4):P * (t % 4) + P]
                    for t in range(NT):
                        if t % 4 == 0:
                            dve.wait_ge(nat_done, t // 4 + 1)
                        ln.tile_stats(t, tile(t))
                    ln.finish(dve)
                    for t in range(NT):
                        ych.up(ln.scale(t, y[:, t, :], tile(t)))
                    for t in range(NT):
                        dve.wait_ge(ych.sem, t + 1)
                        nc.vector.tensor_tensor(x[:, t, :], x[:, t, :], y[:, t, :], ALU.add)

                @block.scalar
                def _(act):
                    act.wait_ge(lg_done, 1)
                    nc.scalar.copy(lgt[:, :], psum[0:E, 4, 0:T]).then_inc(lgt_ready, 1)
                    route_act(act, 1)
                    ln.root(act)


def ssm(nc, x, c, d):
    T, NT, NC, W = 2048, 16, 4, 512
    NB, S, K = 2, 64, 4
    with ExitStack() as ctx:
        a = Alloc(nc, ctx, "sm")
        psum = a.ps("psum", [P, 8, W])
        xn = a.sb("xn", [P, NT, P])
        xt = a.sb("xt", [P, T])
        w_in = a.sb("w_in", [P, 2 * NB * P])
        cw = a.sb("conv_w", [P, NB, K])
        cb = a.sb("conv_b", [P, NB])
        wb = a.sb("w_b", [P, NB, S])
        wc = a.sb("w_c", [S, NB * P])
        dp = a.sb("d_param", [P, NB])
        wo = a.sb("w_out", [P, NB, P])
        gamma = a.sb("gamma", [P, P])
        beta = a.sb("beta", [P, P])
        xin = a.sb("x_in", [P, NB, K - 1 + T])
        gate = a.sb("gate", [P, NB, T])
        u = a.sb("u", [P, NB, T])
        bu = a.sb("bu", [S, T])
        decay = a.sb("decay", [S, W])
        hs = a.sb("states", [S, T])
        yg = a.sb("y_gated", [P, NB, T])
        z = a.sb("z", [P, NT, P])
        ln_x, ln_z, ln_o = (Norm(nc, a, n, NT) for n in ("ln_x", "ln_z", "ln_o"))
        loaded, xn_ready, tp_done, xt_ready = (a.sem(s) for s in ("loaded", "xn_ready", "tp_done", "xt_ready"))
        in_done, xin_ready, gate_ready, conv_done, u_ready = (a.sem(s) for s in ("in_psum", "xin_ready", "gate_ready", "conv_done", "u_ready"))
        bu_done, bu_ready, hs_ready, y_done, yg_ready = (a.sem(s) for s in ("bu_psum", "bu_ready", "hs_ready", "y_psum", "yg_ready"))
        yd_ready, o_done, z_ready = (a.sem(s) for s in ("yd_ready", "o_psum", "z_ready"))
        cch, och = Count(a.sem("conv_chain")), Count(a.sem("out_chain"))
        pads = a.sem("pads")
        loads = [(w_in[:, :], d["w_in"]), (cw[:, :, :], d["conv_w"]), (cb[:, :], d["conv_b"]), (wb[:, :, :], d["w_b"]), (wc[:, :], d["w_c"]),
                 (dp[:, :], d["d_param"]), (wo[:, :, :], d["w_out"]), (gamma[:, :], d["gamma"].broadcast_to([P, P])), (beta[:, :], d["beta"].broadcast_to([P, P]))]
        with nc.Block() as block:
            @block.sync
            def _(sp):
                for dst, src in loads:
                    sp.dma_start(dst, src).then_inc(loaded, 16)

            @block.tensor
            def _(pe):
                for ch in range(NC):
                    pe.wait_ge(xn_ready, 4 * ch + 4)
                    for t in range(4):
                        last = nc.tensor.transpose(psum[:, ch, P * t:P * t + P], xn[:, 4 * ch + t, :], c["ident"][:, :])
                    last.then_inc(tp_done, 1)
                pe.wait_ge(loaded, 16 * len(loads))
                pe.wait_ge(xt_ready, NC)

                def project(ch):
                    if ch >= 1:
                        pe.wait_ge(xin_ready, NB * ch)
                        pe.wait_ge(gate_ready, NB * ch)
                    for b in range(2 * NB):
                        nc.tensor.matmul(psum[:, b, :], w_in[:, P * b:P * b + P], xt[:, W * ch:W * ch + W], start=True, stop=True).then_inc(in_done, 1)

                def inputs(ch):
                    pe.wait_ge(u_ready, NB * (ch + 1))
                    if ch >= 1:
                        pe.wait_ge(bu_ready, ch)
                    for b in range(NB):
                        last = nc.tensor.matmul(psum[0:S, 4, :], wb[:, b, :], u[:, b, W * ch:W * ch + W], start=(b == 0), stop=(b == NB - 1))
                    last.then_inc(bu_done, 1)

                def outputs(ch):
                    pe.wait_ge(hs_ready, ch + 1)
                    if ch >= 1:
                        pe.wait_ge(yd_ready, NB * ch)
                    for b in range(NB):
                        nc.tensor.matmul(psum[:, 5 + b, :], wc[:, P * b:P * b + P], hs[:, W * ch:W * ch + W], start=True, stop=True).then_inc(y_done, 1)

                def out(ch):
                    pe.wait_ge(yg_ready, NB * (ch + 1))
                    if ch >= 1:
                        pe.wait_ge(z_ready, ch)
                    for t in range(4):
                        for b in range(NB):
                            last = nc.tensor.matmul(psum[:, 7, P * t:P * t + P], yg[:, b, W * ch + P * t:W * ch + P * t + P], wo[:, b, :], start=(b == 0), stop=(b == NB - 1))
                    last.then_inc(o_done, 1)

                project(0)
                for ch in range(NC):
                    if ch + 1 < NC:
                        project(ch + 1)
                    inputs(ch)
                    if ch >= 1:
                        out(ch - 1)
                    outputs(ch)
                out(NC - 1)

            @block.scalar
            def _(act):
                ln_x.root(act)
                for ch in range(NC):
                    act.wait_ge(tp_done, ch + 1)
                    nc.scalar.copy(xt[:, W * ch:W * ch + W], psum[:, ch, :]).then_inc(xt_ready, 1)

                def take(ch):
                    for b in range(NB):
                        act.wait_ge(in_done, 2 * NB * ch + b + 1)
                        nc.scalar.copy(xin[:, b, K - 1 + W * ch:K - 1 + W * ch + W], psum[:, b, :]).then_inc(xin_ready, 1)
                    for b in range(NB):
                        act.wait_ge(in_done, 2 * NB * ch + NB + b + 1)
                        nc.scalar.activation(gate[:, b, W * ch:W * ch + W], psum[:, NB + b, :], ACT.Silu).then_inc(gate_ready, 1)

                take(0)
                for ch in range(NC):
                    if ch + 1 < NC:
                        take(ch + 1)
                    for b in range(NB):
                        act.wait_ge(conv_done, NB * ch + b + 1)
                        part = u[:, b, W * ch:W * ch + W]
                        nc.scalar.activation(part, part, ACT.Silu).then_inc(u_ready, 1)
                    act.wait_ge(bu_done, ch + 1)
                    nc.scalar.mul(bu[:, W * ch:W * ch + W], psum[0:S, 4, :], 0.05).then_inc(bu_ready, 1)
                ln_z.root(act)
                ln_o.root(act)

            @block.gpsimd
            def _(g):
                for ch in range(NC):
                    for b in range(NB):
                        g.wait_ge(yd_ready, NB * ch + b + 1)
                        g.wait_ge(gate_ready, NB * ch + b + 1)
                        part = yg[:, b, W * ch:W * ch + W]
                        nc.gpsimd.tensor_tensor(part, part, gate[:, b, W * ch:W * ch + W], ALU.mult).then_inc(yg_ready, 1)

            @block.vector
            def _(dve):
                v = nc.vector
                for t in range(NT):
                    ln_x.tile_stats(t, x[:, t, :])
                v.memset(decay[:, :], 0.95)
                v.memset(xin[:, :, 0:K - 1], 0.0).then_inc(pads, 1)
                dve.wait_ge(pads, 1)
                ln_x.finish(dve)
                for t in range(NT):
                    ln_x.scale(t, xn[:, t, :], x[:, t, :]).then_inc(xn_ready, 1)
                dve.wait_ge(loaded, 16 * len(loads))

                def convolve(ch):
                    dve.wait_ge(xin_ready, NB * (ch + 1))
                    tap_at = [0] * NB
                    for k in range(K - 1, -1, -1):
                        for b in range(NB):
                            tap = xin[:, b, W * ch + k:W * ch + k + W]
                            acc = u[:, b, W * ch:W * ch + W]
                            if k == K - 1:
                                tap_at[b] = cch.up(v.tensor_scalar(acc, tap, cw[:, b, k:k + 1], cb[:, b:b + 1], ALU.mult, ALU.add))
                            else:
                                dve.wait_ge(cch.sem, tap_at[b])
                                ins = v.scalar_tensor_tensor(out=acc, in0=tap, scalar=cw[:, b, k:k + 1], in1=acc, op0=ALU.mult, op1=ALU.add)
                                if k == 0:
                                    ins.then_inc(conv_done, 1)
                                else:
                                    tap_at[b] = cch.up(ins)

                def recur(ch):
                    dve.wait_ge(bu_ready, ch + 1)
                    if ch >= 1:
                        dve.wait_ge(hs_ready, ch)
                    start = hs[:, W * ch - 1:W * ch] if ch else 0.0
                    v.tensor_tensor_scan(hs[:, W * ch:W * ch + W], decay[:, :], bu[:, W * ch:W * ch + W], start, ALU.mult, ALU.add).then_inc(hs_ready, 1)

                def skip(ch):
                    for b in range(NB):
                        dve.wait_ge(y_done, NB * ch + b + 1)
                        v.scalar_tensor_tensor(out=yg[:, b, W * ch:W * ch + W], in0=u[:, b, W * ch:W * ch + W], scalar=dp[:, b:b + 1], in1=psum[:, 5 + b, :],
                                               op0=ALU.mult, op1=ALU.add).then_inc(yd_ready, 1)

                def residual(ch):
                    dve.wait_ge(o_done, ch + 1)
                    v.tensor_tensor(z[:, 4 * ch:4 * ch + 4, :], psum[:, 7, :].rearrange("p (t n) -> p t n", t=4), xn[:, 4 * ch:4 * ch + 4, :], ALU.add).then_inc(z_ready, 1)
                    dve.wait_ge(z_ready, ch + 1)
                    for t in range(4):
                        ln_z.tile_stats(4 * ch + t, z[:, 4 * ch + t, :])

                convolve(0)
                for ch in range(NC):
                    if ch + 1 < NC:
                        convolve(ch + 1)
                    recur(ch)
                    if ch >= 1:
                        residual(ch - 1)
                    skip(ch)
                residual(NC - 1)
                ln_z.finish(dve)
                for t in range(NT):
                    och.up(ln_z.scale(t, z[:, t, :], z[:, t, :]))
                och.settle(dve)
                wide = lambda v_: v_[:, :].unsqueeze(1).broadcast_to([P, NT, P])
                och.up(v.tensor_tensor(z[:, :, :], z[:, :, :], wide(gamma), ALU.mult))
                och.settle(dve)
                och.up(v.tensor_tensor(z[:, :, :], z[:, :, :], wide(beta), ALU.add))
                och.settle(dve)
                for t in range(NT):
                    ln_o.tile_stats(t, z[:, t, :])
                ln_o.finish(dve)
                base = och.n
                for t in range(NT):
                    och.up(ln_o.scale(t, z[:, t, :], z[:, t, :]))
                for t in range(NT):
                    dve.wait_ge(och.sem, base + t + 1)
                    v.tensor_tensor(x[:, t, :], x[:, t, :], z[:, t, :], ALU.add)


def soft_moe(nc, x, c, d, out):
    T, NT, NE, NS = 2048, 16, 64, 32
    W = 512
    SL = NE * NS
    HALF = SL // 2
    HE = NE // 2
    with ExitStack() as ctx:
        a = Alloc(nc, ctx, "mo")
        psum = a.ps("psum", [P, 8, W])
        xt = a.sb("xt", [P, T])
        phi = a.sb("phi", [P, SL])
        bcol = a.sb("bias_col", [P, SL // P])
        part_max = a.sb("part_max", [P, 2, NT, NS])
        xs_t = a.sb("xs_t", [P, SL])
        mp_t = a.sb("neg_max_t", [P, T], BF16)
        yt = a.sb("y_slots", [P, SL // P, P])
        selp = a.sb("sel_slot", [P, P], BF16)
        blk = a.sb("same_slot", [P, P])
        sel_done = a.sem("sel_done")
        sel_n = [0]

        with ExitStack() as ctx0:
            b = Alloc(nc, ctx0, "m0")
            xn = b.sb("xn", [P, NT, P])
            rows = b.sb("bias_rows", [96, SL])
            rhi = b.sb("bias_hi", [96, SL], BF16)
            rmid = b.sb("bias_mid", [96, SL], BF16)
            b3 = b.sb("bias_parts", [96, SL], BF16)
            ones3 = b.sb("ones3", [96, P], BF16)
            xs = b.sb("x_tile", [P, 2, 2, P])
            ls = b.sb("logits", [P, 2, HE, NS])
            dn = b.sb("dispatch", [P, 2, HE, NS])
            mn = b.sb("max", [P, 2, HE])
            sm = b.sb("sum", [P, 2, HE])
            rs = b.sb("rsum", [P, 2, HE])
            ln = Norm(nc, b, "ln", NT)
            loaded, zeroed, xn_ready, tp_done, xt_ready, b_ready = (b.sem(s) for s in ("loaded", "zeroed", "xn_ready", "tp_done", "xt_ready", "b_ready"))
            stg, l_done, maxed, sub_done, exp_done, summed, r_ready, d_ready, x_done = (b.sem(s) for s in (
                "staged", "l_psum", "maxed", "sub_done", "exp_done", "summed", "r_ready", "d_ready", "x_psum"))
            xs_ready = b.sem("xs_ready")
            bch = Count(b.sem("bias_chain"))

            def steps(eng, body):
                body(0, 0)
                with eng.Fori(0, (NT - 2) // 2) as i:
                    body(2 * i + 1, 1)
                    body(2 * i + 2, 0)
                body(NT - 1, 1)

            with nc.Block() as block:
                @block.sync
                def _(sp):
                    sp.dma_start(phi[:, :], d["phi"]).then_inc(loaded, 16)
                    sp.dma_start(bcol[:, :], d["phi_b_col"]).then_inc(loaded, 16)
                    sp.wait_ge(zeroed, 1)
                    for k in range(3):
                        sp.dma_start(rows[32 * k:32 * k + 1, :], d["phi_b"]).then_inc(loaded, 16)

                @block.gpsimd
                def _(g):
                    nc.gpsimd.memset(rows[:, :], 0.0).then_inc(zeroed, 1)
                    nc.gpsimd.memset(b3[:, :], 0.0)
                    nc.gpsimd.memset(ones3[:, :], 1.0)
                    ch = Count(sel_done)
                    nc.gpsimd.memset(blk[:, :], 0.0)
                    ch.up(nc.gpsimd.memset(selp[:, :], 0.0))
                    for k in range(3):
                        ch.settle(g)
                        ch.up(nc.gpsimd.affine_select(out=selp[:, :].rearrange("q (n p) -> q n p", n=4), in_=selp[:, :].rearrange("q (n p) -> q n p", n=4),
                                                      compare_op=ALU.not_equal, fill=1.0, base=-NS * k, pattern=[[0, 4], [-1, NS]], channel_multiplier=1))
                    for k in range(-3, 4):
                        ch.settle(g)
                        ch.up(nc.gpsimd.affine_select(out=blk[:, :], in_=blk[:, :], compare_op=ALU.not_equal,
                                                      fill=1.0, base=NS * k, pattern=[[-1, P]], channel_multiplier=1))
                    sel_n[0] = ch.n

                    def stage(z, par):
                        if not (isinstance(z, int) and z < 2):
                            g.wait_ge(x_done, 2 * z - 2)
                        nc.gpsimd.tensor_copy(xs[:, par, 0, :], xt[:, bass.ds(z * P, P)])
                        nc.gpsimd.tensor_copy(xs[:, par, 1, :], xn[:, bass.ds(z, 1), :]).then_inc(stg, 1)

                    def body(z, par):
                        if not (isinstance(z, int) and z == NT - 1):
                            stage(z + 1, 1 - par)
                        for hf in range(2):
                            g.wait_ge(r_ready, 2 * z + hf + 1)
                            if not (isinstance(z, int) and z == 0):
                                g.wait_ge(x_done, 2 * z + hf - 1)
                            nc.gpsimd.tensor_tensor(dn[:, hf, :, :], ls[:, hf, :, :], rs[:, hf, :].unsqueeze(2).broadcast_to([P, HE, NS]), ALU.mult)\
                                .then_inc(d_ready, 1)
                    g.wait_ge(xt_ready, 4)
                    stage(0, 0)
                    steps(g, body)

                @block.tensor
                def _(pe):
                    for ch in range(4):
                        pe.wait_ge(xn_ready, 4 * ch + 4)
                        for t in range(4):
                            last = nc.tensor.transpose(psum[:, ch, P * t:P * t + P], xn[:, 4 * ch + t, :], c["ident"][:, :])
                        last.then_inc(tp_done, 1)

                    def logits(z, par, hf):
                        if hf == 0:
                            pe.wait_ge(stg, z + 1)
                        if not (isinstance(z, int) and z == 0):
                            pe.wait_ge(sub_done, 2 * z + hf - 1)
                        for k in range(2):
                            bank = 2 * hf + k
                            nc.tensor.matmul(psum[:, bank, :], ones3[:, :], b3[:, W * bank:W * bank + W], start=True, stop=False)
                            last = nc.tensor.matmul(psum[:, bank, :], xs[:, par, 0, :], phi[:, W * bank:W * bank + W], start=False, stop=True)
                        last.then_inc(l_done, 1)

                    def gather(z, par, hf):
                        pe.wait_ge(d_ready, 2 * z + hf + 1)
                        for k in range(2):
                            last = nc.tensor.matmul(psum[:, 4 + 2 * hf + k, :], xs[:, par, 1, :], dn[:, hf, :, :].rearrange("p n s -> p (n s)")[:, W * k:W * k + W],
                                                    start=(isinstance(z, int) and z == 0), stop=(isinstance(z, int) and z == NT - 1))
                        last.then_inc(x_done, 1)

                    def body(z, par):
                        for hf in range(2):
                            if not (isinstance(z, int) and z == NT - 1):
                                logits(z + 1, 1 - par, hf)
                            gather(z, par, hf)

                    pe.wait_ge(loaded, 16 * 5)
                    pe.wait_ge(b_ready, 1)
                    pe.wait_ge(xt_ready, 4)
                    logits(0, 0, 0)
                    logits(0, 0, 1)
                    steps(pe, body)

                @block.scalar
                def _(act):
                    ln.root(act)
                    for ch in range(4):
                        act.wait_ge(tp_done, ch + 1)
                        nc.scalar.copy(xt[:, W * ch:W * ch + W], psum[:, ch, :]).then_inc(xt_ready, 1)

                    def body(z, par):
                        for hf in range(2):
                            act.wait_ge(sub_done, 2 * z + hf + 1)
                            part = ls[:, hf, :, :].rearrange("p n s -> p (n s)")
                            nc.scalar.activation(part, part, ACT.Exp).then_inc(exp_done, 1)
                    steps(act, body)

                @block.vector
                def _(dve):
                    v = nc.vector
                    for t in range(NT):
                        ln.tile_stats(t, x[:, t, :])
                    ln.finish(dve)
                    for t in range(NT):
                        ln.scale(t, xn[:, t, :], x[:, t, :]).then_inc(xn_ready, 1)
                    dve.wait_ge(loaded, 16 * 5)
                    dve.wait_ge(sel_done, sel_n[0])
                    bch.up(v.tensor_copy(rhi[:, :], rows[:, :]))
                    bch.settle(dve)
                    v.tensor_copy(b3[0:1, :], rhi[0:1, :])
                    bch.up(v.tensor_tensor(rows[:, :], rows[:, :], rhi[:, :], ALU.subtract))
                    bch.settle(dve)
                    bch.up(v.tensor_copy(rmid[:, :], rows[:, :]))
                    bch.settle(dve)
                    v.tensor_copy(b3[32:33, :], rmid[32:33, :])
                    v.tensor_tensor(b3[64:65, :], rows[64:65, :], rmid[64:65, :], ALU.subtract).then_inc(b_ready, 1)

                    def reduce(z, par, hf):
                        dve.wait_ge(l_done, 2 * z + hf + 1)
                        half = psum[:, 2 * hf:2 * hf + 2, :].rearrange("p b (n s) -> p (b n) s", s=NS)
                        v.tensor_reduce(mn[:, hf, :], half, AX_X, ALU.max).then_inc(maxed, 1)
                        v.tensor_reduce(part_max[:, hf, bass.ds(z, 1), :].rearrange("p o s -> p (o s)"), half.rearrange("p n s -> p s n"), AX_X, ALU.max)
                        if not (isinstance(z, int) and z == 0):
                            dve.wait_ge(d_ready, 2 * z + hf - 1)
                        dve.wait_ge(maxed, 2 * z + hf + 1)
                        v.tensor_tensor(ls[:, hf, :, :], half, mn[:, hf, :].unsqueeze(2).broadcast_to([P, HE, NS]), ALU.subtract).then_inc(sub_done, 1)

                    def sums(z, hf):
                        dve.wait_ge(exp_done, 2 * z + hf + 1)
                        v.tensor_reduce(sm[:, hf, :], ls[:, hf, :, :], AX_X, ALU.add).then_inc(summed, 1)
                        dve.wait_ge(summed, 2 * z + hf + 1)
                        v.reciprocal(rs[:, hf, :], sm[:, hf, :]).then_inc(r_ready, 1)

                    def body(z, par):
                        reduce(z, par, 0)
                        if not (isinstance(z, int) and z == 0):
                            sums(z - 1, 1)
                        reduce(z, par, 1)
                        sums(z, 0)
                    steps(dve, body)
                    sums(NT - 1, 1)
                    dve.wait_ge(x_done, 2 * NT)
                    for k in range(4):
                        v.tensor_scalar(xs_t[:, W * k:W * k + W], psum[:, 4 + k, :], -33000.0, 65000.0, ALU.max, ALU.min).then_inc(xs_ready, 1)

        with ExitStack() as ctx1:
            b = Alloc(nc, ctx1, "m1")
            ew = b.sb("expert_w", [P, NE, P])
            eb = b.sb("expert_b", [P, SL // P, P])
            nm3 = b.sb("neg_max_parts", [P, NT, P], BF16)
            nmax = b.sb("neg_max", [P, NT, NS])
            xh = b.sb("x_hat", [P, NT, P])
            xh_t = b.sb("x_hat_t", [P, SL])
            ln = Norm(nc, b, "ln", NT)
            ch = Count(b.sem("chain"))
            loaded, nat_done, xh_ready, tanh_done, back_done, back_ready, yt_done, yt_ready, nm_ready, mp_done, mp_ready = (b.sem(s) for s in (
                "loaded", "nat_psum", "xh_ready", "tanh_done", "back_psum", "back_ready", "yt_psum", "yt_ready", "nm_ready", "mp_psum", "mp_ready"))
            with nc.Block() as block:
                @block.sync
                def _(sp):
                    sp.dma_start(ew[:, :, :], d["expert_w"]).then_inc(loaded, 16)
                    for k in range(4):
                        sp.dma_start(eb[32 * k:32 * k + 32, :, :], d["expert_b"].rearrange("(j n) h -> n j h", n=4)[k:k + 1].broadcast_to([32, SL // P, P]))\
                            .then_inc(loaded, 16)

                @block.tensor
                def _(pe):
                    for t in range(NT):
                        last = nc.tensor.transpose(psum[:, t // 4, P * (t % 4):P * (t % 4) + P], xs_t[:, P * t:P * t + P], c["ident"][:, :])
                        if t % 4 == 3:
                            last.then_inc(nat_done, 1)
                    pe.wait_ge(nm_ready, 1)
                    for q in range(4):
                        bank = psum[:, 4 + q, 0:256].bitcast(BF16)
                        for t in range(4):
                            last = nc.tensor.transpose(bank[:, P * t:P * t + P], nm3[:, 4 * q + t, :], c["identb"][:, :])
                        last.then_inc(mp_done, 1)
                    pe.wait_ge(xh_ready, NT)
                    for q in range(4):
                        pe.wait_ge(tanh_done, 4 * q + 4)
                        for t in range(4 * q, 4 * q + 4):
                            last = nc.tensor.transpose(psum[:, q, P * (t % 4):P * (t % 4) + P], xh[:, t, :], c["ident"][:, :])
                        last.then_inc(back_done, 1)
                    pe.wait_ge(loaded, 80)
                    pe.wait_ge(mp_ready, 4)
                    for q in range(4):
                        pe.wait_ge(back_ready, q + 1)
                        for j in range(4):
                            for k in range(4):
                                n = 16 * q + 4 * j + k
                                last = nc.tensor.matmul(psum[32 * k:32 * k + 32, 4 + q, P * j:P * j + P], xh_t[:, NS * n:NS * n + NS], ew[:, n, :], start=True, stop=True)
                        last.then_inc(yt_done, 1)

                @block.scalar
                def _(act):
                    ln.root(act)
                    for q in range(4):
                        act.wait_ge(mp_done, q + 1)
                        nc.scalar.copy(mp_t[:, W * q:W * q + W], psum[:, 4 + q, 0:256].bitcast(BF16)).then_inc(mp_ready, 1)
                    for t in range(NT):
                        act.wait_ge(xh_ready, t + 1)
                        nc.scalar.activation(xh[:, t, :], xh[:, t, :], ACT.Tanh).then_inc(tanh_done, 1)
                    for q in range(4):
                        act.wait_ge(back_done, q + 1)
                        nc.scalar.copy(xh_t[:, W * q:W * q + W], psum[:, q, :]).then_inc(back_ready, 1)

                @block.vector
                def _(dve):
                    v = nc.vector
                    v.memset(nm3[:, :, 3 * NS:P], 0.0)
                    ch.up(v.tensor_tensor(nmax[:, :, :], part_max[:, 0, :, :], part_max[:, 1, :, :], ALU.max))
                    ch.settle(dve)
                    ch.up(v.tensor_scalar(nmax[:, :, :], nmax[:, :, :], -1.0, None, ALU.mult))
                    for k in range(2):
                        ch.settle(dve)
                        ch.up(v.tensor_copy(nm3[:, :, NS * k:NS * k + NS], nmax[:, :, :]))
                        ch.settle(dve)
                        ch.up(v.tensor_tensor(nmax[:, :, :], nmax[:, :, :], nm3[:, :, NS * k:NS * k + NS], ALU.subtract))
                    ch.settle(dve)
                    v.tensor_copy(nm3[:, :, 2 * NS:3 * NS], nmax[:, :, :]).then_inc(nm_ready, 1)
                    tile = lambda t: psum[:, t // 4, P * (t % 4):P * (t % 4) + P]
                    for t in range(NT):
                        if t % 4 == 0:
                            dve.wait_ge(nat_done, t // 4 + 1)
                        ln.tile_stats(t, tile(t))
                    ln.finish(dve)
                    for t in range(NT):
                        ln.scale(t, xh[:, t, :], tile(t)).then_inc(xh_ready, 1)
                    dve.wait_ge(loaded, 80)
                    for q in range(4):
                        dve.wait_ge(yt_done, q + 1)
                        v.tensor_tensor(yt[:, 4 * q:4 * q + 4, :], psum[:, 4 + q, :].rearrange("p (j h) -> p j h", j=4), eb[:, 4 * q:4 * q + 4, :], ALU.add)\
                            .then_inc(yt_ready, 1)

        with ExitStack() as ctx2:
            b = Alloc(nc, ctx2, "m2")
            NJ = SL // P
            ec = b.sb("exp", [P, 2, NJ, W])
            tot = b.sb("total", [P, 2, W])
            rt = b.sb("rtotal", [P, 2, W])
            y_t = b.sb("y_t", [P, T])
            y = b.sb("y", [P, NT, P])
            ln = Norm(nc, b, "ln", NT)
            l_done, exp_done, added, tot_ready, tot_done, rt_ready, scaled, y_done, yt_ready, nat_done, o_ready, stored = (b.sem(s) for s in (
                "l_psum", "exp_done", "added", "tot_ready", "tot_psum", "rt_ready", "scaled", "y_psum", "yt_ready", "nat_psum", "o_ready", "stored"))
            ych = Count(b.sem("y_chain"))
            NCH = T // W
            with nc.Block() as block:
                @block.tensor
                def _(pe):
                    def logits(ch, j):
                        n = NJ * ch + j
                        if n >= 4:
                            pe.wait_ge(exp_done, n - 3)
                        cols = slice(W * ch, W * ch + W)
                        nc.tensor.matmul(psum[:, n % 4, :], selp[:, :], mp_t[:, cols], start=True, stop=False)
                        nc.tensor.matmul(psum[:, n % 4, :], phi[:, P * j:P * j + P], xt[:, cols], start=False, stop=True).then_inc(l_done, 1)

                    def total(ch):
                        pe.wait_ge(tot_ready, ch + 1)
                        if ch >= 1:
                            pe.wait_ge(rt_ready, ch)
                        nc.tensor.matmul(psum[:, 4, :], blk[:, :], tot[:, ch % 2, :], start=True, stop=True).then_inc(tot_done, 1)

                    def combine(ch, j):
                        if ch >= 2 and j == 0:
                            pe.wait_ge(yt_ready, ch - 1)
                        pe.wait_ge(scaled, NJ * ch + j + 1)
                        ins = nc.tensor.matmul(psum[:, 5 + ch % 2, :], yt[:, j, :], ec[:, ch % 2, j, :], start=(j == 0), stop=(j == NJ - 1))
                        ins.then_inc(y_done, 1)

                    for j in range(NJ):
                        logits(0, j)
                    for ch in range(NCH):
                        if ch + 1 < NCH:
                            logits(ch + 1, 0)
                            logits(ch + 1, 1)
                        total(ch)
                        for j in range(NJ):
                            if ch + 1 < NCH and j + 2 < NJ:
                                logits(ch + 1, j + 2)
                            combine(ch, j)
                    pe.wait_ge(yt_ready, NCH)
                    for t in range(NT):
                        last = nc.tensor.transpose(psum[:, t // 4, P * (t % 4):P * (t % 4) + P], y_t[:, P * t:P * t + P], c["ident"][:, :])
                        if t % 4 == 3:
                            last.then_inc(nat_done, 1)

                @block.scalar
                def _(act):
                    for ch in range(NCH):
                        for j in range(NJ):
                            n = NJ * ch + j
                            act.wait_ge(l_done, n + 1)
                            if ch >= 2:
                                act.wait_ge(y_done, n - 2 * NJ + 1)
                                act.wait_ge(added, n - 2 * NJ + 1)
                            nc.scalar.activation(ec[:, ch % 2, j, :], psum[:, n % 4, :], ACT.Exp, bias=bcol[:, j:j + 1], scale=1.0).then_inc(exp_done, 1)
                        if ch >= 1:
                            act.wait_ge(y_done, NJ * ch)
                            nc.scalar.copy(y_t[:, W * (ch - 1):W * ch], psum[:, 5 + (ch - 1) % 2, :]).then_inc(yt_ready, 1)
                    act.wait_ge(y_done, NJ * NCH)
                    nc.scalar.copy(y_t[:, W * (NCH - 1):W * NCH], psum[:, 5 + (NCH - 1) % 2, :]).then_inc(yt_ready, 1)
                    ln.root(act)

                @block.gpsimd
                def _(g):
                    for ch in range(NCH):
                        for j in range(1, NJ):
                            n = NJ * ch + j
                            g.wait_ge(exp_done, n + 1)
                            if j == 1:
                                if ch >= 2:
                                    g.wait_ge(tot_done, ch - 1)
                                in0 = ec[:, ch % 2, 0, :]
                            else:
                                g.wait_ge(added, n)
                                in0 = tot[:, ch % 2, :]
                            ins = nc.gpsimd.tensor_tensor(tot[:, ch % 2, :], in0, ec[:, ch % 2, j, :], ALU.add)
                            ins.then_inc(added, 2 if j == 1 else 1)
                        g.wait_ge(added, NJ * (ch + 1))
                        g.sem_inc(tot_ready, 1)

                @block.vector
                def _(dve):
                    v = nc.vector
                    for ch in range(NCH):
                        dve.wait_ge(tot_done, ch + 1)
                        if ch >= 2:
                            dve.wait_ge(scaled, NJ * (ch - 1))
                        v.reciprocal(rt[:, ch % 2, :], psum[:, 4, :]).then_inc(rt_ready, 1)
                        dve.wait_ge(rt_ready, ch + 1)
                        for j in range(NJ):
                            v.tensor_tensor(ec[:, ch % 2, j, :], ec[:, ch % 2, j, :], rt[:, ch % 2, :], ALU.mult).then_inc(scaled, 1)
                    tile = lambda t: psum[:, t // 4, P * (t % 4):P * (t % 4) + P]
                    for t in range(NT):
                        if t % 4 == 0:
                            dve.wait_ge(nat_done, t // 4 + 1)
                        ln.tile_stats(t, tile(t))
                    ln.finish(dve)
                    for t in range(NT):
                        ych.up(ln.scale(t, y[:, t, :], tile(t)))
                    for t in range(NT):
                        dve.wait_ge(ych.sem, t + 1)
                        v.tensor_tensor(x[:, t, :], x[:, t, :], y[:, t, :], ALU.add).then_inc(o_ready, 1)

                @block.sync
                def _(sp):
                    for q in range(4):
                        sp.wait_ge(o_ready, 4 * q + 4)
                        sp.dma_start(out.rearrange("(t p) c -> p t c", p=P)[:, 4 * q:4 * q + 4, :], x[:, 4 * q:4 * q + 4, :]).then_inc(stored, 16)
                    sp.wait_ge(stored, 64)


def sandwich(nc, args, out):
    with ExitStack() as ctx:
        a = Alloc(nc, ctx, "all")
        x = a.sb("x", [P, 16, P])
        consts = dict(ident=a.sb("ident", [P, P]), identb=a.sb("ident_bf16", [P, P], BF16))
        with ExitStack() as ctx0:
            b = Alloc(nc, ctx0, "band")
            consts["mask"] = b.sb("mask", [P, 2, 256], BF16)
            consts["sel"] = b.sb("select", [P, 16, P], BF16)
            attention(nc, x, consts, args)
        with ExitStack() as ctx1:
            b = Alloc(nc, ctx1, "route")
            consts["ones"] = b.sb("ones", [P, P])
            consts["pair"] = b.sb("pair", [P, 64])
            kmoe(nc, x, consts, args)
        ssm(nc, x, consts, args)
        soft_moe(nc, x, consts, args, out)


def kernel(**inputs):
    import numpy as np
    from concourse import bacc
    from concourse.bass_utils import run_bass_kernel_spmd

    first = {name[len("L0_attn_"):]: np.asarray(v) for name, v in inputs.items() if name.startswith("L0_attn_")}
    moe = {name[len("L0_ffn_"):]: np.asarray(v) for name, v in inputs.items() if name.startswith("L0_ffn_")}
    mix = {name[len("L1_attn_"):]: np.asarray(v) for name, v in inputs.items() if name.startswith("L1_attn_")}
    soft = {name[len("L1_ffn_"):]: np.asarray(v) for name, v in inputs.items() if name.startswith("L1_ffn_")}
    laid = {
        "x": first["x"].reshape(2048, 128),
        "ident": np.eye(128, dtype=np.float32),
        "wqkv": first["Wqkv"], "bqkv": first["bqkv"], "wout": first["Wout"], "bout": first["bout"],
        "w_up": moe["W_up"].reshape(64, 8, 128).transpose(2, 1, 0),
        "b_up": moe["B_up"].transpose(2, 0, 1),
        "a_up": moe["A_up"].transpose(2, 0, 1),
        "w_down": moe["W_down"].reshape(64, 64, 64).transpose(2, 1, 0),
        "b_down": moe["B_down"].transpose(2, 0, 1),
        "a_down": moe["A_down"].transpose(2, 0, 1),
        "bias_up": moe["bias_up"].reshape(64, 64).T,
        "bias_down": moe["bias_down"].reshape(32, 32).T,
        "scale_up": moe["scale_up"].reshape(1, 1),
        "scale_down": moe["scale_down"].reshape(1, 1),
        "w_in": mix["W_in"].T,
        "conv_w": mix["conv_w"].reshape(2, 128, 4).transpose(1, 0, 2),
        "conv_b": mix["conv_b"].reshape(2, 128).T,
        "w_b": mix["W_B"].reshape(64, 2, 128).transpose(2, 1, 0),
        "w_c": mix["W_C"].T,
        "d_param": mix["D_param"].reshape(2, 128).T,
        "w_out": mix["W_out"].reshape(128, 2, 128).transpose(2, 1, 0),
        "gamma": mix["ln_gamma"].reshape(1, 128),
        "beta": mix["ln_beta"].reshape(1, 128),
        "phi": soft["phi_w"].T,
        "phi_b": soft["phi_b"].reshape(1, 2048),
        "phi_b_col": soft["phi_b"].reshape(16, 128).T,
        "expert_w": soft["expert_w"].transpose(1, 0, 2),
        "expert_b": soft["expert_b"],
    }
    nc = bacc.Bacc("TRN2", target_bir_lowering=False, num_devices=1)
    arrays, args = {}, {}
    for name, v in laid.items():
        arrays["in_" + name] = np.ascontiguousarray(v)
        args[name] = nc.dram_tensor("in_" + name, v.shape, F32, kind="ExternalInput").ap()
    out = nc.dram_tensor("out_rows", [2048, 128], F32, kind="ExternalOutput").ap()
    sandwich(nc, args, out)
    result = run_bass_kernel_spmd(nc, [arrays], core_ids=[0])
    return result.results[0]["out_rows"].reshape(1, 2048, 128)
```

```python
from contextlib import ExitStack

import concourse.bass as bass
from concourse import mybir

F32 = mybir.dt.float32
BF16 = mybir.dt.bfloat16
I32 = mybir.dt.int32
U32 = mybir.dt.uint32
ALU = mybir.AluOpType
ACT = mybir.ActivationFunctionType
AX_X = mybir.AxisListType.X

P = 128
NEG = -1.0e30
EPS = 1e-5


class Count:

    def __init__(self, sem):
        self.sem, self.n = sem, 0

    def up(self, ins):
        ins.then_inc(self.sem, 1)
        self.n += 1
        return self.n

    def settle(self, eng):
        eng.wait_ge(self.sem, self.n)


class Alloc:

    def __init__(self, nc, ctx, tag, cleared=None):
        self.nc, self.ctx, self.tag, self.cleared = nc, ctx, tag, cleared

    def sb(self, name, shape, dt=F32):
        return self.ctx.enter_context(self.nc.sbuf_tensor(f"{self.tag}_{name}", shape, dt))

    def ps(self, name, shape, dt=F32):
        return self.ctx.enter_context(self.nc.psum_tensor(f"{self.tag}_{name}", shape, dt))

    def sem(self, name):
        if self.cleared is not None:
            self.cleared.append(self.nc.alloc_semaphore(name=f"{self.tag}_{name}"))
            return self.cleared[-1]
        return self.ctx.enter_context(self.nc.semaphore(f"{self.tag}_{name}"))


class Norm:

    def __init__(self, nc, a, name, nt):
        self.nc, self.nt = nc, nt
        self.stats = a.sb(f"{name}_stats", [P, nt, 6])
        self.tmp = a.sb(f"{name}_tmp", [P, 8, nt])
        self.chain = Count(a.sem(f"{name}_chain"))
        self.var_ready = a.sem(f"{name}_var")
        self.std_ready = a.sem(f"{name}_std")

    def tile_stats(self, t, src):
        self.chain.up(self.nc.vector.bn_stats(self.stats[:, t, :], src))

    def finish(self, dve, t0=0, t1=None, mark=0):
        t1 = self.nt if t1 is None else t1
        v, tmp, st = self.nc.vector, self.tmp, self.stats
        col = lambda k: tmp[:, k, t0:t1]
        self.chain.settle(dve)
        me, mo, se, so = (st[:, t0:t1, k] for k in (1, 4, 2, 5))
        v.tensor_tensor(col(0), me, mo, ALU.add)
        v.tensor_tensor(col(1), me, mo, ALU.subtract)
        self.chain.up(v.tensor_tensor(col(3), se, so, ALU.add))
        self.chain.settle(dve)
        v.tensor_scalar(col(2), col(0), 0.5, None, ALU.mult)
        self.chain.up(v.scalar_tensor_tensor(out=col(4), in0=col(1), scalar=0.25, in1=col(1), op0=ALU.mult, op1=ALU.mult))
        self.chain.up(v.tensor_scalar(col(3), col(3), 1.0 / P, EPS, ALU.mult, ALU.add))
        self.chain.settle(dve)
        v.tensor_tensor(col(5), col(3), col(4), ALU.add).then_inc(self.var_ready, 1)
        dve.wait_ge(self.std_ready, mark + 1)
        self.chain.up(v.reciprocal(col(6), col(7)))
        self.chain.settle(dve)

    def root(self, act, t0=0, t1=None, mark=0):
        t1 = self.nt if t1 is None else t1
        act.wait_ge(self.var_ready, mark + 1)
        self.nc.scalar.activation(self.tmp[:, 7, t0:t1], self.tmp[:, 5, t0:t1], ACT.Sqrt).then_inc(self.std_ready, 1)

    def scale(self, t, dst, src):
        return self.nc.vector.tensor_scalar(dst, src, self.tmp[:, 2, t:t + 1], self.tmp[:, 6, t:t + 1],
                                            ALU.subtract, ALU.mult)


def attention(nc, x, c, d):
    H, DH, T = 16, 8, 2048
    NT = T // P
    NG, GH = 4, 4
    NP = H // 2
    NS = NT + 1
    TERMS_Q, TERMS_K = "hhmmhl", "hmhmlh"
    scale = DH ** -0.5

    with ExitStack() as ctx:
        used = []
        a = Alloc(nc, ctx, "at", used)
        qs = a.sb("q_stack", [P, NP, NS * P], BF16)
        ks = a.sb("k_stack", [P, NP, (NT + 2) * P], BF16)
        v9 = a.sb("v_and_one", [P, NT + 2, H, DH + 1])
        a_t = a.sb("attn_t", [P, NS * P])
        wout = a.sb("wout", [P, P])
        bout = a.sb("bout", [P, P])
        ln_y = Norm(nc, a, "ln_y", NT)
        stacked = a.sem("stacked")
        psum = a.ps("psum", [P, 8, 512])

        with ExitStack() as ctx0:
            b = Alloc(nc, ctx0, "pr", used)
            xn = b.sb("xn", [P, NT, P])
            xt = b.sb("xt", [P, T])
            wqkv = b.sb("wqkv", [P, 3 * P])
            bqk = b.sb("bqk", [P, 2])
            bq_s = b.sb("bq_scaled", [P, 1])
            bv = b.sb("bv", [P, P])
            full = b.sb("full", [P, 2, T])
            rest = b.sb("rest", [P, 2, T])
            part = {k: b.sb(f"part_{k}", [P, 2, T], BF16) for k in "hml"}
            flags = b.sb("flags", [16, NP * P], BF16)
            ln = Norm(nc, b, "ln_x", NT)
            loaded = b.sem("loaded")
            x_loaded = b.sem("x_loaded")
            filled, v9_filled = b.sem("filled"), b.sem("v9_filled")
            xn_ready = b.sem("xn_ready")
            tp_done = b.sem("tp_done")
            xt_ready = b.sem("xt_ready")
            proj_done = b.sem("proj_done")
            full_ready = b.sem("full_ready")
            hi_ready = b.sem("hi_ready")
            split_done = b.sem("split_done")
            v_ready = b.sem("v_ready")
            bq_ready = b.sem("bq_ready")
            dch = Count(b.sem("dve_chain"))
            NL = 6
            scratch = nc.dram_tensor("parts_scratch", [3, 2, P, T], BF16).ap()
            bounced = b.sem("bounced")
            with nc.Block() as block:
                @block.sync
                def _(sp):
                    sp.dma_start(x[:, :, :], d["x"].rearrange("(t p) c -> p t c", p=P)).then_inc(x_loaded, 16)
                    sp.dma_start(wqkv[:, :], d["wqkv"]).then_inc(loaded, 16)
                    sp.dma_start(bqk[:, :], d["bqkv"][0:2 * P].rearrange("(k p) -> p k", p=P), allow_slow_non_contiguous=True).then_inc(loaded, 16)
                    sp.dma_start(bv[:, :], d["bqkv"][2 * P:].rearrange("(a n) -> a n", a=1).broadcast_to([P, P])).then_inc(loaded, 16)
                    sp.dma_start(wout[:, :], d["wout"]).then_inc(loaded, 16)
                    sp.dma_start(bout[:, :], d["bout"].rearrange("(a n) -> a n", a=1).broadcast_to([P, P])).then_inc(loaded, 16)
                    sp.dma_start(c["ident"][:, :], d["ident"]).then_inc(loaded, 16)
                    sp.wait_ge(filled, 2)
                    for half in range(2):
                        for edge in (0, NT + 1):
                            sp.dma_start(ks[64 * half + 48:64 * half + 64, :, edge * P:(edge + 1) * P],
                                         flags[:, :].rearrange("r (j n) -> r j n", j=NP)).then_inc(stacked, 16)
                    for ch in range(2):
                        cols = slice(1024 * ch, 1024 * ch + 1024)
                        sp.wait_ge(split_done, 4 * ch + 4)
                        for k, kept in part.items():
                            sp.dma_start(scratch["hml".index(k), :, :, cols].rearrange("w p n -> p w n"), kept[:, :, cols]).then_inc(bounced, 16)
                        sp.wait_ge(bounced, 48 * ch + 48)
                        for which, (stack, terms, pad) in enumerate(((qs, TERMS_Q, 64), (ks, TERMS_K, P))):
                            for n, k in enumerate(terms):
                                rows = scratch["hml".index(k), which].rearrange("(j h r) n -> h r j n", j=NP, h=2)
                                for half in range(2):
                                    r0 = 64 * half + 8 * n
                                    sp.dma_start(stack[r0:r0 + 8, :, pad + 1024 * ch:pad + 1024 * ch + 1024], rows[half][:, :, cols])\
                                        .then_inc(stacked, 16)

                @block.gpsimd
                def _(g):
                    nc.gpsimd.memset(flags[:, :], NEG)
                    nc.gpsimd.memset(ks[:, :, :], 0.0)
                    nc.gpsimd.memset(qs[:, :, :], 1.0).then_inc(filled, 2)
                    ch = Count(b.sem("pool_chain"))
                    nc.gpsimd.memset(c["identb"][:, :], 0.0)
                    nc.gpsimd.memset(c["mask"][:, :, :], 0.0)
                    ch.up(nc.gpsimd.memset(c["sel"][:, :, :], 0.0))
                    ch.settle(g)
                    ch.up(nc.gpsimd.affine_select(out=c["identb"][:, :], in_=c["identb"][:, :], compare_op=ALU.not_equal,
                                                  fill=1.0, base=0, pattern=[[-1, P]], channel_multiplier=1))
                    ch.up(nc.gpsimd.affine_select(out=c["mask"][:, :, :], in_=c["mask"][:, :, :], compare_op=ALU.is_ge,
                                                  fill=NEG, base=0, pattern=[[0, 2], [1, 256]], channel_multiplier=-1))
                    ch.settle(g)
                    ch.up(nc.gpsimd.affine_select(out=c["mask"][:, :, :], in_=c["mask"][:, :, :], compare_op=ALU.is_ge,
                                                  fill=NEG, base=P, pattern=[[0, 2], [-1, 256]], channel_multiplier=1))
                    for k in range(3):
                        ch.settle(g)
                        ch.up(nc.gpsimd.affine_select(out=c["sel"][:, :, :], in_=c["sel"][:, :, :], compare_op=ALU.not_equal,
                                                      fill=1.0, base=-H * k, pattern=[[-1, H], [0, P]], channel_multiplier=1))

                @block.vector
                def _(dve):
                    nc.vector.memset(v9[:, :, :, :], 1.0).then_inc(v9_filled, 1)
                    dve.wait_ge(x_loaded, 16)
                    for t in range(NT):
                        ln.tile_stats(t, x[:, t, :])
                    ln.finish(dve)
                    for t in range(NT):
                        ln.scale(t, xn[:, t, :], x[:, t, :]).then_inc(xn_ready, 1)
                    dve.wait_ge(loaded, 16 * NL)
                    nc.vector.tensor_scalar(bq_s[:, :], bqk[:, 0:1], scale, None, ALU.mult).then_inc(bq_ready, 1)
                    dve.wait_ge(v9_filled, 1)
                    for ch in range(4):
                        cols = slice(512 * ch, 512 * ch + 512)
                        dve.wait_ge(proj_done, ch + 1)
                        nc.vector.tensor_tensor(v9[:, 1 + 4 * ch:5 + 4 * ch, :, 0:DH],
                                                psum[:, 4 + ch % 2, :].rearrange("p (t h d) -> p t h d", t=4, h=H),
                                                bv[:, :].rearrange("p (h d) -> p h d", h=H).unsqueeze(1).broadcast_to([P, 4, H, DH]),
                                                ALU.add).then_inc(v_ready, 1)
                        for w in range(2):
                            dve.wait_ge(hi_ready, 2 * ch + w + 1)
                            dch.up(nc.vector.tensor_tensor(rest[:, w, cols], full[:, w, cols], part["h"][:, w, cols], ALU.subtract))
                            dch.settle(dve)
                            dch.up(nc.vector.tensor_copy(part["m"][:, w, cols], rest[:, w, cols]))
                            dch.settle(dve)
                            nc.vector.tensor_tensor(part["l"][:, w, cols], rest[:, w, cols], part["m"][:, w, cols],
                                                    ALU.subtract).then_inc(split_done, 1)

                @block.scalar
                def _(act):
                    ln.root(act)
                    act.wait_ge(bq_ready, 1)
                    for ch in range(4):
                        act.wait_ge(tp_done, ch + 1)
                        nc.scalar.copy(xt[:, 512 * ch:512 * ch + 512], psum[:, ch % 2, :]).then_inc(xt_ready, 1)
                    for ch in range(4):
                        cols = slice(512 * ch, 512 * ch + 512)
                        act.wait_ge(proj_done, ch + 1)
                        nc.scalar.activation(full[:, 0, cols], psum[:, 2, :], ACT.Identity, bias=bq_s[:, 0:1], scale=scale).then_inc(full_ready, 1)
                        nc.scalar.activation(full[:, 1, cols], psum[:, 3, :], ACT.Identity, bias=bqk[:, 1:2], scale=1.0).then_inc(full_ready, 1)
                        for w in range(2):
                            act.wait_ge(full_ready, 2 * ch + w + 1)
                            nc.scalar.copy(part["h"][:, w, cols], full[:, w, cols]).then_inc(hi_ready, 1)

                @block.tensor
                def _(pe):
                    pe.wait_ge(loaded, 16 * NL)
                    for ch in range(4):
                        pe.wait_ge(xn_ready, 4 * ch + 4)
                        if ch >= 2:
                            pe.wait_ge(xt_ready, ch - 1)
                        for t in range(4):
                            last = nc.tensor.transpose(psum[:, ch % 2, P * t:P * t + P], xn[:, 4 * ch + t, :], c["ident"][:, :])
                        last.then_inc(tp_done, 1)
                    for ch in range(4):
                        pe.wait_ge(xt_ready, ch + 1)
                        if ch >= 1:
                            pe.wait_ge(full_ready, 2 * ch)
                        if ch >= 2:
                            pe.wait_ge(v_ready, ch - 1)
                        for w in range(2):
                            nc.tensor.matmul(psum[:, 2 + w, :], wqkv[:, w * P:w * P + P], xt[:, 512 * ch:512 * ch + 512], start=True, stop=True)
                        for t in range(4):
                            last = nc.tensor.matmul(psum[:, 4 + ch % 2, P * t:P * t + P], xt[:, 512 * ch + P * t:512 * ch + P * t + P],
                                                    wqkv[:, 2 * P:3 * P], start=True, stop=True)
                        last.then_inc(proj_done, 1)
        n_stacked = 16 * (2 * 24 + 4)

        with ExitStack() as ctx1:
            b = Alloc(nc, ctx1, "sc", used)
            kw = b.sb("k_window", [P, 2, NP, 2 * P], BF16)
            qw = b.sb("q_window", [P, 2, NP, P], BF16)
            negm = b.sb("neg_max", [P, H])
            nrest = b.sb("neg_max_rest", [P, H])
            nm3 = b.sb("neg_max_parts", [P, P], BF16)
            m_t = b.sb("neg_max_t", [P, 2, P], BF16)
            e = b.sb("exp", [P, 2, GH, 2, P])
            rec = b.sb("rec", [P, H])
            attn = b.sb("attn", [P, H, DH])
            vw = b.sb("v_window", [P, 2, 2, H, 32])
            o_sb = b.sb("values_t", [P, NG, P])
            y = b.sb("y", [P, NT, P])
            win, n_done, max_done, nm_ready, mtp, mt = (b.sem(s) for s in ("window", "nat_done", "max_done", "nm_ready", "mt_psum", "mt_ready"))
            t_done, exp_done, sel_done, pv_done = (b.sem(s) for s in ("t_done", "exp_done", "sel_done", "pv_done"))
            vwin, otp, o_done = (b.sem(s) for s in ("v_window", "values_psum", "values_sbuf"))
            norm_done, atp, at_done = (b.sem(s) for s in ("norm_done", "at_psum", "at_done"))
            proj, y_ready = b.sem("proj"), b.sem("y_ready")
            dch = b.sem("dve_chain")
            rch = b.sem("rec_chain")
            cleared = b.sem("cleared")
            sel_begun = b.sem("sel_begun")
            SN, ST, PV, MISC = 0, 4, 6, 7
            misc_bf = psum[:, MISC, 0:64].bitcast(BF16)

            def steps(eng, body):
                body(0, 0)
                with eng.Fori(0, (NS - 3) // 2) as i:
                    body(2 * i + 1, 1)
                    body(2 * i + 2, 0)
                body(NS - 2, 1)
                body(NS - 1, 0)

            with nc.Block() as block:
                @block.tensor
                def _(pe):
                    def natural(w, wp, g):
                        first = isinstance(w, int) and 4 * w + g < 2
                        if g == 0:
                            pe.wait_ge(win, w + 1)
                        if not first:
                            pe.wait_ge(max_done, 4 * w + g - 1)
                        for r in range(2):
                            nc.tensor.matmul(psum[:, SN + 2 * (g % 2) + r, :], c["identb"][:, :], c["mask"][:, :, :].rearrange("p a b -> p (a b)"),
                                             start=True, stop=False)
                        for u in range(2):
                            for r in range(2):
                                rows = slice(64 * r, 64 * r + 64)
                                last = nc.tensor.matmul(psum[:, SN + 2 * (g % 2) + r, 256 * u:256 * u + 256], qw[rows, wp, 2 * g + u, :],
                                                        kw[rows, wp, 2 * g + u, :], start=False, stop=(u == 1))
                        last.then_inc(n_done, 1)

                    def transposed(s, sp, g):
                        if g == 0:
                            pe.wait_ge(mt, s + 1)
                        if not (isinstance(s, int) and 4 * s + g < 1):
                            pe.wait_ge(exp_done, 4 * s + g)
                        for r in range(2):
                            for u in range(2):
                                nc.tensor.matmul(psum[:, ST + r, 256 * u:256 * u + 256].rearrange("p (j q) -> p j q", j=2), c["sel"][:, 4 * g + 2 * u + r, :],
                                                 m_t[:, sp, :].unsqueeze(1).broadcast_to([P, 2, P]), start=(u == 0), stop=False)
                        for u in range(2):
                            for j in range(2):
                                for r in range(2):
                                    rows = slice(64 * r, 64 * r + 64)
                                    last = nc.tensor.matmul(psum[:, ST + r, 256 * u + P * j:256 * u + P * j + P], kw[rows, sp, 2 * g + u, P * j:P * j + P],
                                                            qw[rows, sp, 2 * g + u, :], start=False, stop=(u == 1 and j == 1))
                        last.then_inc(t_done, 1)

                    def values(s, sp, g):
                        if g == 0:
                            pe.wait_ge(vwin, s + 1)
                            if not (isinstance(s, int) and s == 0):
                                pe.wait_ge(o_done, s)
                        pe.wait_ge(sel_done, 4 * s + g + 1)
                        for k in range(GH):
                            h = GH * g + 2 * (k % 2) + k // 2
                            for j in range(2):
                                last = nc.tensor.matmul(psum[32 * k:32 * k + 32, PV, P * g:P * g + P], vw[:, sp, j, h, :], e[:, g % 2, k, j, :],
                                                        start=(j == 0), stop=(j == 1))
                        last.then_inc(pv_done, 1)

                    def maxima_t(w):
                        pe.wait_ge(nm_ready, w + 1)
                        if not (isinstance(w, int) and w < 2):
                            pe.wait_ge(at_done, w - 1)
                        nc.tensor.transpose(misc_bf, nm3[:, :], c["identb"][:, :]).then_inc(mtp, 1)

                    def values_nat(s):
                        pe.wait_ge(o_done, s + 1)
                        for g in range(NG):
                            last = nc.tensor.transpose(psum[:, MISC, P * g:P * g + P], o_sb[:, g, :], c["ident"][:, :])
                        last.then_inc(otp, 1)

                    def attn_t(s):
                        pe.wait_ge(norm_done, s + 1)
                        nc.tensor.transpose(psum[:, MISC, 0:P], attn[:, :, :].rearrange("p h d -> p (h d)"), c["ident"][:, :]).then_inc(atp, 1)

                    def body(s, sp):
                        more = not (isinstance(s, int) and s == NS - 1)
                        late = not (isinstance(s, int) and s == 0)
                        nat = (lambda g: natural(s + 1, 1 - sp, g)) if more else (lambda g: None)
                        nat(0)
                        transposed(s, sp, 0)
                        if late:
                            values(s - 1, 1 - sp, 3)
                        nat(1)
                        if late:
                            values_nat(s - 1)
                        transposed(s, sp, 1)
                        nat(2)
                        values(s, sp, 0)
                        transposed(s, sp, 2)
                        nat(3)
                        values(s, sp, 1)
                        if late:
                            attn_t(s - 1)
                        transposed(s, sp, 3)
                        values(s, sp, 2)
                        if more:
                            maxima_t(s + 1)

                    pe.wait_ge(stacked, n_stacked)
                    for g in range(NG):
                        natural(0, 0, g)
                    maxima_t(0)
                    steps(pe, body)
                    values(NS - 1, 0, 3)
                    values_nat(NS - 1)
                    attn_t(NS - 1)
                    pe.wait_ge(at_done, NS)
                    for t in range(NT):
                        if t % 4 == 0 and t >= 8:
                            pe.wait_ge(y_ready, t - 4)
                        last = nc.tensor.matmul(psum[:, SN + (t // 4) % 2, P * (t % 4):P * (t % 4) + P], a_t[:, 64 + P * t:64 + P * t + P], wout[:, :],
                                                start=True, stop=True)
                        if t % 4 == 3:
                            last.then_inc(proj, 1)

                @block.vector
                def _(dve):
                    def window(w, wp):
                        nc.vector.tensor_copy(kw[:, wp, :, :], ks[:, :, bass.ds(w * P, 2 * P)])
                        nc.vector.tensor_copy(qw[:, wp, :, :], qs[:, :, bass.ds(w * P, P)]).then_inc(win, 1)

                    def window_v(w, wp):
                        nc.vector.tensor_copy(vw[:, wp, :, :, 0:DH + 1], v9[:, bass.ds(w, 2), :, :]).then_inc(vwin, 1)

                    def maxima(w, g):
                        dve.wait_ge(n_done, 4 * w + g + 1)
                        nc.vector.tensor_reduce(negm[:, GH * g:GH * g + GH].rearrange("p (u r) -> p r u", r=2),
                                                psum[:, SN + 2 * (g % 2):SN + 2 * (g % 2) + 2, :].rearrange("p r (u k) -> p r u k", u=2),
                                                AX_X, ALU.max, negate=True).then_inc(max_done, 1)

                    def parts(w):
                        dve.wait_ge(max_done, 4 * w + 4)
                        if not (isinstance(w, int) and w == 0):
                            dve.wait_ge(mtp, w)
                        nc.vector.tensor_copy(nm3[:, 0:H], negm[:, :]).then_inc(dch, 1)
                        dve.wait_ge(dch, 4 * w + 1)
                        nc.vector.tensor_tensor(nrest[:, :], negm[:, :], nm3[:, 0:H], ALU.subtract).then_inc(dch, 1)
                        dve.wait_ge(dch, 4 * w + 2)
                        nc.vector.tensor_copy(nm3[:, H:2 * H], nrest[:, :]).then_inc(dch, 1)
                        dve.wait_ge(dch, 4 * w + 3)
                        nc.vector.tensor_tensor(nm3[:, 2 * H:3 * H], nrest[:, :], nm3[:, H:2 * H], ALU.subtract).then_inc(nm_ready, 1)
                        dve.sem_inc(dch, 1)

                    def maxima_t(w, wp):
                        dve.wait_ge(mtp, w + 1)
                        if not (isinstance(w, int) and w < 2):
                            dve.wait_ge(t_done, 4 * w - 4)
                        nc.vector.tensor_copy(m_t[:, wp, :], misc_bf).then_inc(mt, 1)

                    def norm(s):
                        dve.wait_ge(otp, s + 1)
                        if not (isinstance(s, int) and s == 0):
                            dve.wait_ge(atp, s)
                        nat = psum[:, MISC, :].rearrange("p (g r u m) -> p g r u m", g=NG, r=2, u=2)
                        rv = rec[:, :].rearrange("p (g u r) -> p g r u", g=NG, u=2)
                        av = attn[:, :, :].rearrange("p (g u r) d -> p g r u d", g=NG, u=2)
                        nc.vector.reciprocal(rv, nat[:, :, :, :, DH]).then_inc(rch, 1)
                        dve.wait_ge(rch, s + 1)
                        for r in range(2):
                            last = nc.vector.tensor_tensor(av[:, :, r], nat[:, :, r, :, 0:DH], rv[:, :, r].unsqueeze(3).broadcast_to([P, NG, 2, DH]), ALU.mult)
                        last.then_inc(norm_done, 1)

                    def body(s, sp):
                        last = isinstance(s, int) and s == NS - 1
                        if not last:
                            maxima(s + 1, 0)
                        if last:
                            norm(s - 1)
                            return
                        if not (isinstance(s, int) and s == 0):
                            dve.wait_ge(pv_done, 4 * s)
                        window_v(s + 1, 1 - sp)
                        maxima(s + 1, 1)
                        if not (isinstance(s, int) and s == 0):
                            norm(s - 1)
                        maxima(s + 1, 2)
                        maxima(s + 1, 3)
                        parts(s + 1)
                        if not (isinstance(s, int) and s == NS - 2):
                            dve.wait_ge(t_done, 4 * s + 4)
                            window(s + 2, sp)
                        maxima_t(s + 1, 1 - sp)

                    nc.vector.memset(vw[:, :, :, :, :], 0.0)
                    nc.vector.memset(nm3[:, :], 0.0).then_inc(cleared, 1)
                    dve.wait_ge(cleared, 1)
                    dve.wait_ge(stacked, n_stacked)
                    window(0, 0)
                    window(1, 1)
                    window_v(0, 0)
                    for g in range(NG):
                        maxima(0, g)
                    parts(0)
                    maxima_t(0, 0)
                    steps(dve, body)
                    norm(NS - 1)
                    ych = Count(b.sem("y_chain"))
                    for t in range(NT):
                        if t % 4 == 0:
                            dve.wait_ge(proj, t // 4 + 1)
                        nc.vector.tensor_tensor(y[:, t, :], psum[:, SN + (t // 4) % 2, P * (t % 4):P * (t % 4) + P], bout[:, :], ALU.add).then_inc(y_ready, 1)
                        dve.wait_ge(y_ready, t + 1)
                        ln_y.tile_stats(t, y[:, t, :])
                    ln_y.finish(dve)
                    for t in range(NT):
                        ych.up(ln_y.scale(t, y[:, t, :], y[:, t, :]))
                    for t in range(NT):
                        dve.wait_ge(ych.sem, t + 1)
                        nc.vector.tensor_tensor(x[:, t, :], x[:, t, :], y[:, t, :], ALU.add)

                @block.scalar
                def _(act):
                    def exps(s, g):
                        act.wait_ge(t_done, 4 * s + g + 1)
                        if not (isinstance(s, int) and 4 * s + g < 2):
                            act.wait_ge(pv_done, 4 * s + g - 1)
                        nc.scalar.activation(e[:, g % 2, :, :, :].rearrange("p h j q -> p (h j q)"),
                                             psum[:, ST:ST + 2, :].rearrange("p b n -> p (b n)"), ACT.Exp).then_inc(exp_done, 1)

                    def attn_t(s):
                        act.wait_ge(atp, s + 1)
                        nc.scalar.copy(a_t[:, bass.ds(s * P, P)], psum[:, MISC, 0:P]).then_inc(at_done, 1)

                    def values_out(s):
                        act.wait_ge(pv_done, 4 * s + 4)
                        if not (isinstance(s, int) and s == 0):
                            act.wait_ge(otp, s)
                        nc.scalar.copy(o_sb[:, :, :].rearrange("p g q -> p (g q)"), psum[:, PV, :]).then_inc(o_done, 1)

                    def body(s, sp):
                        late = not (isinstance(s, int) and s == 0)
                        exps(s, 0)
                        if late:
                            values_out(s - 1)
                        exps(s, 1)
                        exps(s, 2)
                        if late:
                            attn_t(s - 1)
                        exps(s, 3)

                    steps(act, body)
                    values_out(NS - 1)
                    attn_t(NS - 1)
                    ln_y.root(act)

                @block.gpsimd
                def _(pool):
                    def body(s, sp):
                        for g in range(NG):
                            pool.wait_ge(exp_done, 4 * s + g + 1)
                            pool.sem_inc(sel_begun, 1)
                            nc.gpsimd.affine_select(out=e[:, g % 2, :, 0, :], in_=e[:, g % 2, :, 0, :], compare_op=ALU.is_ge,
                                                    fill=0.0, base=0, pattern=[[0, GH], [-1, P]], channel_multiplier=1)
                            nc.gpsimd.affine_select(out=e[:, g % 2, :, 1, :], in_=e[:, g % 2, :, 1, :], compare_op=ALU.is_ge,
                                                    fill=0.0, base=0, pattern=[[0, GH], [1, P]], channel_multiplier=-1).then_inc(sel_done, 1)
                    steps(pool, body)
        nc.clear_and_free_semaphores(used)
        nc.all_engine_barrier()


def kmoe(nc, x, c, d):
    T, R, E = 256, 8, 64
    D1, F1 = 32, 64
    NT, H, K = 16, 2, 2
    N = T // H
    NG = N // 2
    W = 512
    with ExitStack() as ctx:
        a = Alloc(nc, ctx, "ff")
        psum = a.ps("psum", [P, 8, W])
        h = a.sb("h", [P, N, F1])
        wdn = a.sb("w_down", [P, F1, H, E])
        bias_up = a.sb("bias_up", [P, F1])
        bias_dn = a.sb("bias_down", [D1, D1])
        scales = a.sb("scales", [P, 2])
        ids = a.sb("expert_ids", [P, E])
        lg = a.sb("logits", [P, H, E])
        mx = a.sb("top_values", [P, H, 8])
        ix = a.sb("top_index", [P, H, 8], U32)
        ef = a.sb("experts", [P, H, K])
        dv = a.sb("gap", [P, H])
        ev = a.sb("gap_exp", [P, H])
        pr = a.sb("probs", [P, K, H])
        oh = a.sb("one_hot", [P, 2, K, H, E])
        oht = a.sb("one_hot_t", [P, 2, K, N])
        loaded, down_loaded = a.sem("loaded"), a.sem("down_loaded")
        rch = Count(a.sem("route_chain"))
        gap_ready, exp_ready, oh_ready, oh_tp, routed = (a.sem(s) for s in ("gap_ready", "exp_ready", "one_hot_ready", "one_hot_psum", "routed"))

        def route_dve(dve, n, src):
            v = nc.vector
            rch.up(v.tensor_copy(lg[:, :, :], src))
            rch.settle(dve)
            for t in range(H):
                rch.up(v.max(mx[:, t, :], lg[:, t, :]))
            rch.settle(dve)
            v.tensor_tensor(dv[:, :], mx[:, :, 1], mx[:, :, 0], ALU.subtract).then_inc(gap_ready, 1)
            for t in range(H):
                rch.up(v.max_index(ix[:, t, :], mx[:, t, :], lg[:, t, :]))
            rch.settle(dve)
            rch.up(v.tensor_copy(ef[:, :, :], ix[:, :, 0:K]))
            rch.settle(dve)
            for k in range(K):
                for t in range(H):
                    v.tensor_scalar(oh[:, 0, k, t, :], ids[:, :], ef[:, t, k:k + 1], None, ALU.is_equal)
            dve.wait_ge(exp_ready, n + 1)
            rch.up(v.tensor_scalar(dv[:, :], ev[:, :], 1.0, None, ALU.add))
            rch.settle(dve)
            rch.up(v.reciprocal(pr[:, 0, :], dv[:, :]))
            rch.settle(dve)
            rch.up(v.tensor_tensor(pr[:, 1, :], ev[:, :], pr[:, 0, :], ALU.mult))
            rch.settle(dve)
            for k in range(K):
                for t in range(H):
                    last = v.tensor_scalar(oh[:, 1, k, t, :], ids[:, :], ef[:, t, k:k + 1], pr[:, k, t:t + 1], ALU.is_equal, ALU.mult)
            last.then_inc(oh_ready, 1)
            dve.wait_ge(oh_tp, n + 1)
            v.tensor_copy(oht[:, :, :, :].rearrange("p a k n -> p (a k n)"), psum[:, 5, :]).then_inc(routed, 1)

        def route_act(act, n):
            act.wait_ge(gap_ready, n + 1)
            nc.scalar.activation(ev[:, :], dv[:, :], ACT.Exp).then_inc(exp_ready, 1)

        def route_pe(pe, n):
            pe.wait_ge(oh_ready, n + 1)
            for kind in range(2):
                for k in range(K):
                    m = K * kind + k
                    last = nc.tensor.transpose(psum[:, 5, P * m:P * m + P], oh[:, kind, k, :, :].rearrange("p h e -> p (h e)"), c["ident"][:, :])
            last.then_inc(oh_tp, 1)

        def emptied(pe, u, act_done, dve_done):
            if u >= 4:
                pe.wait_ge(act_done if u % 2 == 0 else dve_done, (u - 4) // 2 + 1)

        with ExitStack() as ctx0:
            b0 = Alloc(nc, ctx0, "f0")
            x4 = b0.sb("x_blocks", [P, NG, P])
            gb = b0.sb("b_taken", [P, NG, K, F1])
            ga = b0.sb("a_taken", [P, NG, K, F1])

            with ExitStack() as ctx1:
                b = Alloc(nc, ctx1, "f1")
                flat = h[:, :, :].rearrange("p n o -> p (n o)")
                xt = flat[:, 0:T * R]
                xn = flat[:, T * R:2 * T * R].rearrange("p (t n) -> p t n", t=NT)
                wup = ga[:, 0:R // 2, :, :].rearrange("p g k n -> p (g k) n")
                bup = b.sb("b_up", [P, F1, H, D1])
                aup = b.sb("a_up", [P, F1, H, D1])
                ln = Norm(nc, b, "ln", NT)
                zeroed = b.sem("zeroed")
                wup_loaded, b_loaded, a_loaded = (b.sem(s) for s in ("w_up_loaded", "b_loaded", "a_loaded"))
                xn_ready, tp_done, xt_ready, lg_done, x4_part, got, act_took, dve_took = (b.sem(s) for s in (
                    "xn_ready", "tp_done", "xt_ready", "lg_done", "x_block", "got_psum", "act_took", "dve_took"))
                UB = F1 // 4

                def took(u):
                    dst = (gb, ga)[u // UB]
                    col = 4 * (u % UB)
                    return dst[:, :, :, col:col + 4].rearrange("p g k c -> p k g c"), psum[:, u % 4, :].rearrange("p (c k g) -> p k g c", c=4, k=K)

                with nc.Block() as block:
                    @block.sync
                    def _(sp):
                        sp.dma_start(wup[:, :, :], d["w_up"]).then_inc(wup_loaded, 16)
                        sp.dma_start(ids[:, :], d["expert_ids"].broadcast_to([P, E])).then_inc(wup_loaded, 16)
                        for t in range(H):
                            sp.dma_start(bup[E * t:E * t + E, :, t, :], d["b_up"]).then_inc(b_loaded, 16)
                        for t in range(H):
                            sp.dma_start(aup[E * t:E * t + E, :, t, :], d["a_up"]).then_inc(a_loaded, 16)
                        for t in range(H):
                            sp.dma_start(bias_up[E * t:E * t + E, :], d["bias_up"]).then_inc(loaded, 16)
                        sp.dma_start(bias_dn[:, :], d["bias_down"]).then_inc(loaded, 16)
                        sp.dma_start(scales[:, 0:1], d["scale_up"].broadcast_to([P, 1])).then_inc(loaded, 16)
                        sp.dma_start(scales[:, 1:2], d["scale_down"].broadcast_to([P, 1])).then_inc(loaded, 16)
                        for t in range(H):
                            sp.dma_start(wdn[E * t:E * t + E, :, t, :], d["w_down"]).then_inc(down_loaded, 16)

                    @block.gpsimd
                    def _(g):
                        ch = Count(zeroed)
                        for n, part in enumerate((bup, aup, x4, wdn)):
                            if part is x4:
                                ch.settle(g)
                                ch.up(nc.gpsimd.memset(part[:, :, :], 0.0))
                                continue
                            for t in range(H):
                                ch.settle(g) if ch.n else None
                                ch.up(nc.gpsimd.memset(part[E * t:E * t + E, :, 1 - t, :], 0.0))
                    B_ZERO, A_ZERO, X_ZERO, W_ZERO = 2, 4, 5, 7

                    @block.vector
                    def _(dve):
                        for t in range(NT):
                            ln.tile_stats(t, x[:, t, :])
                        ln.finish(dve)
                        for t in range(NT):
                            ln.scale(t, xn[:, t, :], x[:, t, :]).then_inc(xn_ready, 1)
                        dve.wait_ge(wup_loaded, 32)
                        dve.wait_ge(lg_done, 1)
                        route_dve(dve, 0, psum[:, 4, 0:H * E].rearrange("p (t e) -> p t e", t=H))
                        for u in range(1, 2 * UB, 2):
                            dve.wait_ge(got, u + 1)
                            dst, src = took(u)
                            for k in range(K):
                                last = nc.vector.tensor_copy(dst[:, k], src[:, k])
                            last.then_inc(dve_took, 1)

                    @block.scalar
                    def _(act):
                        ln.root(act)
                        for ch in range(4):
                            act.wait_ge(tp_done, ch + 1)
                            nc.scalar.copy(xt[:, W * ch:W * ch + W], psum[:, ch, :]).then_inc(xt_ready, 1)
                        act.wait_ge(xt_ready, 4)
                        act.wait_ge(zeroed, X_ZERO)
                        rows = xt.rearrange("p (m g t r) -> p m t g r", m=2, t=H, r=R)

                        def blocks(q):
                            for m in range(2):
                                for t in range(H):
                                    tok = 2 * m + t
                                    dst = x4[32 * tok:32 * tok + 32, :, 32 * tok:32 * tok + 32].rearrange("p g (r q) -> p q g r", q=4)
                                    nc.scalar.copy(dst[:, q], rows[32 * q:32 * q + 32, m, t]).then_inc(x4_part, 1)
                        blocks(0)
                        blocks(1)
                        route_act(act, 0)
                        blocks(2)
                        blocks(3)
                        for u in range(0, 2 * UB, 2):
                            act.wait_ge(got, u + 1)
                            dst, src = took(u)
                            for k in range(K):
                                last = nc.scalar.copy(dst[:, k], src[:, k])
                            last.then_inc(act_took, 1)

                    @block.tensor
                    def _(pe):
                        for ch in range(4):
                            pe.wait_ge(xn_ready, 4 * ch + 4)
                            for t in range(4):
                                last = nc.tensor.transpose(psum[:, ch, P * t:P * t + P], xn[:, 4 * ch + t, :], c["ident"][:, :])
                            last.then_inc(tp_done, 1)
                        pe.wait_ge(wup_loaded, 32)
                        pe.wait_ge(xt_ready, 4)
                        rows = xt.rearrange("p (n t r) -> p t r n", t=H, r=R)
                        for t in range(H):
                            for r in range(R):
                                last = nc.tensor.matmul(psum[:, 4, E * t:E * t + E], rows[:, t, r], wup[:, r, :], start=(r == 0), stop=(r == R - 1))
                        last.then_inc(lg_done, 1)
                        route_pe(pe, 0)
                        pe.wait_ge(routed, 1)
                        for u in range(2 * UB):
                            if u == 0:
                                pe.wait_ge(b_loaded, 16 * H)
                                pe.wait_ge(zeroed, B_ZERO)
                            if u == UB:
                                pe.wait_ge(a_loaded, 16 * H)
                                pe.wait_ge(zeroed, A_ZERO)
                            emptied(pe, u, act_took, dve_took)
                            for col in range(4):
                                factor = (bup, aup)[u // UB][:, 4 * (u % UB) + col, :, :].rearrange("p h j -> p (h j)")
                                for m in range(2):
                                    last = nc.tensor.matmul(psum[64 * m:64 * m + 64, u % 4, P * col:P * col + P], factor, oht[:, u // UB, :, NG * m:NG * m + NG],
                                                            start=True, stop=True)
                            last.then_inc(got, 1)

            with ExitStack() as ctx1:
                b = Alloc(nc, ctx1, "f2")
                CG, NCH = 8, NG // 8
                z = b.sb("z", [P, 2, CG, K, F1])
                z_done, z_ready, h_done, hb_ready, gelu_done = (b.sem(s) for s in ("z_psum", "z_ready", "h_psum", "h_biased", "gelu_done"))
                with nc.Block() as block:
                    @block.tensor
                    def _(pe):
                        def first(ch):
                            for half in range(2):
                                if ch >= 1:
                                    pe.wait_ge(z_ready, 2 * (ch - 1) + half + 1)
                                for k in range(4):
                                    g = CG * ch + 4 * half + k
                                    last = nc.tensor.matmul(psum[:, half, P * k:P * k + P], x4[:, g, :], gb[:, g, :, :].rearrange("p k n -> p (k n)"), start=True, stop=True)
                                last.then_inc(z_done, 1)

                        def second(ch):
                            pe.wait_ge(z_ready, 2 * ch + 2)
                            for tok in range(4):
                                u = 4 * ch + tok
                                rows, t = slice(32 * tok, 32 * tok + 32), tok % 2
                                if u >= 6:
                                    pe.wait_ge(hb_ready, u - 5)
                                for g in range(CG):
                                    for k in range(K):
                                        last = nc.tensor.matmul(psum[64 * t:64 * t + 64, 2 + u % 6, F1 * g:F1 * g + F1], z[rows, ch % 2, g, k, :], ga[rows, CG * ch + g, k, :],
                                                                start=(k == 0), stop=(k == K - 1))
                                last.then_inc(h_done, 1)
                        first(0)
                        for ch in range(NCH):
                            if ch + 1 < NCH:
                                first(ch + 1)
                            second(ch)

                    @block.vector
                    def _(dve):
                        dve.wait_ge(loaded, 16 * 5)
                        for ch in range(NCH):
                            for tok in range(4):
                                u = 4 * ch + tok
                                rows, n0 = slice(64 * (tok % 2), 64 * (tok % 2) + 64), NG * (tok // 2) + CG * ch
                                dve.wait_ge(h_done, u + 1)
                                nc.vector.scalar_tensor_tensor(out=h[rows, n0:n0 + CG, :], in0=psum[rows, 2 + u % 6, :].rearrange("p (g o) -> p g o", g=CG),
                                                               scalar=scales[rows, 0:1], in1=bias_up[rows, :].unsqueeze(1).broadcast_to([64, CG, F1]),
                                                               op0=ALU.mult, op1=ALU.add).then_inc(hb_ready, 1)

                    @block.scalar
                    def _(act):
                        def take(ch):
                            if ch >= 2:
                                act.wait_ge(h_done, 4 * (ch - 1))
                            for half in range(2):
                                act.wait_ge(z_done, 2 * ch + half + 1)
                                nc.scalar.copy(z[:, ch % 2, 4 * half:4 * half + 4, :, :].rearrange("p g k n -> p (g k n)"), psum[:, half, :]).then_inc(z_ready, 1)

                        def gelu(ch):
                            act.wait_ge(hb_ready, 4 * ch + 4)
                            for m in range(2):
                                part = h[:, NG * m + CG * ch:NG * m + CG * ch + CG, :].rearrange("p n o -> p (n o)")
                                nc.scalar.activation(part, part, ACT.Gelu).then_inc(gelu_done, 1)
                        take(0)
                        for ch in range(NCH):
                            if ch + 1 < NCH:
                                take(ch + 1)
                            if ch >= 1:
                                gelu(ch - 1)
                        gelu(NCH - 1)

        with ExitStack() as ctx0:
            b = Alloc(nc, ctx0, "f3")
            bdn = b.sb("b_down", [P, D1, H, F1])
            adn = b.sb("a_down", [P, D1, H, F1])
            gb = b.sb("b_taken", [P, N, K, D1])
            ga = b.sb("a_taken", [P, N, K, D1])
            vs = b.sb("v", [P, 2, 8, K, D1])
            yb = wdn[0:D1, :, :, :].rearrange("p o h e -> p (o h e)").rearrange("p (t a) -> p t a", t=T)
            lgt = b.sb("logits_t", [P, N])
            ln = Norm(nc, b, "ln", NT)
            lg_done, lgt_ready, lg_nat, zeroed, b_loaded, a_loaded = (b.sem(s) for s in ("lgt_psum", "lgt_ready", "lg_nat", "zeroed", "b_loaded", "a_loaded"))
            got, act_took, dve_took = (b.sem(s) for s in ("got_psum", "act_took", "dve_took"))
            v_done, v_ready, y_done, y_ready, nat_done = (b.sem(s) for s in ("v_psum", "v_ready", "y_psum", "y_ready", "nat_done"))
            ych = Count(b.sem("y_chain"))
            UB = D1 // 2
            CP, NCH = 8, N // 8

            def took(u):
                dst = (gb, ga)[u // UB]
                col = 2 * (u % UB)
                return dst[:, :, :, col:col + 2].rearrange("p n k c -> p k n c"), psum[:, u % 4, :].rearrange("p (c k n) -> p k n c", c=2, k=K)

            with nc.Block() as block:
                @block.sync
                def _(sp):
                    for t in range(H):
                        sp.dma_start(bdn[E * t:E * t + E, :, t, :], d["b_down"]).then_inc(b_loaded, 16)
                    for t in range(H):
                        sp.dma_start(adn[E * t:E * t + E, :, t, :], d["a_down"]).then_inc(a_loaded, 16)

                @block.gpsimd
                def _(g):
                    ch = Count(zeroed)
                    for part in (bdn, adn):
                        for t in range(H):
                            ch.settle(g) if ch.n else None
                            ch.up(nc.gpsimd.memset(part[E * t:E * t + E, :, 1 - t, :], 0.0))

                @block.tensor
                def _(pe):
                    pe.wait_ge(down_loaded, 32)
                    for o in range(F1):
                        last = nc.tensor.matmul(psum[:, 4, 0:N], wdn[:, o, :, :].rearrange("p h e -> p (h e)"), h[:, :, o], start=(o == 0), stop=(o == F1 - 1))
                    last.then_inc(lg_done, 1)
                    pe.wait_ge(lgt_ready, 1)
                    nc.tensor.transpose(psum[:, 6, 0:P], lgt[:, :], c["ident"][:, :]).then_inc(lg_nat, 1)
                    route_pe(pe, 1)
                    pe.wait_ge(routed, 2)
                    for u in range(2 * UB):
                        if u == 0:
                            pe.wait_ge(b_loaded, 32)
                            pe.wait_ge(zeroed, 2)
                        if u == UB:
                            pe.wait_ge(a_loaded, 32)
                            pe.wait_ge(zeroed, 4)
                        emptied(pe, u, act_took, dve_took)
                        for col in range(2):
                            factor = (bdn, adn)[u // UB][:, 2 * (u % UB) + col, :, :].rearrange("p h j -> p (h j)")
                            last = nc.tensor.matmul(psum[:, u % 4, 256 * col:256 * col + 256], factor, oht[:, u // UB, :, :].rearrange("p k n -> p (k n)"), start=True, stop=True)
                        last.then_inc(got, 1)

                    def first(ch):
                        for t in range(H):
                            rows = slice(64 * t, 64 * t + 64)
                            if ch >= 1:
                                pe.wait_ge(v_ready, H * (ch - 1) + t + 1)
                            for n in range(CP):
                                last = nc.tensor.matmul(psum[rows, 4 + t, F1 * n:F1 * n + F1], h[rows, CP * ch + n, :], gb[rows, CP * ch + n, :, :].rearrange("p k n -> p (k n)"),
                                                        start=True, stop=True)
                            last.then_inc(v_done, 1)

                    def second(ch):
                        for t in range(H):
                            rows = slice(64 * t, 64 * t + 64)
                            pe.wait_ge(v_ready, H * ch + t + 1)
                            if ch >= 2:
                                pe.wait_ge(y_ready, H * (ch - 2) + t + 1)
                            for n in range(CP):
                                for k in range(K):
                                    last = nc.tensor.matmul(psum[0:D1, (6, 0)[ch % 2] + t, D1 * n:D1 * n + D1], vs[rows, ch % 2, n, k, :], ga[rows, CP * ch + n, k, :],
                                                            start=(k == 0), stop=(k == K - 1))
                            last.then_inc(y_done, 1)
                    pe.wait_ge(act_took, UB)
                    pe.wait_ge(dve_took, UB)
                    first(0)
                    for ch in range(NCH):
                        if ch + 1 < NCH:
                            first(ch + 1)
                        second(ch)
                    pe.wait_ge(y_ready, H * NCH)
                    quarters = yb.rearrange("b t (r q) -> b q (t r)", q=4)
                    for t in range(NT):
                        for q in range(4):
                            last = nc.tensor.transpose(psum[:, 2 + t // 4, P * (t % 4) + 32 * q:P * (t % 4) + 32 * q + 32], quarters[:, q, P * t:P * t + P],
                                                       c["ident"][0:D1, 0:D1])
                        if t % 4 == 3:
                            last.then_inc(nat_done, 1)

                @block.vector
                def _(dve):
                    dve.wait_ge(lg_nat, 1)
                    route_dve(dve, 1, psum[:, 6, 0:P].rearrange("p (t e) -> p t e", t=H))
                    for u in range(1, 2 * UB, 2):
                        dve.wait_ge(got, u + 1)
                        dst, src = took(u)
                        for k in range(K):
                            last = nc.vector.tensor_copy(dst[:, k], src[:, k])
                        last.then_inc(dve_took, 1)
                    pairs = yb.rearrange("b (n t) a -> b t n a", t=H)
                    for ch in range(NCH):
                        for t in range(H):
                            dve.wait_ge(y_done, H * ch + t + 1)
                            nc.vector.scalar_tensor_tensor(out=pairs[:, t, CP * ch:CP * ch + CP, :], in0=psum[0:D1, (6, 0)[ch % 2] + t, 0:CP * D1].rearrange("p (n a) -> p n a", n=CP),
                                                           scalar=scales[0:D1, 1:2], in1=bias_dn[:, :].unsqueeze(1).broadcast_to([D1, CP, D1]),
                                                           op0=ALU.mult, op1=ALU.add).then_inc(y_ready, 1)
                    tile = lambda t: psum[:, 2 + t // 4, P * (t % 4):P * (t % 4) + P]
                    for t in range(NT):
                        if t % 4 == 0:
                            dve.wait_ge(nat_done, t // 4 + 1)
                        ln.tile_stats(t, tile(t))
                    ln.finish(dve)
                    y = gb[:, 0:32, :, :].rearrange("p n k a -> p (n k a)").rearrange("p (t n) -> p t n", t=NT)
                    for t in range(NT):
                        ych.up(ln.scale(t, y[:, t, :], tile(t)))
                    for t in range(NT):
                        dve.wait_ge(ych.sem, t + 1)
                        nc.vector.tensor_tensor(x[:, t, :], x[:, t, :], y[:, t, :], ALU.add)

                @block.scalar
                def _(act):
                    act.wait_ge(lg_done, 1)
                    nc.scalar.copy(lgt[:, :], psum[:, 4, 0:N]).then_inc(lgt_ready, 1)
                    route_act(act, 1)
                    for u in range(0, 2 * UB, 2):
                        act.wait_ge(got, u + 1)
                        dst, src = took(u)
                        for k in range(K):
                            last = nc.scalar.copy(dst[:, k], src[:, k])
                        last.then_inc(act_took, 1)
                    for ch in range(NCH):
                        for t in range(H):
                            rows = slice(64 * t, 64 * t + 64)
                            act.wait_ge(v_done, H * ch + t + 1)
                            if ch >= 2:
                                act.wait_ge(y_done, H * (ch - 2) + t + 1)
                            nc.scalar.copy(vs[rows, ch % 2, :, :, :].rearrange("p n k b -> p (n k b)"), psum[rows, 4 + t, :]).then_inc(v_ready, 1)
                    ln.root(act)


def ssm(nc, x, c, d):
    T, NT, NC, W = 2048, 16, 4, 512
    NB, S, K = 2, 64, 4
    with ExitStack() as ctx:
        a = Alloc(nc, ctx, "sm")
        psum = a.ps("psum", [P, 8, W])
        xn = a.sb("xn", [P, NT, P])
        xt = a.sb("xt", [P, T])
        w_in = a.sb("w_in", [P, 2 * NB * P])
        cw = a.sb("conv_w", [P, NB, K])
        cb = a.sb("conv_b", [P, NB])
        wb = a.sb("w_b", [P, NB, S])
        wc = a.sb("w_c", [S, NB * P])
        dp = a.sb("d_param", [P, NB])
        wo = a.sb("w_out", [P, NB, P])
        gamma = a.sb("gamma", [P, P])
        beta = a.sb("beta", [P, P])
        xin = a.sb("x_in", [P, NB, K - 1 + T])
        gate = a.sb("gate", [P, NB, T])
        u = a.sb("u", [P, NB, T])
        bu = a.sb("bu", [S, T])
        decay = a.sb("decay", [S, W])
        hs = a.sb("states", [S, T])
        yg = a.sb("y_gated", [P, NB, T])
        z = a.sb("z", [P, NT, P])
        ln_x, ln_z, ln_o = (Norm(nc, a, n, NT) for n in ("ln_x", "ln_z", "ln_o"))
        loaded, xn_ready, tp_done, xt_ready = (a.sem(s) for s in ("loaded", "xn_ready", "tp_done", "xt_ready"))
        in_done, xin_ready, gate_ready, conv_done, u_ready = (a.sem(s) for s in ("in_psum", "xin_ready", "gate_ready", "conv_done", "u_ready"))
        bu_done, bu_ready, hs_ready, y_done, yg_ready = (a.sem(s) for s in ("bu_psum", "bu_ready", "hs_ready", "y_psum", "yg_ready"))
        yd_ready, o_done, z_ready = (a.sem(s) for s in ("yd_ready", "o_psum", "z_ready"))
        cch, och = Count(a.sem("conv_chain")), Count(a.sem("out_chain"))
        pads = a.sem("pads")
        loads = [(w_in[:, :], d["w_in"]), (cw[:, :, :], d["conv_w"]), (cb[:, :], d["conv_b"]), (wb[:, :, :], d["w_b"]), (wc[:, :], d["w_c"]),
                 (dp[:, :], d["d_param"]), (wo[:, :, :], d["w_out"]), (gamma[:, :], d["gamma"].broadcast_to([P, P])), (beta[:, :], d["beta"].broadcast_to([P, P]))]
        with nc.Block() as block:
            @block.sync
            def _(sp):
                for dst, src in loads:
                    sp.dma_start(dst, src).then_inc(loaded, 16)

            @block.tensor
            def _(pe):
                for ch in range(NC):
                    pe.wait_ge(xn_ready, 4 * ch + 4)
                    for t in range(4):
                        last = nc.tensor.transpose(psum[:, ch, P * t:P * t + P], xn[:, 4 * ch + t, :], c["ident"][:, :])
                    last.then_inc(tp_done, 1)
                pe.wait_ge(loaded, 16 * len(loads))
                pe.wait_ge(xt_ready, NC)

                def project(ch):
                    if ch >= 1:
                        pe.wait_ge(xin_ready, NB * ch)
                        pe.wait_ge(gate_ready, NB * ch)
                    for b in range(2 * NB):
                        nc.tensor.matmul(psum[:, b, :], w_in[:, P * b:P * b + P], xt[:, W * ch:W * ch + W], start=True, stop=True).then_inc(in_done, 1)

                def inputs(ch):
                    pe.wait_ge(u_ready, NB * (ch + 1))
                    if ch >= 1:
                        pe.wait_ge(bu_ready, ch)
                    for b in range(NB):
                        last = nc.tensor.matmul(psum[0:S, 4, :], wb[:, b, :], u[:, b, W * ch:W * ch + W], start=(b == 0), stop=(b == NB - 1))
                    last.then_inc(bu_done, 1)

                def outputs(ch):
                    pe.wait_ge(hs_ready, ch + 1)
                    if ch >= 1:
                        pe.wait_ge(yd_ready, NB * ch)
                    for b in range(NB):
                        nc.tensor.matmul(psum[:, 5 + b, :], wc[:, P * b:P * b + P], hs[:, W * ch:W * ch + W], start=True, stop=True).then_inc(y_done, 1)

                def out(ch):
                    pe.wait_ge(yg_ready, NB * (ch + 1))
                    if ch >= 1:
                        pe.wait_ge(z_ready, ch)
                    for t in range(4):
                        for b in range(NB):
                            last = nc.tensor.matmul(psum[:, 7, P * t:P * t + P], yg[:, b, W * ch + P * t:W * ch + P * t + P], wo[:, b, :], start=(b == 0), stop=(b == NB - 1))
                    last.then_inc(o_done, 1)

                project(0)
                for ch in range(NC):
                    if ch + 1 < NC:
                        project(ch + 1)
                    inputs(ch)
                    if ch >= 1:
                        out(ch - 1)
                    outputs(ch)
                out(NC - 1)

            @block.scalar
            def _(act):
                ln_x.root(act)
                for ch in range(NC):
                    act.wait_ge(tp_done, ch + 1)
                    nc.scalar.copy(xt[:, W * ch:W * ch + W], psum[:, ch, :]).then_inc(xt_ready, 1)

                def take(ch):
                    for b in range(NB):
                        act.wait_ge(in_done, 2 * NB * ch + b + 1)
                        nc.scalar.copy(xin[:, b, K - 1 + W * ch:K - 1 + W * ch + W], psum[:, b, :]).then_inc(xin_ready, 1)
                    for b in range(NB):
                        act.wait_ge(in_done, 2 * NB * ch + NB + b + 1)
                        nc.scalar.activation(gate[:, b, W * ch:W * ch + W], psum[:, NB + b, :], ACT.Silu).then_inc(gate_ready, 1)

                take(0)
                for ch in range(NC):
                    if ch + 1 < NC:
                        take(ch + 1)
                    for b in range(NB):
                        act.wait_ge(conv_done, NB * ch + b + 1)
                        part = u[:, b, W * ch:W * ch + W]
                        nc.scalar.activation(part, part, ACT.Silu).then_inc(u_ready, 1)
                    act.wait_ge(bu_done, ch + 1)
                    nc.scalar.mul(bu[:, W * ch:W * ch + W], psum[0:S, 4, :], 0.05).then_inc(bu_ready, 1)
                ln_z.root(act)
                ln_o.root(act)

            @block.gpsimd
            def _(g):
                for ch in range(NC):
                    for b in range(NB):
                        g.wait_ge(yd_ready, NB * ch + b + 1)
                        g.wait_ge(gate_ready, NB * ch + b + 1)
                        part = yg[:, b, W * ch:W * ch + W]
                        nc.gpsimd.tensor_tensor(part, part, gate[:, b, W * ch:W * ch + W], ALU.mult).then_inc(yg_ready, 1)

            @block.vector
            def _(dve):
                v = nc.vector
                for t in range(NT):
                    ln_x.tile_stats(t, x[:, t, :])
                v.memset(decay[:, :], 0.95)
                v.memset(xin[:, :, 0:K - 1], 0.0).then_inc(pads, 1)
                dve.wait_ge(pads, 1)
                ln_x.finish(dve)
                for t in range(NT):
                    ln_x.scale(t, xn[:, t, :], x[:, t, :]).then_inc(xn_ready, 1)
                dve.wait_ge(loaded, 16 * len(loads))

                def convolve(ch):
                    dve.wait_ge(xin_ready, NB * (ch + 1))
                    tap_at = [0] * NB
                    for k in range(K - 1, -1, -1):
                        for b in range(NB):
                            tap = xin[:, b, W * ch + k:W * ch + k + W]
                            acc = u[:, b, W * ch:W * ch + W]
                            if k == K - 1:
                                tap_at[b] = cch.up(v.tensor_scalar(acc, tap, cw[:, b, k:k + 1], cb[:, b:b + 1], ALU.mult, ALU.add))
                            else:
                                dve.wait_ge(cch.sem, tap_at[b])
                                ins = v.scalar_tensor_tensor(out=acc, in0=tap, scalar=cw[:, b, k:k + 1], in1=acc, op0=ALU.mult, op1=ALU.add)
                                if k == 0:
                                    ins.then_inc(conv_done, 1)
                                else:
                                    tap_at[b] = cch.up(ins)

                def recur(ch):
                    dve.wait_ge(bu_ready, ch + 1)
                    if ch >= 1:
                        dve.wait_ge(hs_ready, ch)
                    start = hs[:, W * ch - 1:W * ch] if ch else 0.0
                    v.tensor_tensor_scan(hs[:, W * ch:W * ch + W], decay[:, :], bu[:, W * ch:W * ch + W], start, ALU.mult, ALU.add).then_inc(hs_ready, 1)

                def skip(ch):
                    for b in range(NB):
                        dve.wait_ge(y_done, NB * ch + b + 1)
                        v.scalar_tensor_tensor(out=yg[:, b, W * ch:W * ch + W], in0=u[:, b, W * ch:W * ch + W], scalar=dp[:, b:b + 1], in1=psum[:, 5 + b, :],
                                               op0=ALU.mult, op1=ALU.add).then_inc(yd_ready, 1)

                def residual(ch):
                    dve.wait_ge(o_done, ch + 1)
                    v.tensor_tensor(z[:, 4 * ch:4 * ch + 4, :], psum[:, 7, :].rearrange("p (t n) -> p t n", t=4), xn[:, 4 * ch:4 * ch + 4, :], ALU.add).then_inc(z_ready, 1)
                    dve.wait_ge(z_ready, ch + 1)
                    for t in range(4):
                        ln_z.tile_stats(4 * ch + t, z[:, 4 * ch + t, :])

                convolve(0)
                for ch in range(NC):
                    if ch + 1 < NC:
                        convolve(ch + 1)
                    recur(ch)
                    if ch >= 1:
                        residual(ch - 1)
                    skip(ch)
                residual(NC - 1)
                ln_z.finish(dve)
                for t in range(NT):
                    och.up(ln_z.scale(t, z[:, t, :], z[:, t, :]))
                och.settle(dve)
                wide = lambda v_: v_[:, :].unsqueeze(1).broadcast_to([P, NT, P])
                och.up(v.tensor_tensor(z[:, :, :], z[:, :, :], wide(gamma), ALU.mult))
                och.settle(dve)
                och.up(v.tensor_tensor(z[:, :, :], z[:, :, :], wide(beta), ALU.add))
                och.settle(dve)
                for t in range(NT):
                    ln_o.tile_stats(t, z[:, t, :])
                ln_o.finish(dve)
                base = och.n
                for t in range(NT):
                    och.up(ln_o.scale(t, z[:, t, :], z[:, t, :]))
                for t in range(NT):
                    dve.wait_ge(och.sem, base + t + 1)
                    v.tensor_tensor(x[:, t, :], x[:, t, :], z[:, t, :], ALU.add)


def soft_moe(nc, x, c, d, out):
    T, NT, NE, NS = 2048, 16, 64, 32
    W = 512
    SL = NE * NS
    HALF = SL // 2
    HE = NE // 2
    with ExitStack() as ctx:
        a = Alloc(nc, ctx, "mo")
        psum = a.ps("psum", [P, 8, W])
        xt = a.sb("xt", [P, T])
        phi = a.sb("phi", [P, SL])
        bcol = a.sb("bias_col", [P, SL // P])
        part_max = a.sb("part_max", [P, 2, NT, NS])
        xs_t = a.sb("xs_t", [P, SL])
        mp_t = a.sb("neg_max_t", [P, T], BF16)
        yt = a.sb("y_slots", [P, SL // P, P])
        selp = a.sb("sel_slot", [P, P], BF16)
        blk = a.sb("same_slot", [P, P])
        sel_done = a.sem("sel_done")
        sel_n = [0]

        with ExitStack() as ctx0:
            b = Alloc(nc, ctx0, "m0")
            xn = b.sb("xn", [P, NT, P])
            rows = b.sb("bias_rows", [96, SL])
            rhi = b.sb("bias_hi", [96, SL], BF16)
            rmid = b.sb("bias_mid", [96, SL], BF16)
            b3 = b.sb("bias_parts", [96, SL], BF16)
            ones3 = b.sb("ones3", [96, P], BF16)
            xs = b.sb("x_tile", [P, 2, 2, P])
            lc = b.sb("logits", [P, 2, 2, HE, NS])
            ls = b.sb("exps", [P, 2, 2, HE, NS])
            dn = b.sb("dispatch", [P, 2, 2, HE, NS])
            mn = b.sb("max", [P, 2, 2, HE])
            sm = b.sb("sum", [P, 2, 2, HE])
            rs = b.sb("rsum", [P, 2, 2, HE])
            ln = Norm(nc, b, "ln", NT)
            loaded, zeroed, xn_ready, tp_done, xt_ready, b_ready = (b.sem(s) for s in ("loaded", "zeroed", "xn_ready", "tp_done", "xt_ready", "b_ready"))
            stg_t, stg_n, l_done, lc_ready, slot_maxed, maxed, sub_done, exp_done, summed, r_ready, d_ready, x_done = (b.sem(s) for s in (
                "staged_t", "staged", "l_psum", "l_ready", "slot_maxed", "maxed", "sub_done", "exp_done", "summed", "r_ready", "d_ready", "x_psum"))
            xs_ready = b.sem("xs_ready")
            bch = Count(b.sem("bias_chain"))

            def steps(eng, body):
                body(0, 0)
                body(1, 1)
                with eng.Fori(1, NT // 2 - 1) as i:
                    body(2 * i, 0)
                    body(2 * i + 1, 1)
                body(NT - 2, 0)
                body(NT - 1, 1)

            early = lambda z, n: isinstance(z, int) and z < n

            with nc.Block() as block:
                @block.sync
                def _(sp):
                    sp.dma_start(phi[:, :], d["phi"]).then_inc(loaded, 16)
                    sp.dma_start(bcol[:, :], d["phi_b_col"]).then_inc(loaded, 16)
                    sp.wait_ge(zeroed, 1)
                    for k in range(3):
                        sp.dma_start(rows[32 * k:32 * k + 1, :], d["phi_b"]).then_inc(loaded, 16)

                @block.gpsimd
                def _(g):
                    nc.gpsimd.memset(rows[:, :], 0.0).then_inc(zeroed, 1)
                    nc.gpsimd.memset(b3[:, :], 0.0)
                    nc.gpsimd.memset(ones3[:, :], 1.0)
                    ch = Count(sel_done)
                    nc.gpsimd.memset(blk[:, :], 0.0)
                    ch.up(nc.gpsimd.memset(selp[:, :], 0.0))
                    for k in range(3):
                        ch.settle(g)
                        ch.up(nc.gpsimd.affine_select(out=selp[:, :].rearrange("q (n p) -> q n p", n=4), in_=selp[:, :].rearrange("q (n p) -> q n p", n=4),
                                                      compare_op=ALU.not_equal, fill=1.0, base=-NS * k, pattern=[[0, 4], [-1, NS]], channel_multiplier=1))
                    for k in range(-3, 4):
                        ch.settle(g)
                        ch.up(nc.gpsimd.affine_select(out=blk[:, :], in_=blk[:, :], compare_op=ALU.not_equal,
                                                      fill=1.0, base=NS * k, pattern=[[-1, P]], channel_multiplier=1))
                    sel_n[0] = ch.n

                    def subtract(z, par, hf):
                        g.wait_ge(maxed, 2 * z + hf + 1)
                        if not early(z, 2):
                            g.wait_ge(d_ready, 2 * z + hf - 3)
                        nc.gpsimd.tensor_tensor(ls[:, par, hf, :, :], lc[:, par, hf, :, :], mn[:, par, hf, :].unsqueeze(2).broadcast_to([P, HE, NS]), ALU.subtract)\
                            .then_inc(sub_done, 1)

                    def normalise(z, par, hf):
                        g.wait_ge(r_ready, 2 * z + hf + 1)
                        if not early(z, 2):
                            g.wait_ge(x_done, 2 * z + hf - 3)
                        nc.gpsimd.tensor_tensor(dn[:, par, hf, :, :], ls[:, par, hf, :, :], rs[:, par, hf, :].unsqueeze(2).broadcast_to([P, HE, NS]), ALU.mult)\
                            .then_inc(d_ready, 1)

                    def body(z, par):
                        subtract(z, par, 0)
                        if not early(z, 1):
                            normalise(z - 1, 1 - par, 1)
                        subtract(z, par, 1)
                        normalise(z, par, 0)
                    steps(g, body)
                    normalise(NT - 1, 1, 1)

                @block.tensor
                def _(pe):
                    for ch in range(4):
                        pe.wait_ge(xn_ready, 4 * ch + 4)
                        for t in range(4):
                            last = nc.tensor.transpose(psum[:, ch, P * t:P * t + P], xn[:, 4 * ch + t, :], c["ident"][:, :])
                        last.then_inc(tp_done, 1)

                    def logits(z, par, hf):
                        if hf == 0:
                            pe.wait_ge(stg_t, z + 1)
                        if not early(z, 1):
                            pe.wait_ge(lc_ready, 2 * z + hf - 1)
                        for k in range(2):
                            bank = 2 * hf + k
                            nc.tensor.matmul(psum[:, bank, :], ones3[:, :], b3[:, W * bank:W * bank + W], start=True, stop=False)
                            last = nc.tensor.matmul(psum[:, bank, :], xs[:, par, 0, :], phi[:, W * bank:W * bank + W], start=False, stop=True)
                        last.then_inc(l_done, 1)

                    def gather(z, par, hf):
                        if hf == 0:
                            pe.wait_ge(stg_n, z + 1)
                        pe.wait_ge(d_ready, 2 * z + hf + 1)
                        for k in range(2):
                            last = nc.tensor.matmul(psum[:, 4 + 2 * hf + k, :], xs[:, par, 1, :], dn[:, par, hf, :, :].rearrange("p n s -> p (n s)")[:, W * k:W * k + W],
                                                    start=early(z, 1), stop=(isinstance(z, int) and z == NT - 1))
                        last.then_inc(x_done, 1)

                    def body(z, par):
                        final = isinstance(z, int) and z == NT - 1
                        if not final:
                            logits(z + 1, 1 - par, 0)
                        if not early(z, 1):
                            gather(z - 1, 1 - par, 1)
                        if not final:
                            logits(z + 1, 1 - par, 1)
                        gather(z, par, 0)

                    pe.wait_ge(loaded, 16 * 5)
                    pe.wait_ge(b_ready, 1)
                    pe.wait_ge(xt_ready, 4)
                    logits(0, 0, 0)
                    logits(0, 0, 1)
                    steps(pe, body)
                    gather(NT - 1, 1, 1)

                @block.scalar
                def _(act):
                    ln.root(act)
                    for ch in range(4):
                        act.wait_ge(tp_done, ch + 1)
                        nc.scalar.copy(xt[:, W * ch:W * ch + W], psum[:, ch, :]).then_inc(xt_ready, 1)

                    def stage_t(z, par):
                        if not early(z, 2):
                            act.wait_ge(l_done, 2 * z - 2)
                        nc.scalar.copy(xs[:, par, 0, :], xt[:, bass.ds(z * P, P)]).then_inc(stg_t, 1)

                    def stage_n(z, par):
                        if not early(z, 2):
                            act.wait_ge(x_done, 2 * z - 2)
                        nc.scalar.copy(xs[:, par, 1, :].unsqueeze(1), xn[:, bass.ds(z, 1), :]).then_inc(stg_n, 1)

                    def take(z, par, hf):
                        act.wait_ge(l_done, 2 * z + hf + 1)
                        if not early(z, 2):
                            act.wait_ge(sub_done, 2 * z + hf - 3)
                            act.wait_ge(slot_maxed, 2 * z + hf - 3)
                        nc.scalar.copy(lc[:, par, hf, :, :].rearrange("p n s -> p (n s)"), psum[:, 2 * hf:2 * hf + 2, :].rearrange("p b n -> p (b n)")).then_inc(lc_ready, 1)

                    def exps(z, par, hf):
                        act.wait_ge(sub_done, 2 * z + hf + 1)
                        part = ls[:, par, hf, :, :].rearrange("p n s -> p (n s)")
                        nc.scalar.activation(part, part, ACT.Exp).then_inc(exp_done, 1)

                    def body(z, par):
                        final = isinstance(z, int) and z == NT - 1
                        exps(z, par, 0)
                        if not final:
                            take(z + 1, 1 - par, 0)
                        stage_n(z, par)
                        exps(z, par, 1)
                        if not final:
                            take(z + 1, 1 - par, 1)
                            if not (isinstance(z, int) and z == NT - 2):
                                stage_t(z + 2, par)

                    act.wait_ge(xt_ready, 4)
                    act.wait_ge(xn_ready, NT)
                    stage_t(0, 0)
                    stage_t(1, 1)
                    take(0, 0, 0)
                    take(0, 0, 1)
                    steps(act, body)

                @block.vector
                def _(dve):
                    v = nc.vector
                    for t in range(NT):
                        ln.tile_stats(t, x[:, t, :])
                    ln.finish(dve)
                    for t in range(NT):
                        ln.scale(t, xn[:, t, :], x[:, t, :]).then_inc(xn_ready, 1)
                    dve.wait_ge(loaded, 16 * 5)
                    dve.wait_ge(sel_done, sel_n[0])
                    bch.up(v.tensor_copy(rhi[:, :], rows[:, :]))
                    bch.settle(dve)
                    v.tensor_copy(b3[0:1, :], rhi[0:1, :])
                    bch.up(v.tensor_tensor(rows[:, :], rows[:, :], rhi[:, :], ALU.subtract))
                    bch.settle(dve)
                    bch.up(v.tensor_copy(rmid[:, :], rows[:, :]))
                    bch.settle(dve)
                    v.tensor_copy(b3[32:33, :], rmid[32:33, :])
                    v.tensor_tensor(b3[64:65, :], rows[64:65, :], rmid[64:65, :], ALU.subtract).then_inc(b_ready, 1)

                    def reduce(z, par, hf):
                        dve.wait_ge(lc_ready, 2 * z + hf + 1)
                        if not early(z, 2):
                            dve.wait_ge(sub_done, 2 * z + hf - 3)
                        v.tensor_reduce(mn[:, par, hf, :], lc[:, par, hf, :, :], AX_X, ALU.max).then_inc(maxed, 1)
                        v.tensor_reduce(part_max[:, hf, bass.ds(z, 1), :].rearrange("p o s -> p (o s)"), lc[:, par, hf, :, :].rearrange("p n s -> p s n"), AX_X, ALU.max)\
                            .then_inc(slot_maxed, 1)

                    def sums(z, par, hf):
                        dve.wait_ge(exp_done, 2 * z + hf + 1)
                        v.tensor_reduce(sm[:, par, hf, :], ls[:, par, hf, :, :], AX_X, ALU.add).then_inc(summed, 1)
                        dve.wait_ge(summed, 2 * z + hf + 1)
                        if not early(z, 2):
                            dve.wait_ge(d_ready, 2 * z + hf - 3)
                        v.reciprocal(rs[:, par, hf, :], sm[:, par, hf, :]).then_inc(r_ready, 1)

                    def body(z, par):
                        reduce(z, par, 0)
                        if not early(z, 1):
                            sums(z - 1, 1 - par, 1)
                        reduce(z, par, 1)
                        sums(z, par, 0)
                    steps(dve, body)
                    sums(NT - 1, 1, 1)
                    dve.wait_ge(x_done, 2 * NT)
                    for k in range(4):
                        v.tensor_scalar(xs_t[:, W * k:W * k + W], psum[:, 4 + k, :], -33000.0, 65000.0, ALU.max, ALU.min).then_inc(xs_ready, 1)

        with ExitStack() as ctx1:
            b = Alloc(nc, ctx1, "m1")
            ew = b.sb("expert_w", [P, NE, P])
            eb = b.sb("expert_b", [P, SL // P, P])
            nm3 = b.sb("neg_max_parts", [P, NT, P], BF16)
            nmax = b.sb("neg_max", [P, NT, NS])
            xh = b.sb("x_hat", [P, NT, P])
            xh_t = b.sb("x_hat_t", [P, SL])
            ln = Norm(nc, b, "ln", NT)
            ch = Count(b.sem("chain"))
            loaded, nat_done, xh_ready, tanh_done, back_done, back_ready, yt_done, yt_ready, nm_ready, mp_done, mp_ready = (b.sem(s) for s in (
                "loaded", "nat_psum", "xh_ready", "tanh_done", "back_psum", "back_ready", "yt_psum", "yt_ready", "nm_ready", "mp_psum", "mp_ready"))
            with nc.Block() as block:
                @block.sync
                def _(sp):
                    sp.dma_start(ew[:, :, :], d["expert_w"]).then_inc(loaded, 16)
                    for k in range(4):
                        sp.dma_start(eb[32 * k:32 * k + 32, :, :], d["expert_b"].rearrange("(j n) h -> n j h", n=4)[k:k + 1].broadcast_to([32, SL // P, P]))\
                            .then_inc(loaded, 16)

                @block.tensor
                def _(pe):
                    for t in range(NT):
                        last = nc.tensor.transpose(psum[:, t // 4, P * (t % 4):P * (t % 4) + P], xs_t[:, P * t:P * t + P], c["ident"][:, :])
                        if t % 4 == 3:
                            last.then_inc(nat_done, 1)
                    pe.wait_ge(nm_ready, 1)
                    for q in range(4):
                        bank = psum[:, 4 + q, 0:256].bitcast(BF16)
                        for t in range(4):
                            last = nc.tensor.transpose(bank[:, P * t:P * t + P], nm3[:, 4 * q + t, :], c["identb"][:, :])
                        last.then_inc(mp_done, 1)
                    pe.wait_ge(xh_ready, NT)
                    for q in range(4):
                        pe.wait_ge(tanh_done, 4 * q + 4)
                        for t in range(4 * q, 4 * q + 4):
                            last = nc.tensor.transpose(psum[:, q, P * (t % 4):P * (t % 4) + P], xh[:, t, :], c["ident"][:, :])
                        last.then_inc(back_done, 1)
                    pe.wait_ge(loaded, 80)
                    pe.wait_ge(mp_ready, 4)
                    for q in range(4):
                        pe.wait_ge(back_ready, q + 1)
                        for j in range(4):
                            for k in range(4):
                                n = 16 * q + 4 * j + k
                                last = nc.tensor.matmul(psum[32 * k:32 * k + 32, 4 + q, P * j:P * j + P], xh_t[:, NS * n:NS * n + NS], ew[:, n, :], start=True, stop=True)
                        last.then_inc(yt_done, 1)

                @block.scalar
                def _(act):
                    ln.root(act)
                    for q in range(4):
                        act.wait_ge(mp_done, q + 1)
                        nc.scalar.copy(mp_t[:, W * q:W * q + W], psum[:, 4 + q, 0:256].bitcast(BF16)).then_inc(mp_ready, 1)
                    for t in range(NT):
                        act.wait_ge(xh_ready, t + 1)
                        nc.scalar.activation(xh[:, t, :], xh[:, t, :], ACT.Tanh).then_inc(tanh_done, 1)
                    for q in range(4):
                        act.wait_ge(back_done, q + 1)
                        nc.scalar.copy(xh_t[:, W * q:W * q + W], psum[:, q, :]).then_inc(back_ready, 1)

                @block.vector
                def _(dve):
                    v = nc.vector
                    v.memset(nm3[:, :, 3 * NS:P], 0.0)
                    ch.up(v.tensor_tensor(nmax[:, :, :], part_max[:, 0, :, :], part_max[:, 1, :, :], ALU.max))
                    ch.settle(dve)
                    ch.up(v.tensor_scalar(nmax[:, :, :], nmax[:, :, :], -1.0, None, ALU.mult))
                    for k in range(2):
                        ch.settle(dve)
                        ch.up(v.tensor_copy(nm3[:, :, NS * k:NS * k + NS], nmax[:, :, :]))
                        ch.settle(dve)
                        ch.up(v.tensor_tensor(nmax[:, :, :], nmax[:, :, :], nm3[:, :, NS * k:NS * k + NS], ALU.subtract))
                    ch.settle(dve)
                    v.tensor_copy(nm3[:, :, 2 * NS:3 * NS], nmax[:, :, :]).then_inc(nm_ready, 1)
                    tile = lambda t: psum[:, t // 4, P * (t % 4):P * (t % 4) + P]
                    for t in range(NT):
                        if t % 4 == 0:
                            dve.wait_ge(nat_done, t // 4 + 1)
                        ln.tile_stats(t, tile(t))
                    ln.finish(dve)
                    for t in range(NT):
                        ln.scale(t, xh[:, t, :], tile(t)).then_inc(xh_ready, 1)
                    dve.wait_ge(loaded, 80)
                    for q in range(4):
                        dve.wait_ge(yt_done, q + 1)
                        v.tensor_tensor(yt[:, 4 * q:4 * q + 4, :], psum[:, 4 + q, :].rearrange("p (j h) -> p j h", j=4), eb[:, 4 * q:4 * q + 4, :], ALU.add)\
                            .then_inc(yt_ready, 1)

        with ExitStack() as ctx2:
            b = Alloc(nc, ctx2, "m2")
            NJ = SL // P
            ec = b.sb("exp", [P, 2, NJ, W])
            tot = b.sb("total", [P, 2, W])
            rt = b.sb("rtotal", [P, 2, W])
            y_t = b.sb("y_t", [P, T])
            y = b.sb("y", [P, NT, P])
            ln = Norm(nc, b, "ln", NT)
            l_done, exp_done, added, tot_done, rt_ready, scaled, y_done, yt_ready, nat_done, o_ready, stored = (b.sem(s) for s in (
                "l_psum", "exp_done", "added", "tot_psum", "rt_ready", "scaled", "y_psum", "yt_ready", "nat_psum", "o_ready", "stored"))
            ych = Count(b.sem("y_chain"))
            NCH = T // W
            with nc.Block() as block:
                @block.tensor
                def _(pe):
                    def logits(ch, j):
                        n = NJ * ch + j
                        if n >= 4:
                            pe.wait_ge(exp_done, n - 3)
                        cols = slice(W * ch, W * ch + W)
                        nc.tensor.matmul(psum[:, n % 4, :], selp[:, :], mp_t[:, cols], start=True, stop=False)
                        nc.tensor.matmul(psum[:, n % 4, :], phi[:, P * j:P * j + P], xt[:, cols], start=False, stop=True).then_inc(l_done, 1)

                    def total(ch):
                        pe.wait_ge(added, (NJ - 1) * (ch + 1))
                        if ch >= 1:
                            pe.wait_ge(rt_ready, ch)
                        nc.tensor.matmul(psum[:, 4, :], blk[:, :], tot[:, ch % 2, :], start=True, stop=True).then_inc(tot_done, 1)

                    def combine(ch, j):
                        if ch >= 2 and j == 0:
                            pe.wait_ge(yt_ready, ch - 1)
                        pe.wait_ge(scaled, NJ * ch + j + 1)
                        ins = nc.tensor.matmul(psum[:, 5 + ch % 2, :], yt[:, j, :], ec[:, ch % 2, j, :], start=(j == 0), stop=(j == NJ - 1))
                        ins.then_inc(y_done, 1)

                    AHEAD = 4
                    for j in range(NJ):
                        logits(0, j)
                    for ch in range(NCH):
                        if ch + 1 < NCH:
                            for j in range(AHEAD):
                                logits(ch + 1, j)
                                if j == 0:
                                    total(ch)
                        else:
                            total(ch)
                        for j in range(NJ):
                            if ch + 1 < NCH and j + AHEAD < NJ:
                                logits(ch + 1, j + AHEAD)
                            combine(ch, j)
                    pe.wait_ge(yt_ready, NCH)
                    for t in range(NT):
                        last = nc.tensor.transpose(psum[:, t // 4, P * (t % 4):P * (t % 4) + P], y_t[:, P * t:P * t + P], c["ident"][:, :])
                        if t % 4 == 3:
                            last.then_inc(nat_done, 1)

                @block.scalar
                def _(act):
                    for ch in range(NCH):
                        for j in range(NJ):
                            n = NJ * ch + j
                            act.wait_ge(l_done, n + 1)
                            if ch >= 2:
                                act.wait_ge(y_done, n - 2 * NJ + 1)
                                act.wait_ge(added, (NJ - 1) * (ch - 1))
                            nc.scalar.activation(ec[:, ch % 2, j, :], psum[:, n % 4, :], ACT.Exp, bias=bcol[:, j:j + 1], scale=1.0).then_inc(exp_done, 1)
                        if ch >= 1:
                            act.wait_ge(y_done, NJ * ch)
                            nc.scalar.copy(y_t[:, W * (ch - 1):W * ch], psum[:, 5 + (ch - 1) % 2, :]).then_inc(yt_ready, 1)
                    act.wait_ge(y_done, NJ * NCH)
                    nc.scalar.copy(y_t[:, W * (NCH - 1):W * NCH], psum[:, 5 + (NCH - 1) % 2, :]).then_inc(yt_ready, 1)
                    ln.root(act)

                @block.vector
                def _(dve):
                    v = nc.vector

                    def add(ch, j):
                        dve.wait_ge(exp_done, NJ * ch + j + 1)
                        if j == 0:
                            return
                        if j == 1:
                            if ch >= 2:
                                dve.wait_ge(tot_done, ch - 1)
                            in0 = ec[:, ch % 2, 0, :]
                        else:
                            dve.wait_ge(added, (NJ - 1) * ch + j - 1)
                            in0 = tot[:, ch % 2, :]
                        v.tensor_tensor(tot[:, ch % 2, :], in0, ec[:, ch % 2, j, :], ALU.add).then_inc(added, 1)

                    for j in range(NJ):
                        add(0, j)
                    for ch in range(NCH):
                        dve.wait_ge(tot_done, ch + 1)
                        if ch >= 2:
                            dve.wait_ge(scaled, NJ * (ch - 1))
                        v.reciprocal(rt[:, ch % 2, :], psum[:, 4, :]).then_inc(rt_ready, 1)
                        dve.wait_ge(rt_ready, ch + 1)
                        for j in range(NJ):
                            v.tensor_tensor(ec[:, ch % 2, j, :], ec[:, ch % 2, j, :], rt[:, ch % 2, :], ALU.mult).then_inc(scaled, 1)
                            if ch + 1 < NCH:
                                add(ch + 1, j)
                    tile = lambda t: psum[:, t // 4, P * (t % 4):P * (t % 4) + P]
                    for t in range(NT):
                        if t % 4 == 0:
                            dve.wait_ge(nat_done, t // 4 + 1)
                        ln.tile_stats(t, tile(t))
                    ln.finish(dve)
                    for t in range(NT):
                        ych.up(ln.scale(t, y[:, t, :], tile(t)))
                    for t in range(NT):
                        dve.wait_ge(ych.sem, t + 1)
                        v.tensor_tensor(x[:, t, :], x[:, t, :], y[:, t, :], ALU.add).then_inc(o_ready, 1)

                @block.sync
                def _(sp):
                    for q in range(4):
                        sp.wait_ge(o_ready, 4 * q + 4)
                        sp.dma_start(out.rearrange("(t p) c -> p t c", p=P)[:, 4 * q:4 * q + 4, :], x[:, 4 * q:4 * q + 4, :]).then_inc(stored, 16)
                    sp.wait_ge(stored, 64)


def sandwich(nc, args, out):
    with ExitStack() as ctx:
        a = Alloc(nc, ctx, "all")
        x = a.sb("x", [P, 16, P])
        consts = dict(ident=a.sb("ident", [P, P]), identb=a.sb("ident_bf16", [P, P], BF16))
        with ExitStack() as ctx0:
            b = Alloc(nc, ctx0, "band")
            consts["mask"] = b.sb("mask", [P, 2, 256], BF16)
            consts["sel"] = b.sb("select", [P, 16, P], BF16)
            attention(nc, x, consts, args)
        kmoe(nc, x, consts, args)
        ssm(nc, x, consts, args)
        soft_moe(nc, x, consts, args, out)


def kernel(**inputs):
    import numpy as np
    from concourse import bacc
    from concourse.bass_utils import run_bass_kernel_spmd

    first = {name[len("L0_attn_"):]: np.asarray(v) for name, v in inputs.items() if name.startswith("L0_attn_")}
    moe = {name[len("L0_ffn_"):]: np.asarray(v) for name, v in inputs.items() if name.startswith("L0_ffn_")}
    mix = {name[len("L1_attn_"):]: np.asarray(v) for name, v in inputs.items() if name.startswith("L1_attn_")}
    soft = {name[len("L1_ffn_"):]: np.asarray(v) for name, v in inputs.items() if name.startswith("L1_ffn_")}
    laid = {
        "x": first["x"].reshape(2048, 128),
        "ident": np.eye(128, dtype=np.float32),
        "wqkv": first["Wqkv"], "bqkv": first["bqkv"], "wout": first["Wout"], "bout": first["bout"],
        "expert_ids": np.arange(64, dtype=np.float32).reshape(1, 64),
        "w_up": moe["W_up"].reshape(64, 8, 128).transpose(2, 1, 0),
        "b_up": moe["B_up"],
        "a_up": moe["A_up"],
        "w_down": moe["W_down"].reshape(64, 64, 64).transpose(2, 1, 0),
        "b_down": moe["B_down"],
        "a_down": moe["A_down"],
        "bias_up": moe["bias_up"].reshape(64, 64).T,
        "bias_down": moe["bias_down"].reshape(32, 32).T,
        "scale_up": moe["scale_up"].reshape(1, 1),
        "scale_down": moe["scale_down"].reshape(1, 1),
        "w_in": mix["W_in"].T,
        "conv_w": mix["conv_w"].reshape(2, 128, 4).transpose(1, 0, 2),
        "conv_b": mix["conv_b"].reshape(2, 128).T,
        "w_b": mix["W_B"].reshape(64, 2, 128).transpose(2, 1, 0),
        "w_c": mix["W_C"].T,
        "d_param": mix["D_param"].reshape(2, 128).T,
        "w_out": mix["W_out"].reshape(128, 2, 128).transpose(2, 1, 0),
        "gamma": mix["ln_gamma"].reshape(1, 128),
        "beta": mix["ln_beta"].reshape(1, 128),
        "phi": soft["phi_w"].T,
        "phi_b": soft["phi_b"].reshape(1, 2048),
        "phi_b_col": soft["phi_b"].reshape(16, 128).T,
        "expert_w": soft["expert_w"].transpose(1, 0, 2),
        "expert_b": soft["expert_b"],
    }
    nc = bacc.Bacc("TRN2", target_bir_lowering=False, num_devices=1)
    arrays, args = {}, {}
    for name, v in laid.items():
        arrays["in_" + name] = np.ascontiguousarray(v)
        args[name] = nc.dram_tensor("in_" + name, v.shape, F32, kind="ExternalInput").ap()
    out = nc.dram_tensor("out_rows", [2048, 128], F32, kind="ExternalOutput").ap()
    sandwich(nc, args, out)
    result = run_bass_kernel_spmd(nc, [arrays], core_ids=[0])
    return result.results[0]["out_rows"].reshape(1, 2048, 128)
```

```python
from contextlib import ExitStack

import numpy as np

import concourse.bass as bass
from concourse import mybir

F32 = mybir.dt.float32
BF16 = mybir.dt.bfloat16
I32 = mybir.dt.int32
U32 = mybir.dt.uint32
ALU = mybir.AluOpType
ACT = mybir.ActivationFunctionType
AX_X = mybir.AxisListType.X

P = 128
NEG = -1.0e30
EPS = 1e-5


class Count:

    def __init__(self, sem):
        self.sem, self.n = sem, 0

    def up(self, ins):
        ins.then_inc(self.sem, 1)
        self.n += 1
        return self.n

    def settle(self, eng):
        eng.wait_ge(self.sem, self.n)


class Alloc:

    def __init__(self, nc, ctx, tag, cleared=None):
        self.nc, self.ctx, self.tag, self.cleared = nc, ctx, tag, cleared

    def sb(self, name, shape, dt=F32):
        return self.ctx.enter_context(self.nc.sbuf_tensor(f"{self.tag}_{name}", shape, dt))

    def ps(self, name, shape, dt=F32):
        return self.ctx.enter_context(self.nc.psum_tensor(f"{self.tag}_{name}", shape, dt))

    def sem(self, name):
        if self.cleared is not None:
            self.cleared.append(self.nc.alloc_semaphore(name=f"{self.tag}_{name}"))
            return self.cleared[-1]
        return self.ctx.enter_context(self.nc.semaphore(f"{self.tag}_{name}"))


class Norm:

    def __init__(self, nc, a, name, nt, in_psum=False):
        self.nc, self.nt = nc, nt
        self.dve_tiles = range(0, nt // 2) if in_psum else range(0, nt, 2)
        self.act_tiles = range(nt // 2, nt) if in_psum else range(1, nt, 2)
        self.stats = a.sb(f"{name}_stats", [P, nt, 6])
        self.tmp = a.sb(f"{name}_tmp", [P, 8, nt])
        self.chain = Count(a.sem(f"{name}_chain"))
        self.var_ready = a.sem(f"{name}_var")
        self.std_ready = a.sem(f"{name}_std")
        self.factors = a.sem(f"{name}_factors")
        self.by_dve = a.sem(f"{name}_by_dve")
        self.by_act = a.sem(f"{name}_by_act")

    def tile_stats(self, t, src):
        self.chain.up(self.nc.vector.bn_stats(self.stats[:, t, :], src))

    def finish(self, dve, t0=0, t1=None, mark=0):
        t1 = self.nt if t1 is None else t1
        v, tmp, st = self.nc.vector, self.tmp, self.stats
        col = lambda k: tmp[:, k, t0:t1]
        self.chain.settle(dve)
        me, mo, se, so = (st[:, t0:t1, k] for k in (1, 4, 2, 5))
        v.tensor_tensor(col(0), me, mo, ALU.add)
        v.tensor_tensor(col(1), me, mo, ALU.subtract)
        self.chain.up(v.tensor_tensor(col(3), se, so, ALU.add))
        self.chain.settle(dve)
        v.tensor_scalar(col(2), col(0), 0.5, None, ALU.mult)
        self.chain.up(v.scalar_tensor_tensor(out=col(4), in0=col(1), scalar=0.25, in1=col(1), op0=ALU.mult, op1=ALU.mult))
        self.chain.up(v.tensor_scalar(col(3), col(3), 1.0 / P, EPS, ALU.mult, ALU.add))
        self.chain.settle(dve)
        v.tensor_tensor(col(5), col(3), col(4), ALU.add).then_inc(self.var_ready, 1)
        dve.wait_ge(self.std_ready, mark + 1)
        self.chain.up(v.reciprocal(col(6), col(7)))
        self.chain.settle(dve)
        v.scalar_tensor_tensor(out=col(1), in0=col(2), scalar=-1.0, in1=col(6), op0=ALU.mult, op1=ALU.mult).then_inc(self.factors, 1)

    def root(self, act, t0=0, t1=None, mark=0):
        t1 = self.nt if t1 is None else t1
        act.wait_ge(self.var_ready, mark + 1)
        self.nc.scalar.activation(self.tmp[:, 7, t0:t1], self.tmp[:, 5, t0:t1], ACT.Sqrt).then_inc(self.std_ready, 1)

    def scale(self, t, dst, src):
        return self.nc.vector.tensor_scalar(dst, src, self.tmp[:, 2, t:t + 1], self.tmp[:, 6, t:t + 1],
                                            ALU.subtract, ALU.mult)


def scale_on_dve(ln, dst, src):
    for t in ln.dve_tiles:
        ln.scale(t, dst(t), src(t)).then_inc(ln.by_dve, 1)


def scale_on_act(act, ln, dst, src):
    act.wait_ge(ln.factors, 1)
    for t in ln.act_tiles:
        ln.nc.scalar.activation(dst(t), src(t), ACT.Identity, bias=ln.tmp[:, 1, t:t + 1], scale=ln.tmp[:, 6, t:t + 1]).then_inc(ln.by_act, 1)


def tiles_scaled(eng, ln, n):
    eng.wait_ge(ln.by_dve, n // 2)
    eng.wait_ge(ln.by_act, n // 2)


def add_dve_tiles(dve, ln, x, y, done=None):
    for n, t in enumerate(ln.dve_tiles):
        dve.wait_ge(ln.by_dve, n + 1)
        ins = ln.nc.vector.tensor_tensor(x[:, t, :], x[:, t, :], y(t), ALU.add)
        if done is not None:
            ins.then_inc(done, 1)


def add_act_tiles(pool, ln, x, y, done=None):
    for n, t in enumerate(ln.act_tiles):
        pool.wait_ge(ln.by_act, n + 1)
        ins = ln.nc.gpsimd.tensor_tensor(x[:, t, :], x[:, t, :], y(t), ALU.add)
        if done is not None:
            ins.then_inc(done, 1)


def attention(nc, x, c, d):
    H, DH, T = 16, 8, 2048
    NT = T // P
    NG, GH = 4, 4
    NP = H // 2
    NS = NT + 1
    TERMS_Q, TERMS_K = "hhmmhl", "hmhmlh"
    scale = DH ** -0.5

    with ExitStack() as ctx:
        used = []
        a = Alloc(nc, ctx, "at", used)
        qs = a.sb("q_stack", [P, NP, NS * P], BF16)
        ks = a.sb("k_stack", [P, NP, (NT + 2) * P], BF16)
        v9 = a.sb("v_and_one", [P, NT + 2, H, DH + 1])
        a_t = a.sb("attn_t", [P, NS * P])
        wout = a.sb("wout", [P, P])
        bout = a.sb("bout", [P, P])
        ln_y = Norm(nc, a, "ln_y", NT)
        psum = a.ps("psum", [P, 8, 512])

        with ExitStack() as ctx0:
            b = Alloc(nc, ctx0, "pr", used)
            xn = b.sb("xn", [P, NT, P])
            xt = b.sb("xt", [P, T])
            wqkv = b.sb("wqkv", [P, 3 * P])
            bqk = b.sb("bqk", [P, 2])
            bq_s = b.sb("bq_scaled", [P, 1])
            bv = b.sb("bv", [P, P])
            full = b.sb("full", [P, 2, 2, 512])
            rest = b.sb("rest", [P, 2, 512])
            part = {k: b.sb(f"part_{k}", [P, 2, T], BF16) for k in "hml"}
            flags = b.sb("flags", [16, NP * P], BF16)
            ln = Norm(nc, b, "ln_x", NT)
            loaded = b.sem("loaded")
            x_loaded = b.sem("x_loaded")
            filled, v9_filled = b.sem("filled"), b.sem("v9_filled")
            tp_done = b.sem("tp_done")
            xt_ready = b.sem("xt_ready")
            proj_done = b.sem("proj_done")
            full_ready = b.sem("full_ready")
            hi_ready = b.sem("hi_ready")
            split_done = b.sem("split_done")
            v_ready = b.sem("v_ready")
            bq_ready = b.sem("bq_ready")
            dch = Count(b.sem("dve_chain"))
            NL = 6
            scratch = nc.dram_tensor("parts_scratch", [3, 2, P, T], BF16).ap()
            kw = b.sb("k_window", [P, 2, NP, 2 * P], BF16)
            qw = b.sb("q_window", [P, 2, NP, P], BF16)
            negm = b.sb("neg_max", [P, H])
            nrest = b.sb("neg_max_rest", [P, H])
            nm3 = b.sb("neg_max_parts", [P, P], BF16)
            m_t = b.sb("neg_max_t", [P, 2, P], BF16)
            e = b.sb("exp", [P, 4, GH, 2, P])
            rec = b.sb("rec", [P, H])
            attn = b.sb("attn", [P, H, DH])
            vw = b.sb("v_window", [P, 2, 2, H, 32])
            o_sb = b.sb("values_t", [P, NG, P])
            y = xn
            win, n_done, max_done, nm_ready, mtp, mt = (b.sem(s) for s in ("window", "nat_done", "max_done", "nm_ready", "mt_psum", "mt_ready"))
            t_done, exp_done, sel_done, pv_done = (b.sem(s) for s in ("t_done", "exp_done", "sel_done", "pv_done"))
            vwin, otp, o_done = (b.sem(s) for s in ("v_window", "values_psum", "values_sbuf"))
            norm_done, atp, at_done = (b.sem(s) for s in ("norm_done", "at_psum", "at_done"))
            proj, y_ready = b.sem("proj"), b.sem("y_ready")
            wch = b.sem("window_chain")
            rch = b.sem("rec_chain")
            cleared = b.sem("cleared")
            sel_begun = b.sem("sel_begun")
            SN, ST, PV, MISC = 0, 4, 6, 7
            misc_bf = psum[:, MISC, 0:64].bitcast(BF16)

            def steps(eng, body):
                body(0, 0)
                with eng.Fori(0, (NS - 3) // 2) as i:
                    body(2 * i + 1, 1)
                    body(2 * i + 2, 0)
                body(NS - 2, 1)
                body(NS - 1, 0)

            ROWS = ((0, 512), (512, 1024), (1024, T))
            TILES = (4, 4, NS - 8)
            stacked = [b.sem(f"stacked_{k}") for k in range(3)]
            bounced = [b.sem(f"bounced_{k}") for k in range(3)]
            tiles_ready, consts_ready = b.sem("tiles_ready"), b.sem("consts_ready")
            n_consts = [0]
            ONE_ONE = float(np.array([0x3F803F80], dtype=np.uint32).view(np.float32)[0])

            def tiles_in(sp, ch):
                sp.wait_ge(stacked[ch], 16 * (24 + (4 if ch == 0 else 0)))
                sp.sem_inc(tiles_ready, TILES[ch])

            with nc.Block() as block:
                @block.sync
                def _(sp):
                    sp.dma_start(x[:, :, :], d["x"].rearrange("(t p) c -> p t c", p=P)).then_inc(x_loaded, 16)
                    sp.dma_start(wqkv[:, :], d["wqkv"]).then_inc(loaded, 16)
                    sp.dma_start(bqk[:, :], d["bqkv"][0:2 * P].rearrange("(k p) -> p k", p=P), allow_slow_non_contiguous=True).then_inc(loaded, 16)
                    sp.dma_start(bv[:, :], d["bqkv"][2 * P:].rearrange("(a n) -> a n", a=1).broadcast_to([P, P])).then_inc(loaded, 16)
                    sp.dma_start(wout[:, :], d["wout"]).then_inc(loaded, 16)
                    sp.dma_start(bout[:, :], d["bout"].rearrange("(a n) -> a n", a=1).broadcast_to([P, P])).then_inc(loaded, 16)
                    sp.dma_start(c["ident"][:, :], d["ident"]).then_inc(loaded, 16)
                    sp.wait_ge(filled, 2)
                    for half in range(2):
                        for edge in (0, NT + 1):
                            sp.dma_start(ks[64 * half + 48:64 * half + 64, :, edge * P:(edge + 1) * P],
                                         flags[:, :].rearrange("r (j n) -> r j n", j=NP)).then_inc(stacked[0], 16)
                    for ch, (r0, r1) in enumerate(ROWS):
                        sp.wait_ge(split_done, 2 * r1 // 512)
                        for k, kept in part.items():
                            sp.dma_start(scratch["hml".index(k), :, :, r0:r1].rearrange("w p n -> p w n"), kept[:, :, r0:r1]).then_inc(bounced[ch], 16)
                        if ch >= 1:
                            tiles_in(sp, ch - 1)
                        sp.wait_ge(bounced[ch], 48)
                        for which, (stack, terms, pad) in enumerate(((qs, TERMS_Q, 64), (ks, TERMS_K, P))):
                            for n, k in enumerate(terms):
                                rows = scratch["hml".index(k), which].rearrange("(j h r) n -> h r j n", j=NP, h=2)
                                for half in range(2):
                                    p0 = 64 * half + 8 * n
                                    sp.dma_start(stack[p0:p0 + 8, :, pad + r0:pad + r1], rows[half][:, :, r0:r1]).then_inc(stacked[ch], 16)
                    tiles_in(sp, len(ROWS) - 1)

                @block.gpsimd
                def _(pool):
                    nc.gpsimd.memset(flags[:, :], NEG)
                    nc.gpsimd.memset(ks[:, :, :].rearrange("p j n -> p (j n)").bitcast(F32), 0.0)
                    nc.gpsimd.memset(qs[:, :, :].rearrange("p j n -> p (j n)").bitcast(F32), ONE_ONE).then_inc(filled, 2)
                    ch = Count(consts_ready)
                    nc.gpsimd.memset(c["identb"][:, :], 0.0)
                    nc.gpsimd.memset(c["mask"][:, :, :], 0.0)
                    ch.up(nc.gpsimd.memset(c["sel"][:, :, :], 0.0))
                    ch.settle(pool)
                    ch.up(nc.gpsimd.affine_select(out=c["identb"][:, :], in_=c["identb"][:, :], compare_op=ALU.not_equal,
                                                  fill=1.0, base=0, pattern=[[-1, P]], channel_multiplier=1))
                    ch.up(nc.gpsimd.affine_select(out=c["mask"][:, :, :], in_=c["mask"][:, :, :], compare_op=ALU.is_ge,
                                                  fill=NEG, base=0, pattern=[[0, 2], [1, 256]], channel_multiplier=-1))
                    ch.settle(pool)
                    ch.up(nc.gpsimd.affine_select(out=c["mask"][:, :, :], in_=c["mask"][:, :, :], compare_op=ALU.is_ge,
                                                  fill=NEG, base=P, pattern=[[0, 2], [-1, 256]], channel_multiplier=1))
                    for k in range(3):
                        ch.settle(pool)
                        ch.up(nc.gpsimd.affine_select(out=c["sel"][:, :, :], in_=c["sel"][:, :, :], compare_op=ALU.not_equal,
                                                      fill=1.0, base=-H * k, pattern=[[-1, H], [0, P]], channel_multiplier=1))
                    n_consts[0] = ch.n

                    def body(s, sp):
                        for g in range(NG):
                            pool.wait_ge(exp_done, 4 * s + g + 1)
                            pool.sem_inc(sel_begun, 1)
                            nc.gpsimd.affine_select(out=e[:, g, :, 0, :], in_=e[:, g, :, 0, :], compare_op=ALU.is_ge,
                                                    fill=0.0, base=0, pattern=[[0, GH], [-1, P]], channel_multiplier=1)
                            nc.gpsimd.affine_select(out=e[:, g, :, 1, :], in_=e[:, g, :, 1, :], compare_op=ALU.is_ge,
                                                    fill=0.0, base=0, pattern=[[0, GH], [1, P]], channel_multiplier=-1).then_inc(sel_done, 1)
                    steps(pool, body)
                    add_act_tiles(pool, ln_y, x, lambda t: y[:, t, :])

                @block.vector
                def _(dve):
                    nc.vector.memset(v9[:, :, :, :], 1.0).then_inc(v9_filled, 1)
                    nc.vector.memset(vw[:, :, :, :, :], 0.0)
                    nc.vector.memset(nm3[:, :], 0.0).then_inc(cleared, 1)
                    dve.wait_ge(x_loaded, 16)
                    for t in range(NT):
                        ln.tile_stats(t, x[:, t, :])
                    ln.finish(dve)
                    scale_on_dve(ln, lambda t: xn[:, t, :], lambda t: x[:, t, :])
                    dve.wait_ge(loaded, 16 * NL)
                    nc.vector.tensor_scalar(bq_s[:, :], bqk[:, 0:1], scale, None, ALU.mult).then_inc(bq_ready, 1)
                    dve.wait_ge(v9_filled, 1)
                    for ch in range(4):
                        cols = slice(512 * ch, 512 * ch + 512)
                        dve.wait_ge(proj_done, ch + 1)
                        nc.vector.tensor_tensor(v9[:, 1 + 4 * ch:5 + 4 * ch, :, 0:DH],
                                                psum[:, 4 + ch % 2, :].rearrange("p (t h d) -> p t h d", t=4, h=H),
                                                bv[:, :].rearrange("p (h d) -> p h d", h=H).unsqueeze(1).broadcast_to([P, 4, H, DH]),
                                                ALU.add).then_inc(v_ready, 1)
                        for w in range(2):
                            dve.wait_ge(hi_ready, 2 * ch + w + 1)
                            if ch >= 1:
                                dve.wait_ge(split_done, 2 * ch + w - 1)
                            dch.up(nc.vector.tensor_tensor(rest[:, w, :], full[:, ch % 2, w, :], part["h"][:, w, cols], ALU.subtract))
                            dch.settle(dve)
                            dch.up(nc.vector.tensor_copy(part["m"][:, w, cols], rest[:, w, :]))
                            dch.settle(dve)
                            nc.vector.tensor_tensor(part["l"][:, w, cols], rest[:, w, :], part["m"][:, w, cols],
                                                    ALU.subtract).then_inc(split_done, 1)

                    def window(w, wp):
                        dve.wait_ge(tiles_ready, w + 1)
                        nc.vector.tensor_copy(kw[:, wp, :, :], ks[:, :, bass.ds(w * P, 2 * P)])
                        nc.vector.tensor_copy(qw[:, wp, :, :], qs[:, :, bass.ds(w * P, P)]).then_inc(win, 1)

                    def window_v(w, wp):
                        nc.vector.tensor_copy(vw[:, wp, :, :, 0:DH + 1], v9[:, bass.ds(w, 2), :, :]).then_inc(vwin, 1)

                    def maxima(w, g):
                        dve.wait_ge(n_done, 4 * w + g + 1)
                        nc.vector.tensor_reduce(negm[:, GH * g:GH * g + GH].rearrange("p (u r) -> p r u", r=2),
                                                psum[:, SN + 2 * (g % 2):SN + 2 * (g % 2) + 2, :].rearrange("p r (u k) -> p r u k", u=2),
                                                AX_X, ALU.max, negate=True).then_inc(max_done, 1)

                    def parts(w):
                        dve.wait_ge(max_done, 4 * w + 4)
                        if not (isinstance(w, int) and w == 0):
                            dve.wait_ge(mtp, w)
                        nc.vector.tensor_copy(nm3[:, 0:H], negm[:, :]).then_inc(wch, 1)
                        dve.wait_ge(wch, 4 * w + 1)
                        nc.vector.tensor_tensor(nrest[:, :], negm[:, :], nm3[:, 0:H], ALU.subtract).then_inc(wch, 1)
                        dve.wait_ge(wch, 4 * w + 2)
                        nc.vector.tensor_copy(nm3[:, H:2 * H], nrest[:, :]).then_inc(wch, 1)
                        dve.wait_ge(wch, 4 * w + 3)
                        nc.vector.tensor_tensor(nm3[:, 2 * H:3 * H], nrest[:, :], nm3[:, H:2 * H], ALU.subtract).then_inc(nm_ready, 1)
                        dve.sem_inc(wch, 1)

                    def maxima_t(w, wp):
                        dve.wait_ge(mtp, w + 1)
                        if not (isinstance(w, int) and w < 2):
                            dve.wait_ge(t_done, 4 * w - 4)
                        nc.vector.tensor_copy(m_t[:, wp, :], misc_bf).then_inc(mt, 1)

                    def norm(s):
                        dve.wait_ge(otp, s + 1)
                        if not (isinstance(s, int) and s == 0):
                            dve.wait_ge(atp, s)
                        nat = psum[:, MISC, :].rearrange("p (g r u m) -> p g r u m", g=NG, r=2, u=2)
                        rv = rec[:, :].rearrange("p (g u r) -> p g r u", g=NG, u=2)
                        av = attn[:, :, :].rearrange("p (g u r) d -> p g r u d", g=NG, u=2)
                        nc.vector.reciprocal(rv, nat[:, :, :, :, DH]).then_inc(rch, 1)
                        dve.wait_ge(rch, s + 1)
                        for r in range(2):
                            last = nc.vector.tensor_tensor(av[:, :, r], nat[:, :, r, :, 0:DH], rv[:, :, r].unsqueeze(3).broadcast_to([P, NG, 2, DH]), ALU.mult)
                        last.then_inc(norm_done, 1)

                    def body(s, sp):
                        last = isinstance(s, int) and s == NS - 1
                        if not last:
                            maxima(s + 1, 0)
                        if last:
                            norm(s - 1)
                            return
                        if not (isinstance(s, int) and s == 0):
                            dve.wait_ge(pv_done, 4 * s)
                        window_v(s + 1, 1 - sp)
                        maxima(s + 1, 1)
                        if not (isinstance(s, int) and s == 0):
                            norm(s - 1)
                        maxima(s + 1, 2)
                        maxima(s + 1, 3)
                        parts(s + 1)
                        if not (isinstance(s, int) and s == NS - 2):
                            dve.wait_ge(t_done, 4 * s + 4)
                            window(s + 2, sp)
                        maxima_t(s + 1, 1 - sp)

                    dve.wait_ge(cleared, 1)
                    dve.wait_ge(v_ready, 4)
                    window(0, 0)
                    window(1, 1)
                    window_v(0, 0)
                    for g in range(NG):
                        maxima(0, g)
                    parts(0)
                    maxima_t(0, 0)
                    steps(dve, body)
                    def with_bias(q):
                        dve.wait_ge(proj, q + 1)
                        nc.vector.tensor_tensor(y[:, 4 * q:4 * q + 4, :], psum[:, SN + q, :].rearrange("p (t n) -> p t n", t=4),
                                                bout[:, :].unsqueeze(1).broadcast_to([P, 4, P]), ALU.add).then_inc(y_ready, 1)
                        dve.wait_ge(y_ready, q + 1)
                        for t in range(4 * q, 4 * q + 4):
                            ln_y.tile_stats(t, y[:, t, :])

                    for q in range(3):
                        with_bias(q)
                    norm(NS - 1)
                    with_bias(3)
                    ln_y.finish(dve)
                    scale_on_dve(ln_y, lambda t: y[:, t, :], lambda t: y[:, t, :])
                    add_dve_tiles(dve, ln_y, x, lambda t: y[:, t, :])

                @block.scalar
                def _(act):
                    ln.root(act)
                    scale_on_act(act, ln, lambda t: xn[:, t, :], lambda t: x[:, t, :])
                    act.wait_ge(bq_ready, 1)
                    for ch in range(4):
                        act.wait_ge(tp_done, ch + 1)
                        nc.scalar.copy(xt[:, 512 * ch:512 * ch + 512], psum[:, ch % 2, :]).then_inc(xt_ready, 1)
                    for ch in range(4):
                        cols = slice(512 * ch, 512 * ch + 512)
                        act.wait_ge(proj_done, ch + 1)
                        if ch >= 2:
                            act.wait_ge(split_done, 2 * ch - 2)
                        nc.scalar.activation(full[:, ch % 2, 0, :], psum[:, 2, :], ACT.Identity, bias=bq_s[:, 0:1], scale=scale).then_inc(full_ready, 1)
                        nc.scalar.activation(full[:, ch % 2, 1, :], psum[:, 3, :], ACT.Identity, bias=bqk[:, 1:2], scale=1.0).then_inc(full_ready, 1)
                        for w in range(2):
                            act.wait_ge(full_ready, 2 * ch + w + 1)
                            nc.scalar.copy(part["h"][:, w, cols], full[:, ch % 2, w, :]).then_inc(hi_ready, 1)

                    def exps(s, g):
                        act.wait_ge(t_done, 4 * s + g + 1)
                        if not (isinstance(s, int) and s == 0):
                            act.wait_ge(pv_done, 4 * s + g - 3)
                        nc.scalar.activation(e[:, g, :, :, :].rearrange("p h j q -> p (h j q)"),
                                             psum[:, ST:ST + 2, :].rearrange("p b n -> p (b n)"), ACT.Exp).then_inc(exp_done, 1)

                    def attn_t(s):
                        act.wait_ge(atp, s + 1)
                        nc.scalar.copy(a_t[:, bass.ds(s * P, P)], psum[:, MISC, 0:P]).then_inc(at_done, 1)

                    def values_out(s):
                        act.wait_ge(pv_done, 4 * s + 4)
                        if not (isinstance(s, int) and s == 0):
                            act.wait_ge(otp, s)
                        nc.scalar.copy(o_sb[:, :, :].rearrange("p g q -> p (g q)"), psum[:, PV, :]).then_inc(o_done, 1)

                    def body(s, sp):
                        late = not (isinstance(s, int) and s == 0)
                        exps(s, 0)
                        if late:
                            values_out(s - 1)
                        exps(s, 1)
                        exps(s, 2)
                        if late:
                            attn_t(s - 1)
                        exps(s, 3)

                    steps(act, body)
                    values_out(NS - 1)
                    attn_t(NS - 1)
                    ln_y.root(act)
                    scale_on_act(act, ln_y, lambda t: y[:, t, :], lambda t: y[:, t, :])

                @block.tensor
                def _(pe):
                    pe.wait_ge(loaded, 16 * NL)
                    for ch in range(4):
                        tiles_scaled(pe, ln, 4 * ch + 4)
                        if ch >= 2:
                            pe.wait_ge(xt_ready, ch - 1)
                        for t in range(4):
                            last = nc.tensor.transpose(psum[:, ch % 2, P * t:P * t + P], xn[:, 4 * ch + t, :], c["ident"][:, :])
                        last.then_inc(tp_done, 1)
                    for ch in range(4):
                        pe.wait_ge(xt_ready, ch + 1)
                        if ch >= 1:
                            pe.wait_ge(full_ready, 2 * ch)
                        if ch >= 2:
                            pe.wait_ge(v_ready, ch - 1)
                        for w in range(2):
                            nc.tensor.matmul(psum[:, 2 + w, :], wqkv[:, w * P:w * P + P], xt[:, 512 * ch:512 * ch + 512], start=True, stop=True)
                        for t in range(4):
                            last = nc.tensor.matmul(psum[:, 4 + ch % 2, P * t:P * t + P], xt[:, 512 * ch + P * t:512 * ch + P * t + P],
                                                    wqkv[:, 2 * P:3 * P], start=True, stop=True)
                        last.then_inc(proj_done, 1)

                    def natural(w, wp, g):
                        first = isinstance(w, int) and 4 * w + g < 2
                        if g == 0:
                            pe.wait_ge(win, w + 1)
                        if not first:
                            pe.wait_ge(max_done, 4 * w + g - 1)
                        for r in range(2):
                            nc.tensor.matmul(psum[:, SN + 2 * (g % 2) + r, :], c["identb"][:, :], c["mask"][:, :, :].rearrange("p a b -> p (a b)"),
                                             start=True, stop=False)
                        for u in range(2):
                            for r in range(2):
                                rows = slice(64 * r, 64 * r + 64)
                                last = nc.tensor.matmul(psum[:, SN + 2 * (g % 2) + r, 256 * u:256 * u + 256], qw[rows, wp, 2 * g + u, :],
                                                        kw[rows, wp, 2 * g + u, :], start=False, stop=(u == 1))
                        last.then_inc(n_done, 1)

                    def transposed(s, sp, g):
                        if g == 0:
                            pe.wait_ge(mt, s + 1)
                        if not (isinstance(s, int) and 4 * s + g < 1):
                            pe.wait_ge(exp_done, 4 * s + g)
                        for r in range(2):
                            for u in range(2):
                                nc.tensor.matmul(psum[:, ST + r, 256 * u:256 * u + 256].rearrange("p (j q) -> p j q", j=2), c["sel"][:, 4 * g + 2 * u + r, :],
                                                 m_t[:, sp, :].unsqueeze(1).broadcast_to([P, 2, P]), start=(u == 0), stop=False)
                        for u in range(2):
                            for j in range(2):
                                for r in range(2):
                                    rows = slice(64 * r, 64 * r + 64)
                                    last = nc.tensor.matmul(psum[:, ST + r, 256 * u + P * j:256 * u + P * j + P], kw[rows, sp, 2 * g + u, P * j:P * j + P],
                                                            qw[rows, sp, 2 * g + u, :], start=False, stop=(u == 1 and j == 1))
                        last.then_inc(t_done, 1)

                    def values(s, sp, g):
                        if g == 0:
                            pe.wait_ge(vwin, s + 1)
                            if not (isinstance(s, int) and s == 0):
                                pe.wait_ge(o_done, s)
                        pe.wait_ge(sel_done, 4 * s + g + 1)
                        for k in range(GH):
                            h = GH * g + 2 * (k % 2) + k // 2
                            for j in range(2):
                                last = nc.tensor.matmul(psum[32 * k:32 * k + 32, PV, P * g:P * g + P], vw[:, sp, j, h, :], e[:, g, k, j, :],
                                                        start=(j == 0), stop=(j == 1))
                        last.then_inc(pv_done, 1)

                    def maxima_t(w):
                        pe.wait_ge(nm_ready, w + 1)
                        if not (isinstance(w, int) and w < 2):
                            pe.wait_ge(at_done, w - 1)
                        nc.tensor.transpose(misc_bf, nm3[:, :], c["identb"][:, :]).then_inc(mtp, 1)

                    def values_nat(s):
                        pe.wait_ge(o_done, s + 1)
                        for g in range(NG):
                            last = nc.tensor.transpose(psum[:, MISC, P * g:P * g + P], o_sb[:, g, :], c["ident"][:, :])
                        last.then_inc(otp, 1)

                    def attn_t(s):
                        pe.wait_ge(norm_done, s + 1)
                        nc.tensor.transpose(psum[:, MISC, 0:P], attn[:, :, :].rearrange("p h d -> p (h d)"), c["ident"][:, :]).then_inc(atp, 1)

                    def project(q):
                        pe.wait_ge(at_done, min(4 * q + 5, NS))
                        for t in range(4):
                            col = 64 + P * (4 * q + t)
                            last = nc.tensor.matmul(psum[:, SN + q, P * t:P * t + P], a_t[:, col:col + P], wout[:, :], start=True, stop=True)
                        last.then_inc(proj, 1)

                    def body(s, sp):
                        more = not (isinstance(s, int) and s == NS - 1)
                        late = not (isinstance(s, int) and s == 0)
                        nat = (lambda g: natural(s + 1, 1 - sp, g)) if more else (lambda g: None)
                        nat(0)
                        transposed(s, sp, 0)
                        if not more:
                            project(0)
                        if late:
                            values(s - 1, 1 - sp, 3)
                        if not more:
                            project(1)
                        nat(1)
                        if late:
                            values_nat(s - 1)
                        transposed(s, sp, 1)
                        if not more:
                            project(2)
                        nat(2)
                        transposed(s, sp, 2)
                        nat(3)
                        values(s, sp, 0)
                        if late:
                            attn_t(s - 1)
                        transposed(s, sp, 3)
                        values(s, sp, 1)
                        values(s, sp, 2)
                        if more:
                            maxima_t(s + 1)

                    pe.wait_ge(consts_ready, n_consts[0])
                    pe.wait_ge(xt_ready, 4)
                    pe.wait_ge(full_ready, 8)
                    pe.wait_ge(v_ready, 4)
                    for g in range(NG):
                        natural(0, 0, g)
                    maxima_t(0)
                    steps(pe, body)
                    values(NS - 1, 0, 3)
                    values_nat(NS - 1)
                    attn_t(NS - 1)
                    project(3)
        nc.clear_and_free_semaphores(used)
        nc.all_engine_barrier()


def kmoe(nc, x, c, d):
    T, R, E = 256, 8, 64
    D1, F1 = 32, 64
    NT, H, K = 16, 2, 2
    N = T // H
    NG = N // 2
    W = 512
    with ExitStack() as ctx:
        a = Alloc(nc, ctx, "ff")
        psum = a.ps("psum", [P, 8, W])
        h = a.sb("h", [P, N, F1])
        wdn = a.sb("w_down", [P, F1, H, E])
        bias_up = a.sb("bias_up", [F1, F1])
        bias_dn = a.sb("bias_down", [D1, D1])
        scales = a.sb("scales", [P, 2])
        ids = a.sb("expert_ids", [P, E])
        lg = a.sb("logits", [P, H, E])
        mx = a.sb("top_values", [P, H, 8])
        ix = a.sb("top_index", [P, H, 8], U32)
        ef = a.sb("experts", [P, H, K])
        dv = a.sb("gap", [P, H])
        ev = a.sb("gap_exp", [P, H])
        pr = a.sb("probs", [P, K, H])
        oh = a.sb("one_hot", [P, 2, K, H, E])
        oht = a.sb("one_hot_t", [P, 2, K, N])
        loaded, down_loaded = a.sem("loaded"), a.sem("down_loaded")
        rch = Count(a.sem("route_chain"))
        gap_ready, exp_ready, oh_ready, oh_tp, routed = (a.sem(s) for s in ("gap_ready", "exp_ready", "one_hot_ready", "one_hot_psum", "routed"))

        def route_dve(dve, n, src):
            v = nc.vector
            rch.up(v.tensor_copy(lg[:, :, :], src))
            rch.settle(dve)
            for t in range(H):
                rch.up(v.max(mx[:, t, :], lg[:, t, :]))
            rch.settle(dve)
            v.tensor_tensor(dv[:, :], mx[:, :, 1], mx[:, :, 0], ALU.subtract).then_inc(gap_ready, 1)
            for t in range(H):
                rch.up(v.max_index(ix[:, t, :], mx[:, t, :], lg[:, t, :]))
            rch.settle(dve)
            rch.up(v.tensor_copy(ef[:, :, :], ix[:, :, 0:K]))
            rch.settle(dve)
            for k in range(K):
                for t in range(H):
                    v.tensor_scalar(oh[:, 0, k, t, :], ids[:, :], ef[:, t, k:k + 1], None, ALU.is_equal)
            dve.wait_ge(exp_ready, n + 1)
            rch.up(v.tensor_scalar(dv[:, :], ev[:, :], 1.0, None, ALU.add))
            rch.settle(dve)
            rch.up(v.reciprocal(pr[:, 0, :], dv[:, :]))
            rch.settle(dve)
            rch.up(v.tensor_tensor(pr[:, 1, :], ev[:, :], pr[:, 0, :], ALU.mult))
            rch.settle(dve)
            for k in range(K):
                for t in range(H):
                    last = v.tensor_scalar(oh[:, 1, k, t, :], ids[:, :], ef[:, t, k:k + 1], pr[:, k, t:t + 1], ALU.is_equal, ALU.mult)
            last.then_inc(oh_ready, 1)
            dve.wait_ge(oh_tp, n + 1)
            v.tensor_copy(oht[:, :, :, :].rearrange("p a k n -> p (a k n)"), psum[:, 5, :]).then_inc(routed, 1)

        def route_act(act, n):
            act.wait_ge(gap_ready, n + 1)
            nc.scalar.activation(ev[:, :], dv[:, :], ACT.Exp).then_inc(exp_ready, 1)

        def route_pe(pe, n):
            pe.wait_ge(oh_ready, n + 1)
            for kind in range(2):
                for k in range(K):
                    m = K * kind + k
                    last = nc.tensor.transpose(psum[:, 5, P * m:P * m + P], oh[:, kind, k, :, :].rearrange("p h e -> p (h e)"), c["ident"][:, :])
            last.then_inc(oh_tp, 1)

        def emptied(pe, u, act_done, dve_done):
            if u >= 4:
                pe.wait_ge(act_done if u % 2 == 0 else dve_done, (u - 4) // 2 + 1)

        with ExitStack() as ctx0:
            b0 = Alloc(nc, ctx0, "f0")
            x4 = b0.sb("x_blocks", [P, NG, P])
            gb = b0.sb("b_taken", [P, NG, K, F1])
            ga = b0.sb("a_taken", [P, NG, K, F1])

            with ExitStack() as ctx1:
                b = Alloc(nc, ctx1, "f1")
                flat = h[:, :, :].rearrange("p n o -> p (n o)")
                xt = flat[:, 0:T * R]
                xn = flat[:, T * R:2 * T * R].rearrange("p (t n) -> p t n", t=NT)
                wup = ga[:, 0:R // 2, :, :].rearrange("p g k n -> p (g k) n")
                bup = b.sb("b_up", [P, F1, H, D1])
                aup = b.sb("a_up", [P, F1, H, D1])
                ln = Norm(nc, b, "ln", NT)
                zeroed = b.sem("zeroed")
                wup_loaded, b_loaded, a_loaded = (b.sem(s) for s in ("w_up_loaded", "b_loaded", "a_loaded"))
                tp_done, xt_ready, lg_done, x4_part, got, act_took, dve_took = (b.sem(s) for s in (
                    "tp_done", "xt_ready", "lg_done", "x_block", "got_psum", "act_took", "dve_took"))
                UB = F1 // 4

                def took(u):
                    dst, col = (gb, ga)[u // UB], 4 * (u % UB)
                    src = psum[:, u % 4, :].rearrange("p (c k m g) -> p m c k g", c=2, k=K, m=2)
                    return [(dst[64 * m:64 * m + 64, :, :, col + odd:col + odd + 3:2].rearrange("p g k c -> p c k g"), src[64 * odd:64 * odd + 64, m])
                            for odd in range(2) for m in range(2)]

                with nc.Block() as block:
                    @block.sync
                    def _(sp):
                        sp.dma_start(wup[:, :, :], d["w_up"]).then_inc(wup_loaded, 16)
                        sp.dma_start(ids[:, :], d["expert_ids"].broadcast_to([P, E])).then_inc(wup_loaded, 16)
                        for t in range(H):
                            sp.dma_start(bup[E * t:E * t + E, :, t, :], d["b_up"]).then_inc(b_loaded, 16)
                        for t in range(H):
                            sp.dma_start(aup[E * t:E * t + E, :, t, :], d["a_up"]).then_inc(a_loaded, 16)
                        sp.dma_start(bias_up[:, :], d["bias_up"]).then_inc(loaded, 16)
                        sp.dma_start(bias_dn[:, :], d["bias_down"]).then_inc(loaded, 16)
                        sp.dma_start(scales[:, 0:1], d["scale_up"].broadcast_to([P, 1])).then_inc(loaded, 16)
                        sp.dma_start(scales[:, 1:2], d["scale_down"].broadcast_to([P, 1])).then_inc(loaded, 16)
                        for t in range(H):
                            sp.dma_start(wdn[E * t:E * t + E, :, t, :], d["w_down"]).then_inc(down_loaded, 16)

                    @block.gpsimd
                    def _(g):
                        ch = Count(zeroed)
                        for n, part in enumerate((bup, aup, x4, wdn)):
                            if part is x4:
                                ch.settle(g)
                                ch.up(nc.gpsimd.memset(part[:, :, :], 0.0))
                                continue
                            for t in range(H):
                                ch.settle(g) if ch.n else None
                                ch.up(nc.gpsimd.memset(part[E * t:E * t + E, :, 1 - t, :], 0.0))
                    B_ZERO, A_ZERO, X_ZERO, W_ZERO = 2, 4, 5, 7

                    @block.vector
                    def _(dve):
                        for t in range(NT):
                            ln.tile_stats(t, x[:, t, :])
                        ln.finish(dve)
                        scale_on_dve(ln, lambda t: xn[:, t, :], lambda t: x[:, t, :])
                        dve.wait_ge(wup_loaded, 32)
                        dve.wait_ge(lg_done, 1)
                        route_dve(dve, 0, psum[:, 4, 0:H * E].rearrange("p (t e) -> p t e", t=H))
                        for u in range(1, 2 * UB, 2):
                            dve.wait_ge(got, u + 1)
                            for dst, src in took(u):
                                last = nc.vector.tensor_copy(dst, src)
                            last.then_inc(dve_took, 1)

                    @block.scalar
                    def _(act):
                        ln.root(act)
                        scale_on_act(act, ln, lambda t: xn[:, t, :], lambda t: x[:, t, :])
                        for ch in range(4):
                            act.wait_ge(tp_done, ch + 1)
                            nc.scalar.copy(xt[:, W * ch:W * ch + W], psum[:, ch, :]).then_inc(xt_ready, 1)
                        act.wait_ge(xt_ready, 4)
                        act.wait_ge(zeroed, X_ZERO)
                        rows = xt.rearrange("p (m g t r) -> p m t g r", m=2, t=H, r=R)

                        def blocks(q):
                            for m in range(2):
                                for t in range(H):
                                    tok = 2 * m + t
                                    dst = x4[32 * tok:32 * tok + 32, :, 32 * tok:32 * tok + 32].rearrange("p g (r q) -> p q g r", q=4)
                                    nc.scalar.copy(dst[:, q], rows[32 * q:32 * q + 32, m, t]).then_inc(x4_part, 1)
                        blocks(0)
                        route_act(act, 0)
                        blocks(1)
                        blocks(2)
                        blocks(3)
                        for u in range(0, 2 * UB, 2):
                            act.wait_ge(got, u + 1)
                            for dst, src in took(u):
                                last = nc.scalar.copy(dst, src)
                            last.then_inc(act_took, 1)

                    @block.tensor
                    def _(pe):
                        for ch in range(4):
                            tiles_scaled(pe, ln, 4 * ch + 4)
                            for t in range(4):
                                last = nc.tensor.transpose(psum[:, ch, P * t:P * t + P], xn[:, 4 * ch + t, :], c["ident"][:, :])
                            last.then_inc(tp_done, 1)
                        pe.wait_ge(wup_loaded, 32)
                        pe.wait_ge(xt_ready, 4)
                        rows = xt.rearrange("p (n t r) -> p t r n", t=H, r=R)
                        for t in range(H):
                            for r in range(R):
                                last = nc.tensor.matmul(psum[:, 4, E * t:E * t + E], rows[:, t, r], wup[:, r, :], start=(r == 0), stop=(r == R - 1))
                        last.then_inc(lg_done, 1)
                        route_pe(pe, 0)
                        pe.wait_ge(routed, 1)
                        for u in range(2 * UB):
                            if u == 0:
                                pe.wait_ge(b_loaded, 16 * H)
                                pe.wait_ge(zeroed, B_ZERO)
                            if u == UB:
                                pe.wait_ge(a_loaded, 16 * H)
                                pe.wait_ge(zeroed, A_ZERO)
                            emptied(pe, u, act_took, dve_took)
                            for half in range(2):
                                col = 4 * (u % UB) + 2 * half
                                factor = (bup, aup)[u // UB][:, col:col + 2, :, :].rearrange("p c h j -> p (c h j)")
                                last = nc.tensor.matmul(psum[:, u % 4, 256 * half:256 * half + 256], factor, oht[:, u // UB, :, :].rearrange("p k n -> p (k n)"),
                                                        start=True, stop=True)
                            last.then_inc(got, 1)

            with ExitStack() as ctx1:
                b = Alloc(nc, ctx1, "f2")
                CG, NCH = 8, NG // 8
                z = b.sb("z", [P, 2, CG, K, H, F1])
                z_clear, zeroed, z_done, z_ready, h_done, hb_ready, gelu_done = (b.sem(s) for s in ("z_clear", "zeroed", "z_psum", "z_ready", "h_psum", "h_biased", "gelu_done"))
                with nc.Block() as block:
                    @block.gpsimd
                    def _(g):
                        nc.gpsimd.memset(z[:, 1, :, :, :, :], 0.0).then_inc(zeroed, 1)

                    @block.tensor
                    def _(pe):
                        def first(ch):
                            for half in range(2):
                                if ch >= 1:
                                    pe.wait_ge(z_ready, 2 * (ch - 1) + half + 1)
                                for k in range(4):
                                    g = CG * ch + 4 * half + k
                                    last = nc.tensor.matmul(psum[:, half, P * k:P * k + P], x4[:, g, :], gb[:, g, :, :].rearrange("p k n -> p (k n)"), start=True, stop=True)
                                last.then_inc(z_done, 1)

                        def second(ch):
                            pe.wait_ge(z_ready, 2 * ch + 2)
                            for tok in range(4):
                                u, m, t = 4 * ch + tok, tok // 2, tok % 2
                                rows = slice(64 * m, 64 * m + 64)
                                if u >= 6:
                                    pe.wait_ge(hb_ready, u - 5)
                                for g in range(CG):
                                    for k in range(K):
                                        last = nc.tensor.matmul(psum[0:F1, 2 + u % 6, F1 * g:F1 * g + F1], z[rows, ch % 2, g, k, t, :], ga[rows, CG * ch + g, k, :],
                                                                start=(k == 0), stop=(k == K - 1))
                                last.then_inc(h_done, 1)
                        first(0)
                        for ch in range(NCH):
                            if ch + 1 < NCH:
                                first(ch + 1)
                            second(ch)

                    @block.vector
                    def _(dve):
                        nc.vector.memset(z[:, 0, :, :, :, :], 0.0).then_inc(z_clear, 1)
                        dve.wait_ge(loaded, 16 * 4)
                        for ch in range(NCH):
                            for tok in range(4):
                                u, n0 = 4 * ch + tok, NG * (tok // 2) + CG * ch
                                rows = slice(64 * (tok % 2), 64 * (tok % 2) + 64)
                                dve.wait_ge(h_done, u + 1)
                                nc.vector.scalar_tensor_tensor(out=h[rows, n0:n0 + CG, :], in0=psum[0:F1, 2 + u % 6, :].rearrange("p (g o) -> p g o", g=CG),
                                                               scalar=scales[0:F1, 0:1], in1=bias_up[:, :].unsqueeze(1).broadcast_to([F1, CG, F1]),
                                                               op0=ALU.mult, op1=ALU.add).then_inc(hb_ready, 1)

                    @block.scalar
                    def _(act):
                        def take(ch):
                            if ch == 0:
                                act.wait_ge(z_clear, 1)
                            if ch == 1:
                                act.wait_ge(zeroed, 1)
                            if ch >= 2:
                                act.wait_ge(h_done, 4 * (ch - 1))
                            for half in range(2):
                                act.wait_ge(z_done, 2 * ch + half + 1)
                                for tok in range(4):
                                    rows = slice(32 * tok, 32 * tok + 32)
                                    last = nc.scalar.copy(z[rows, ch % 2, 4 * half:4 * half + 4, :, tok % 2, :].rearrange("p g k n -> p (g k) n"),
                                                          psum[rows, half, :].rearrange("p (g n) -> p g n", n=F1))
                                last.then_inc(z_ready, 1)

                        def gelu(ch):
                            act.wait_ge(hb_ready, 4 * ch + 4)
                            for m in range(2):
                                part = h[:, NG * m + CG * ch:NG * m + CG * ch + CG, :].rearrange("p n o -> p (n o)")
                                nc.scalar.activation(part, part, ACT.Gelu).then_inc(gelu_done, 1)
                        take(0)
                        for ch in range(NCH):
                            if ch + 1 < NCH:
                                take(ch + 1)
                            if ch >= 1:
                                gelu(ch - 1)
                        gelu(NCH - 1)

        with ExitStack() as ctx0:
            b = Alloc(nc, ctx0, "f3")
            bdn = b.sb("b_down", [P, D1, H, F1])
            adn = b.sb("a_down", [P, D1, H, F1])
            gb = b.sb("b_taken", [P, N, K, D1])
            ga = b.sb("a_taken", [P, N, K, D1])
            vs = b.sb("v", [P, 2, 8, K, D1])
            yb = wdn[0:D1, :, :, :].rearrange("p o h e -> p (o h e)").rearrange("p (t a) -> p t a", t=T)
            lgt = b.sb("logits_t", [P, N])
            ln = Norm(nc, b, "ln", NT, in_psum=True)
            lg_done, lgt_ready, lg_nat, zeroed, b_loaded, a_loaded = (b.sem(s) for s in ("lgt_psum", "lgt_ready", "lg_nat", "zeroed", "b_loaded", "a_loaded"))
            got, act_took, dve_took = (b.sem(s) for s in ("got_psum", "act_took", "dve_took"))
            v_done, v_ready, y_done, y_ready, nat_done = (b.sem(s) for s in ("v_psum", "v_ready", "y_psum", "y_ready", "nat_done"))
            tile = lambda t: psum[:, 2 + t // 4, P * (t % 4):P * (t % 4) + P]
            y_rows = gb[:, 0:32, :, :].rearrange("p n k a -> p (n k a)").rearrange("p (t n) -> p t n", t=NT)
            y = lambda t: y_rows[:, t, :]
            UB = D1 // 2
            CP, NCH = 8, N // 8

            def took(u):
                dst = (gb, ga)[u // UB]
                col = 2 * (u % UB)
                return dst[:, :, :, col:col + 2].rearrange("p n k c -> p k n c"), psum[:, u % 4, :].rearrange("p (c k n) -> p k n c", c=2, k=K)

            with nc.Block() as block:
                @block.sync
                def _(sp):
                    for t in range(H):
                        sp.dma_start(bdn[E * t:E * t + E, :, t, :], d["b_down"]).then_inc(b_loaded, 16)
                    for t in range(H):
                        sp.dma_start(adn[E * t:E * t + E, :, t, :], d["a_down"]).then_inc(a_loaded, 16)

                @block.gpsimd
                def _(g):
                    ch = Count(zeroed)
                    for part in (bdn, adn):
                        for t in range(H):
                            ch.settle(g) if ch.n else None
                            ch.up(nc.gpsimd.memset(part[E * t:E * t + E, :, 1 - t, :], 0.0))
                    add_act_tiles(g, ln, x, y)

                @block.tensor
                def _(pe):
                    pe.wait_ge(down_loaded, 32)
                    for o in range(F1):
                        last = nc.tensor.matmul(psum[:, 4, 0:N], wdn[:, o, :, :].rearrange("p h e -> p (h e)"), h[:, :, o], start=(o == 0), stop=(o == F1 - 1))
                    last.then_inc(lg_done, 1)
                    pe.wait_ge(lgt_ready, 1)
                    nc.tensor.transpose(psum[:, 6, 0:P], lgt[:, :], c["ident"][:, :]).then_inc(lg_nat, 1)
                    route_pe(pe, 1)
                    pe.wait_ge(routed, 2)
                    for u in range(2 * UB):
                        if u == 0:
                            pe.wait_ge(b_loaded, 32)
                            pe.wait_ge(zeroed, 2)
                        if u == UB:
                            pe.wait_ge(a_loaded, 32)
                            pe.wait_ge(zeroed, 4)
                        emptied(pe, u, act_took, dve_took)
                        for col in range(2):
                            factor = (bdn, adn)[u // UB][:, 2 * (u % UB) + col, :, :].rearrange("p h j -> p (h j)")
                            last = nc.tensor.matmul(psum[:, u % 4, 256 * col:256 * col + 256], factor, oht[:, u // UB, :, :].rearrange("p k n -> p (k n)"), start=True, stop=True)
                        last.then_inc(got, 1)

                    def first(ch):
                        for t in range(H):
                            rows = slice(64 * t, 64 * t + 64)
                            if ch >= 1:
                                pe.wait_ge(v_ready, H * (ch - 1) + t + 1)
                            for n in range(CP):
                                last = nc.tensor.matmul(psum[0:F1, 4 + t, F1 * n:F1 * n + F1], h[rows, CP * ch + n, :], gb[rows, CP * ch + n, :, :].rearrange("p k n -> p (k n)"),
                                                        start=True, stop=True)
                            last.then_inc(v_done, 1)

                    def second(ch):
                        for t in range(H):
                            rows = slice(64 * t, 64 * t + 64)
                            pe.wait_ge(v_ready, H * ch + t + 1)
                            if ch >= 2:
                                pe.wait_ge(y_ready, H * (ch - 2) + t + 1)
                            for n in range(CP):
                                for k in range(K):
                                    last = nc.tensor.matmul(psum[0:D1, (6, 0)[ch % 2] + t, D1 * n:D1 * n + D1], vs[rows, ch % 2, n, k, :], ga[rows, CP * ch + n, k, :],
                                                            start=(k == 0), stop=(k == K - 1))
                            last.then_inc(y_done, 1)
                    pe.wait_ge(act_took, UB)
                    pe.wait_ge(dve_took, UB)
                    first(0)
                    for ch in range(NCH):
                        if ch + 1 < NCH:
                            first(ch + 1)
                        second(ch)
                    pe.wait_ge(y_ready, H * NCH)
                    quarters = yb.rearrange("b t (r q) -> b q (t r)", q=4)
                    for t in range(NT):
                        for q in range(4):
                            last = nc.tensor.transpose(psum[:, 2 + t // 4, P * (t % 4) + 32 * q:P * (t % 4) + 32 * q + 32], quarters[:, q, P * t:P * t + P],
                                                       c["ident"][0:D1, 0:D1])
                        if t % 4 == 3:
                            last.then_inc(nat_done, 1)

                @block.vector
                def _(dve):
                    dve.wait_ge(lg_nat, 1)
                    route_dve(dve, 1, psum[:, 6, 0:P].rearrange("p (t e) -> p t e", t=H))
                    for u in range(1, 2 * UB, 2):
                        dve.wait_ge(got, u + 1)
                        dst, src = took(u)
                        nc.vector.tensor_copy(dst, src).then_inc(dve_took, 1)
                    pairs = yb.rearrange("b (n t) a -> b t n a", t=H)
                    for ch in range(NCH):
                        for t in range(H):
                            dve.wait_ge(y_done, H * ch + t + 1)
                            nc.vector.scalar_tensor_tensor(out=pairs[:, t, CP * ch:CP * ch + CP, :], in0=psum[0:D1, (6, 0)[ch % 2] + t, 0:CP * D1].rearrange("p (n a) -> p n a", n=CP),
                                                           scalar=scales[0:D1, 1:2], in1=bias_dn[:, :].unsqueeze(1).broadcast_to([D1, CP, D1]),
                                                           op0=ALU.mult, op1=ALU.add).then_inc(y_ready, 1)
                    for t in range(NT):
                        if t % 4 == 0:
                            dve.wait_ge(nat_done, t // 4 + 1)
                        ln.tile_stats(t, tile(t))
                    ln.finish(dve)
                    scale_on_dve(ln, y, tile)
                    add_dve_tiles(dve, ln, x, y)

                @block.scalar
                def _(act):
                    act.wait_ge(lg_done, 1)
                    nc.scalar.copy(lgt[:, :], psum[:, 4, 0:N]).then_inc(lgt_ready, 1)
                    route_act(act, 1)
                    for u in range(0, 2 * UB, 2):
                        act.wait_ge(got, u + 1)
                        dst, src = took(u)
                        nc.scalar.copy(dst, src).then_inc(act_took, 1)
                    for ch in range(NCH):
                        for t in range(H):
                            rows = slice(64 * t, 64 * t + 64)
                            act.wait_ge(v_done, H * ch + t + 1)
                            if ch >= 2:
                                act.wait_ge(y_done, H * (ch - 2) + t + 1)
                            nc.scalar.copy(vs[rows, ch % 2, :, :, :].rearrange("p n k b -> p (n k b)"), psum[0:F1, 4 + t, :]).then_inc(v_ready, 1)
                    ln.root(act)
                    scale_on_act(act, ln, y, tile)


def ssm(nc, x, c, d):
    T, NT, NC, W = 2048, 16, 4, 512
    NB, S, K = 2, 64, 4
    with ExitStack() as ctx:
        a = Alloc(nc, ctx, "sm")
        psum = a.ps("psum", [P, 8, W])
        xn = a.sb("xn", [P, NT, P])
        xt = a.sb("xt", [P, T])
        w_in = a.sb("w_in", [P, 2 * NB * P])
        cw = a.sb("conv_w", [P, NB, K])
        cb = a.sb("conv_b", [P, NB])
        wb = a.sb("w_b", [P, NB, S])
        wc = a.sb("w_c", [S, NB * P])
        dp = a.sb("d_param", [P, NB])
        wo = a.sb("w_out", [P, NB, P])
        gamma = a.sb("gamma", [P, P])
        beta = a.sb("beta", [P, P])
        xin = a.sb("x_in", [P, NB, K - 1 + T])
        gate = a.sb("gate", [P, NB, T])
        u = a.sb("u", [P, NB, T])
        bu = a.sb("bu", [S, T])
        decay = a.sb("decay", [S, W])
        hs = a.sb("states", [S, T])
        yg = a.sb("y_gated", [P, NB, T])
        z = a.sb("z", [P, NT, P])
        ln_x, ln_z, ln_o = (Norm(nc, a, n, NT) for n in ("ln_x", "ln_z", "ln_o"))
        loaded, tp_done, xt_ready = (a.sem(s) for s in ("loaded", "tp_done", "xt_ready"))
        in_done, xin_ready, gate_ready, conv_done, u_ready = (a.sem(s) for s in ("in_psum", "xin_ready", "gate_ready", "conv_done", "u_ready"))
        bu_done, bu_ready, hs_ready, y_done, yg_ready = (a.sem(s) for s in ("bu_psum", "bu_ready", "hs_ready", "y_psum", "yg_ready"))
        yd_ready, o_done, z_ready = (a.sem(s) for s in ("yd_ready", "o_psum", "z_ready"))
        cch, och = Count(a.sem("conv_chain")), Count(a.sem("out_chain"))
        pads = a.sem("pads")
        loads = [(w_in[:, :], d["w_in"]), (cw[:, :, :], d["conv_w"]), (cb[:, :], d["conv_b"]), (wb[:, :, :], d["w_b"]), (wc[:, :], d["w_c"]),
                 (dp[:, :], d["d_param"]), (wo[:, :, :], d["w_out"]), (gamma[:, :], d["gamma"].broadcast_to([P, P])), (beta[:, :], d["beta"].broadcast_to([P, P]))]
        with nc.Block() as block:
            @block.sync
            def _(sp):
                for dst, src in loads:
                    sp.dma_start(dst, src).then_inc(loaded, 16)

            @block.tensor
            def _(pe):
                for ch in range(NC):
                    tiles_scaled(pe, ln_x, 4 * ch + 4)
                    for t in range(4):
                        last = nc.tensor.transpose(psum[:, 4 + ch, P * t:P * t + P], xn[:, 4 * ch + t, :], c["ident"][:, :])
                    last.then_inc(tp_done, 1)
                pe.wait_ge(loaded, 16 * len(loads))

                def project(ch):
                    pe.wait_ge(xt_ready, ch + 1)
                    if ch >= 1:
                        pe.wait_ge(xin_ready, NB * ch)
                        pe.wait_ge(gate_ready, NB * ch)
                    for b in range(2 * NB):
                        nc.tensor.matmul(psum[:, b, :], w_in[:, P * b:P * b + P], xt[:, W * ch:W * ch + W], start=True, stop=True).then_inc(in_done, 1)

                def inputs(ch):
                    pe.wait_ge(u_ready, NB * (ch + 1))
                    if ch >= 1:
                        pe.wait_ge(bu_ready, ch)
                    for b in range(NB):
                        last = nc.tensor.matmul(psum[0:S, 4, :], wb[:, b, :], u[:, b, W * ch:W * ch + W], start=(b == 0), stop=(b == NB - 1))
                    last.then_inc(bu_done, 1)

                def outputs(ch):
                    pe.wait_ge(hs_ready, ch + 1)
                    if ch >= 1:
                        pe.wait_ge(yd_ready, NB * ch)
                    for b in range(NB):
                        nc.tensor.matmul(psum[:, 5 + b, :], wc[:, P * b:P * b + P], hs[:, W * ch:W * ch + W], start=True, stop=True).then_inc(y_done, 1)

                def out(ch):
                    pe.wait_ge(yg_ready, NB * (ch + 1))
                    if ch >= 1:
                        pe.wait_ge(z_ready, ch)
                    for t in range(4):
                        for b in range(NB):
                            last = nc.tensor.matmul(psum[:, 7, P * t:P * t + P], yg[:, b, W * ch + P * t:W * ch + P * t + P], wo[:, b, :], start=(b == 0), stop=(b == NB - 1))
                    last.then_inc(o_done, 1)

                project(0)
                project(1)
                pe.wait_ge(xt_ready, NC)
                for ch in range(NC):
                    inputs(ch)
                    if ch + 2 < NC:
                        project(ch + 2)
                    if ch >= 1:
                        out(ch - 1)
                    outputs(ch)
                out(NC - 1)

            @block.scalar
            def _(act):
                ln_x.root(act)
                scale_on_act(act, ln_x, lambda t: xn[:, t, :], lambda t: x[:, t, :])
                for ch in range(NC):
                    act.wait_ge(tp_done, ch + 1)
                    nc.scalar.copy(xt[:, W * ch:W * ch + W], psum[:, 4 + ch, :]).then_inc(xt_ready, 1)

                def take_x(ch):
                    for b in range(NB):
                        act.wait_ge(in_done, 2 * NB * ch + b + 1)
                        nc.scalar.copy(xin[:, b, K - 1 + W * ch:K - 1 + W * ch + W], psum[:, b, :])
                        nc.scalar.activation(u[:, b, W * ch:W * ch + W], psum[:, b, :], ACT.Identity, bias=cb[:, b:b + 1], scale=cw[:, b, K - 1:K]).then_inc(xin_ready, 1)

                def take_gate(ch):
                    for b in range(NB):
                        act.wait_ge(in_done, 2 * NB * ch + NB + b + 1)
                        nc.scalar.activation(gate[:, b, W * ch:W * ch + W], psum[:, NB + b, :], ACT.Silu).then_inc(gate_ready, 1)

                act.wait_ge(loaded, 16 * len(loads))
                take_x(0)
                take_gate(0)
                take_x(1)
                for ch in range(NC):
                    for b in range(NB):
                        act.wait_ge(conv_done, NB * ch + b + 1)
                        part = u[:, b, W * ch:W * ch + W]
                        nc.scalar.activation(part, part, ACT.Silu).then_inc(u_ready, 1)
                    if ch + 1 < NC:
                        take_gate(ch + 1)
                    act.wait_ge(bu_done, ch + 1)
                    nc.scalar.mul(bu[:, W * ch:W * ch + W], psum[0:S, 4, :], 0.05).then_inc(bu_ready, 1)
                    if ch + 2 < NC:
                        take_x(ch + 2)
                ln_z.root(act)
                ln_o.root(act)
                scale_on_act(act, ln_o, lambda t: z[:, t, :], lambda t: z[:, t, :])

            @block.gpsimd
            def _(g):
                for ch in range(NC):
                    for b in range(NB):
                        g.wait_ge(yd_ready, NB * ch + b + 1)
                        g.wait_ge(gate_ready, NB * ch + b + 1)
                        part = yg[:, b, W * ch:W * ch + W]
                        nc.gpsimd.tensor_tensor(part, part, gate[:, b, W * ch:W * ch + W], ALU.mult).then_inc(yg_ready, 1)
                add_act_tiles(g, ln_o, x, lambda t: z[:, t, :])

            @block.vector
            def _(dve):
                v = nc.vector
                for t in range(NT):
                    ln_x.tile_stats(t, x[:, t, :])
                v.memset(decay[:, :], 0.95)
                v.memset(xin[:, :, 0:K - 1], 0.0).then_inc(pads, 1)
                dve.wait_ge(pads, 1)
                ln_x.finish(dve)
                scale_on_dve(ln_x, lambda t: xn[:, t, :], lambda t: x[:, t, :])
                dve.wait_ge(loaded, 16 * len(loads))

                def convolve(ch):
                    dve.wait_ge(xin_ready, NB * (ch + 1))
                    tap_at = [0] * NB
                    for k in range(K - 2, -1, -1):
                        for b in range(NB):
                            tap = xin[:, b, W * ch + k:W * ch + k + W]
                            acc = u[:, b, W * ch:W * ch + W]
                            if k < K - 2:
                                dve.wait_ge(cch.sem, tap_at[b])
                            ins = v.scalar_tensor_tensor(out=acc, in0=tap, scalar=cw[:, b, k:k + 1], in1=acc, op0=ALU.mult, op1=ALU.add)
                            if k == 0:
                                ins.then_inc(conv_done, 1)
                            else:
                                tap_at[b] = cch.up(ins)

                def recur(ch):
                    dve.wait_ge(bu_ready, ch + 1)
                    if ch >= 1:
                        dve.wait_ge(hs_ready, ch)
                    start = hs[:, W * ch - 1:W * ch] if ch else 0.0
                    v.tensor_tensor_scan(hs[:, W * ch:W * ch + W], decay[:, :], bu[:, W * ch:W * ch + W], start, ALU.mult, ALU.add).then_inc(hs_ready, 1)

                def skip(ch):
                    for b in range(NB):
                        dve.wait_ge(y_done, NB * ch + b + 1)
                        v.scalar_tensor_tensor(out=yg[:, b, W * ch:W * ch + W], in0=u[:, b, W * ch:W * ch + W], scalar=dp[:, b:b + 1], in1=psum[:, 5 + b, :],
                                               op0=ALU.mult, op1=ALU.add).then_inc(yd_ready, 1)

                def residual(ch):
                    dve.wait_ge(o_done, ch + 1)
                    if ch == 0:
                        dve.wait_ge(ln_x.by_act, NT // 2)
                    v.tensor_tensor(z[:, 4 * ch:4 * ch + 4, :], psum[:, 7, :].rearrange("p (t n) -> p t n", t=4), xn[:, 4 * ch:4 * ch + 4, :], ALU.add).then_inc(z_ready, 1)
                    dve.wait_ge(z_ready, ch + 1)
                    for t in range(4):
                        ln_z.tile_stats(4 * ch + t, z[:, 4 * ch + t, :])

                convolve(0)
                recur(0)
                for ch in range(1, NC):
                    convolve(ch)
                    skip(ch - 1)
                    if ch >= 2:
                        residual(ch - 2)
                    recur(ch)
                skip(NC - 1)
                residual(NC - 2)
                residual(NC - 1)
                ln_z.finish(dve)
                for t in range(NT):
                    och.up(v.scalar_tensor_tensor(out=z[:, t, :], in0=z[:, t, :], scalar=ln_z.tmp[:, 2, t:t + 1], in1=gamma[:, :], op0=ALU.subtract, op1=ALU.mult))
                base = och.n
                for t in range(NT):
                    dve.wait_ge(och.sem, base - NT + t + 1)
                    och.up(v.scalar_tensor_tensor(out=z[:, t, :], in0=z[:, t, :], scalar=ln_z.tmp[:, 6, t:t + 1], in1=beta[:, :], op0=ALU.mult, op1=ALU.add))
                for t in range(NT):
                    dve.wait_ge(och.sem, base + t + 1)
                    ln_o.tile_stats(t, z[:, t, :])
                ln_o.finish(dve)
                scale_on_dve(ln_o, lambda t: z[:, t, :], lambda t: z[:, t, :])
                add_dve_tiles(dve, ln_o, x, lambda t: z[:, t, :])


def soft_moe(nc, x, c, d, out):
    T, NT, NE, NS = 2048, 16, 64, 32
    W = 512
    SL = NE * NS
    HALF = SL // 2
    HE = NE // 2
    with ExitStack() as ctx:
        a = Alloc(nc, ctx, "mo")
        psum = a.ps("psum", [P, 8, W])
        xt = a.sb("xt", [P, T])
        phi = a.sb("phi", [P, SL])
        bcol = a.sb("bias_col", [P, SL // P])
        part_max = a.sb("part_max", [P, 2, NT, NS])
        xs_t = a.sb("xs_t", [P, SL])
        mp_t = a.sb("neg_max_t", [P, T], BF16)
        ew = a.sb("expert_w", [P, NE, P])
        eb = a.sb("expert_b", [P, SL // P, P])
        experts_loaded = a.sem("experts_loaded")
        nm3 = a.sb("neg_max_parts", [P, NT, P], BF16)
        nmax = a.sb("neg_max", [P, NT, NS])
        yt = a.sb("y_slots", [P, SL // P, P])
        selp = a.sb("sel_slot", [P, P], BF16)
        blk = a.sb("same_slot", [P, P])
        sel_done = a.sem("sel_done")
        sel_n = [0]

        with ExitStack() as ctx0:
            b = Alloc(nc, ctx0, "m0")
            xn = b.sb("xn", [P, NT, P])
            bias = b.sb("bias", [SL // P, P])
            bpart = b.sb("bias_part", [SL // P, 3, P], BF16)
            b3 = b.sb("bias_parts", [96, SL], BF16)
            ones3 = b.sb("ones3", [96, P], BF16)
            xs = b.sb("x_tile", [P, 2, 2, P])
            lc = b.sb("logits", [P, 2, 2, HE, NS])
            ls = b.sb("exps", [P, 2, 2, HE, NS])
            dn = b.sb("dispatch", [P, 2, 2, HE, NS])
            mn = b.sb("max", [P, 2, 2, HE])
            sm = b.sb("sum", [P, 2, 2, HE])
            rs = b.sb("rsum", [P, 2, 2, HE])
            ln = Norm(nc, b, "ln", NT)
            loaded, zeroed, tp_done, xt_ready, b_ready = (b.sem(s) for s in ("loaded", "zeroed", "tp_done", "xt_ready", "b_ready"))
            stg_t, stg_n, l_done, lc_ready, slot_maxed, maxed, sub_done, exp_done, summed, r_ready, d_ready, x_done = (b.sem(s) for s in (
                "staged_t", "staged", "l_psum", "l_ready", "slot_maxed", "maxed", "sub_done", "exp_done", "summed", "r_ready", "d_ready", "x_psum"))
            xs_ready, bias_loaded, parts_ready, bounced = (b.sem(s) for s in ("xs_ready", "bias_loaded", "parts_ready", "bounced"))
            scratch = nc.dram_tensor("bias_scratch", [3, SL], BF16).ap()
            bch = Count(b.sem("bias_chain"))

            def steps(eng, body):
                body(0, 0)
                body(1, 1)
                with eng.Fori(1, NT // 2 - 1) as i:
                    body(2 * i, 0)
                    body(2 * i + 1, 1)
                body(NT - 2, 0)
                body(NT - 1, 1)

            early = lambda z, n: isinstance(z, int) and z < n

            with nc.Block() as block:
                @block.sync
                def _(sp):
                    sp.dma_start(bias[:, :], d["phi_b"].rearrange("o (a b) -> (o a) b", b=P)).then_inc(bias_loaded, 16)
                    sp.dma_start(phi[:, :], d["phi"]).then_inc(loaded, 16)
                    sp.dma_start(bcol[:, :], d["phi_b_col"]).then_inc(loaded, 16)
                    sp.wait_ge(zeroed, 1)
                    sp.wait_ge(parts_ready, 1)
                    sp.dma_start(scratch.rearrange("k (a b) -> a k b", b=P), bpart[:, :, :]).then_inc(bounced, 16)
                    sp.wait_ge(bounced, 16)
                    for k in range(3):
                        sp.dma_start(b3[32 * k:32 * k + 1, :], scratch[k:k + 1, :]).then_inc(b_ready, 16)
                    sp.dma_start(ew[:, :, :], d["expert_w"]).then_inc(experts_loaded, 16)
                    for k in range(4):
                        sp.dma_start(eb[32 * k:32 * k + 32, :, :], d["expert_b"].rearrange("(j n) h -> n j h", n=4)[k:k + 1].broadcast_to([32, SL // P, P]))\
                            .then_inc(experts_loaded, 16)

                @block.gpsimd
                def _(g):
                    nc.gpsimd.memset(b3[:, :], 0.0).then_inc(zeroed, 1)
                    nc.gpsimd.memset(ones3[:, :], 1.0)
                    ch = Count(sel_done)
                    nc.gpsimd.memset(blk[:, :], 0.0)
                    ch.up(nc.gpsimd.memset(selp[:, :], 0.0))
                    for k in range(3):
                        ch.settle(g)
                        ch.up(nc.gpsimd.affine_select(out=selp[:, :].rearrange("q (n p) -> q n p", n=4), in_=selp[:, :].rearrange("q (n p) -> q n p", n=4),
                                                      compare_op=ALU.not_equal, fill=1.0, base=-NS * k, pattern=[[0, 4], [-1, NS]], channel_multiplier=1))
                    for k in range(-3, 4):
                        ch.settle(g)
                        ch.up(nc.gpsimd.affine_select(out=blk[:, :], in_=blk[:, :], compare_op=ALU.not_equal,
                                                      fill=1.0, base=NS * k, pattern=[[-1, P]], channel_multiplier=1))
                    sel_n[0] = ch.n

                    def subtract(z, par, hf):
                        g.wait_ge(maxed, 2 * z + hf + 1)
                        if not early(z, 2):
                            g.wait_ge(d_ready, 2 * z + hf - 3)
                        nc.gpsimd.tensor_tensor(ls[:, par, hf, :, :], lc[:, par, hf, :, :], mn[:, par, hf, :].unsqueeze(2).broadcast_to([P, HE, NS]), ALU.subtract)\
                            .then_inc(sub_done, 1)

                    def normalise(z, par, hf):
                        g.wait_ge(r_ready, 2 * z + hf + 1)
                        if not early(z, 2):
                            g.wait_ge(x_done, 2 * z + hf - 3)
                        nc.gpsimd.tensor_tensor(dn[:, par, hf, :, :], ls[:, par, hf, :, :], rs[:, par, hf, :].unsqueeze(2).broadcast_to([P, HE, NS]), ALU.mult)\
                            .then_inc(d_ready, 1)

                    def body(z, par):
                        subtract(z, par, 0)
                        if not early(z, 1):
                            normalise(z - 1, 1 - par, 1)
                        subtract(z, par, 1)
                        normalise(z, par, 0)
                    steps(g, body)
                    normalise(NT - 1, 1, 1)

                @block.tensor
                def _(pe):
                    for ch in range(4):
                        tiles_scaled(pe, ln, 4 * ch + 4)
                        for t in range(4):
                            last = nc.tensor.transpose(psum[:, ch, P * t:P * t + P], xn[:, 4 * ch + t, :], c["ident"][:, :])
                        last.then_inc(tp_done, 1)

                    def logits(z, par, hf):
                        if hf == 0:
                            pe.wait_ge(stg_t, z + 1)
                        if not early(z, 1):
                            pe.wait_ge(lc_ready, 2 * z + hf - 1)
                        for k in range(2):
                            bank = 2 * hf + k
                            nc.tensor.matmul(psum[:, bank, :], ones3[:, :], b3[:, W * bank:W * bank + W], start=True, stop=False)
                            last = nc.tensor.matmul(psum[:, bank, :], xs[:, par, 0, :], phi[:, W * bank:W * bank + W], start=False, stop=True)
                        last.then_inc(l_done, 1)

                    def gather(z, par, hf):
                        if hf == 0:
                            pe.wait_ge(stg_n, z + 1)
                        pe.wait_ge(d_ready, 2 * z + hf + 1)
                        for k in range(2):
                            last = nc.tensor.matmul(psum[:, 4 + 2 * hf + k, :], xs[:, par, 1, :], dn[:, par, hf, :, :].rearrange("p n s -> p (n s)")[:, W * k:W * k + W],
                                                    start=early(z, 1), stop=(isinstance(z, int) and z == NT - 1))
                        last.then_inc(x_done, 1)

                    def body(z, par):
                        final = isinstance(z, int) and z == NT - 1
                        if not final:
                            logits(z + 1, 1 - par, 0)
                        if not early(z, 1):
                            gather(z - 1, 1 - par, 1)
                        if not final:
                            logits(z + 1, 1 - par, 1)
                        gather(z, par, 0)

                    pe.wait_ge(loaded, 16 * 2)
                    pe.wait_ge(b_ready, 16 * 3)
                    pe.wait_ge(sel_done, sel_n[0])
                    pe.wait_ge(xt_ready, 4)
                    logits(0, 0, 0)
                    logits(0, 0, 1)
                    steps(pe, body)
                    gather(NT - 1, 1, 1)

                @block.scalar
                def _(act):
                    ln.root(act)
                    scale_on_act(act, ln, lambda t: xn[:, t, :], lambda t: x[:, t, :])
                    for ch in range(4):
                        act.wait_ge(tp_done, ch + 1)
                        nc.scalar.copy(xt[:, W * ch:W * ch + W], psum[:, ch, :]).then_inc(xt_ready, 1)

                    def stage_t(z, par):
                        if not early(z, 2):
                            act.wait_ge(l_done, 2 * z - 2)
                        nc.scalar.copy(xs[:, par, 0, :], xt[:, bass.ds(z * P, P)]).then_inc(stg_t, 1)

                    def stage_n(z, par):
                        if not early(z, 2):
                            act.wait_ge(x_done, 2 * z - 2)
                        nc.scalar.copy(xs[:, par, 1, :].unsqueeze(1), xn[:, bass.ds(z, 1), :]).then_inc(stg_n, 1)

                    def take(z, par, hf):
                        act.wait_ge(l_done, 2 * z + hf + 1)
                        if not early(z, 2):
                            act.wait_ge(sub_done, 2 * z + hf - 3)
                            act.wait_ge(slot_maxed, 2 * z + hf - 3)
                        nc.scalar.copy(lc[:, par, hf, :, :].rearrange("p n s -> p (n s)"), psum[:, 2 * hf:2 * hf + 2, :].rearrange("p b n -> p (b n)")).then_inc(lc_ready, 1)

                    def exps(z, par, hf):
                        act.wait_ge(sub_done, 2 * z + hf + 1)
                        part = ls[:, par, hf, :, :].rearrange("p n s -> p (n s)")
                        nc.scalar.activation(part, part, ACT.Exp).then_inc(exp_done, 1)

                    def body(z, par):
                        final = isinstance(z, int) and z == NT - 1
                        exps(z, par, 0)
                        if not final:
                            take(z + 1, 1 - par, 0)
                        stage_n(z, par)
                        exps(z, par, 1)
                        if not final:
                            take(z + 1, 1 - par, 1)
                            if not (isinstance(z, int) and z == NT - 2):
                                stage_t(z + 2, par)

                    act.wait_ge(xt_ready, 4)
                    tiles_scaled(act, ln, NT)
                    stage_t(0, 0)
                    stage_t(1, 1)
                    take(0, 0, 0)
                    take(0, 0, 1)
                    steps(act, body)

                @block.vector
                def _(dve):
                    v = nc.vector
                    for t in range(NT):
                        ln.tile_stats(t, x[:, t, :])
                    dve.wait_ge(bias_loaded, 16)
                    bch.up(v.tensor_copy(bpart[:, 0, :], bias[:, :]))
                    bch.settle(dve)
                    bch.up(v.tensor_tensor(bias[:, :], bias[:, :], bpart[:, 0, :], ALU.subtract))
                    bch.settle(dve)
                    bch.up(v.tensor_copy(bpart[:, 1, :], bias[:, :]))
                    bch.settle(dve)
                    v.tensor_tensor(bpart[:, 2, :], bias[:, :], bpart[:, 1, :], ALU.subtract).then_inc(parts_ready, 1)
                    ln.finish(dve)
                    scale_on_dve(ln, lambda t: xn[:, t, :], lambda t: x[:, t, :])
                    def reduce(z, par, hf):
                        dve.wait_ge(lc_ready, 2 * z + hf + 1)
                        if not early(z, 2):
                            dve.wait_ge(sub_done, 2 * z + hf - 3)
                        v.tensor_reduce(mn[:, par, hf, :], lc[:, par, hf, :, :], AX_X, ALU.max).then_inc(maxed, 1)
                        v.tensor_reduce(part_max[:, hf, bass.ds(z, 1), :].rearrange("p o s -> p (o s)"), lc[:, par, hf, :, :].rearrange("p n s -> p s n"), AX_X, ALU.max)\
                            .then_inc(slot_maxed, 1)

                    def sums(z, par, hf):
                        dve.wait_ge(exp_done, 2 * z + hf + 1)
                        v.tensor_reduce(sm[:, par, hf, :], ls[:, par, hf, :, :], AX_X, ALU.add).then_inc(summed, 1)
                        dve.wait_ge(summed, 2 * z + hf + 1)
                        if not early(z, 2):
                            dve.wait_ge(d_ready, 2 * z + hf - 3)
                        v.reciprocal(rs[:, par, hf, :], sm[:, par, hf, :]).then_inc(r_ready, 1)

                    def body(z, par):
                        reduce(z, par, 0)
                        if not early(z, 1):
                            sums(z - 1, 1 - par, 1)
                        reduce(z, par, 1)
                        sums(z, par, 0)
                    steps(dve, body)
                    sums(NT - 1, 1, 1)
                    v.memset(nm3[:, :, 3 * NS:P], 0.0)
                    dve.wait_ge(slot_maxed, 2 * NT)
                    bch.up(v.tensor_tensor(nmax[:, :, :], part_max[:, 0, :, :], part_max[:, 1, :, :], ALU.max))
                    bch.settle(dve)
                    bch.up(v.tensor_scalar(nmax[:, :, :], nmax[:, :, :], -1.0, None, ALU.mult))
                    for k in range(2):
                        bch.settle(dve)
                        bch.up(v.tensor_copy(nm3[:, :, NS * k:NS * k + NS], nmax[:, :, :]))
                        bch.settle(dve)
                        bch.up(v.tensor_tensor(nmax[:, :, :], nmax[:, :, :], nm3[:, :, NS * k:NS * k + NS], ALU.subtract))
                    bch.settle(dve)
                    v.tensor_copy(nm3[:, :, 2 * NS:3 * NS], nmax[:, :, :])
                    dve.wait_ge(x_done, 2 * NT)
                    for k in range(4):
                        v.tensor_scalar(xs_t[:, W * k:W * k + W], psum[:, 4 + k, :], -33000.0, 65000.0, ALU.max, ALU.min).then_inc(xs_ready, 1)

        with ExitStack() as ctx1:
            b = Alloc(nc, ctx1, "m1")
            xh = b.sb("x_hat", [P, NT, P])
            xh_t = b.sb("x_hat_t", [P, SL])
            ln = Norm(nc, b, "ln", NT)
            nat_done, xh_ready, tanh_done, back_done, back_ready, yt_done, yt_ready, mp_done, mp_ready = (b.sem(s) for s in (
                "nat_psum", "xh_ready", "tanh_done", "back_psum", "back_ready", "yt_psum", "yt_ready", "mp_psum", "mp_ready"))
            with nc.Block() as block:
                @block.tensor
                def _(pe):
                    for t in range(NT):
                        last = nc.tensor.transpose(psum[:, t // 4, P * (t % 4):P * (t % 4) + P], xs_t[:, P * t:P * t + P], c["ident"][:, :])
                        if t % 4 == 3:
                            last.then_inc(nat_done, 1)
                    for q in range(4):
                        bank = psum[:, 4 + q, 0:256].bitcast(BF16)
                        for t in range(4):
                            last = nc.tensor.transpose(bank[:, P * t:P * t + P], nm3[:, 4 * q + t, :], c["identb"][:, :])
                        last.then_inc(mp_done, 1)
                    for q in range(4):
                        pe.wait_ge(tanh_done, 4 * q + 4)
                        for t in range(4 * q, 4 * q + 4):
                            last = nc.tensor.transpose(psum[:, q, P * (t % 4):P * (t % 4) + P], xh[:, t, :], c["ident"][:, :])
                        last.then_inc(back_done, 1)
                    pe.wait_ge(experts_loaded, 80)
                    pe.wait_ge(mp_ready, 4)
                    for q in range(4):
                        pe.wait_ge(back_ready, q + 1)
                        for j in range(4):
                            for k in range(4):
                                n = 16 * q + 4 * j + k
                                last = nc.tensor.matmul(psum[32 * k:32 * k + 32, 4 + q, P * j:P * j + P], xh_t[:, NS * n:NS * n + NS], ew[:, n, :], start=True, stop=True)
                        last.then_inc(yt_done, 1)

                @block.scalar
                def _(act):
                    ln.root(act)
                    for q in range(4):
                        for t in range(4 * q, 4 * q + 4):
                            act.wait_ge(xh_ready, t + 1)
                            nc.scalar.activation(xh[:, t, :], xh[:, t, :], ACT.Tanh).then_inc(tanh_done, 1)
                        act.wait_ge(mp_done, q + 1)
                        nc.scalar.copy(mp_t[:, W * q:W * q + W], psum[:, 4 + q, 0:256].bitcast(BF16)).then_inc(mp_ready, 1)
                    for q in range(4):
                        act.wait_ge(back_done, q + 1)
                        nc.scalar.copy(xh_t[:, W * q:W * q + W], psum[:, q, :]).then_inc(back_ready, 1)

                @block.vector
                def _(dve):
                    v = nc.vector
                    tile = lambda t: psum[:, t // 4, P * (t % 4):P * (t % 4) + P]
                    for t in range(NT):
                        if t % 4 == 0:
                            dve.wait_ge(nat_done, t // 4 + 1)
                        ln.tile_stats(t, tile(t))
                    ln.finish(dve)
                    for t in range(NT):
                        ln.scale(t, xh[:, t, :], tile(t)).then_inc(xh_ready, 1)
                    dve.wait_ge(experts_loaded, 80)
                    for q in range(4):
                        dve.wait_ge(yt_done, q + 1)
                        v.tensor_tensor(yt[:, 4 * q:4 * q + 4, :], psum[:, 4 + q, :].rearrange("p (j h) -> p j h", j=4), eb[:, 4 * q:4 * q + 4, :], ALU.add)\
                            .then_inc(yt_ready, 1)

        with ExitStack() as ctx2:
            b = Alloc(nc, ctx2, "m2")
            NJ = SL // P
            ec = b.sb("exp", [P, 2, NJ, W])
            tot = b.sb("total", [P, 2, W])
            rt = b.sb("rtotal", [P, 2, W])
            y_t = b.sb("y_t", [P, T])
            y = b.sb("y", [P, NT, P])
            ln = Norm(nc, b, "ln", NT, in_psum=True)
            l_done, exp_done, added, tot_done, rt_ready, scaled, y_done, yt_ready, nat_done, o_ready, stored = (b.sem(s) for s in (
                "l_psum", "exp_done", "added", "tot_psum", "rt_ready", "scaled", "y_psum", "yt_ready", "nat_psum", "o_ready", "stored"))
            o_late = b.sem("o_late")
            tile = lambda t: psum[:, t // 4, P * (t % 4):P * (t % 4) + P]
            NCH = T // W
            with nc.Block() as block:
                @block.tensor
                def _(pe):
                    def logits(ch, j):
                        n = NJ * ch + j
                        if n >= 4:
                            pe.wait_ge(exp_done, n - 3)
                        cols = slice(W * ch, W * ch + W)
                        nc.tensor.matmul(psum[:, n % 4, :], selp[:, :], mp_t[:, cols], start=True, stop=False)
                        nc.tensor.matmul(psum[:, n % 4, :], phi[:, P * j:P * j + P], xt[:, cols], start=False, stop=True).then_inc(l_done, 1)

                    def total(ch):
                        pe.wait_ge(added, (NJ - 1) * (ch + 1))
                        if ch >= 1:
                            pe.wait_ge(rt_ready, ch)
                        nc.tensor.matmul(psum[:, 4, :], blk[:, :], tot[:, ch % 2, :], start=True, stop=True).then_inc(tot_done, 1)

                    def combine(ch, j):
                        if ch >= 2 and j == 0:
                            pe.wait_ge(yt_ready, ch - 1)
                        pe.wait_ge(scaled, NJ * ch + j + 1)
                        ins = nc.tensor.matmul(psum[:, 5 + ch % 2, :], yt[:, j, :], ec[:, ch % 2, j, :], start=(j == 0), stop=(j == NJ - 1))
                        ins.then_inc(y_done, 1)

                    AHEAD = 4
                    for j in range(NJ):
                        logits(0, j)
                    for ch in range(NCH):
                        if ch + 1 < NCH:
                            for j in range(AHEAD):
                                logits(ch + 1, j)
                                if j == 0:
                                    total(ch)
                        else:
                            total(ch)
                        for j in range(NJ):
                            if ch + 1 < NCH and j + AHEAD < NJ:
                                logits(ch + 1, j + AHEAD)
                            combine(ch, j)
                    pe.wait_ge(yt_ready, NCH)
                    for t in range(NT):
                        last = nc.tensor.transpose(psum[:, t // 4, P * (t % 4):P * (t % 4) + P], y_t[:, P * t:P * t + P], c["ident"][:, :])
                        if t % 4 == 3:
                            last.then_inc(nat_done, 1)

                @block.scalar
                def _(act):
                    for ch in range(NCH):
                        for j in range(NJ):
                            n = NJ * ch + j
                            act.wait_ge(l_done, n + 1)
                            if ch >= 2:
                                act.wait_ge(y_done, n - 2 * NJ + 1)
                                act.wait_ge(added, (NJ - 1) * (ch - 1))
                            nc.scalar.activation(ec[:, ch % 2, j, :], psum[:, n % 4, :], ACT.Exp, bias=bcol[:, j:j + 1], scale=1.0).then_inc(exp_done, 1)
                        if ch >= 1:
                            act.wait_ge(y_done, NJ * ch)
                            nc.scalar.copy(y_t[:, W * (ch - 1):W * ch], psum[:, 5 + (ch - 1) % 2, :]).then_inc(yt_ready, 1)
                    act.wait_ge(y_done, NJ * NCH)
                    nc.scalar.copy(y_t[:, W * (NCH - 1):W * NCH], psum[:, 5 + (NCH - 1) % 2, :]).then_inc(yt_ready, 1)
                    ln.root(act)
                    scale_on_act(act, ln, lambda t: y[:, t, :], tile)

                @block.vector
                def _(dve):
                    v = nc.vector

                    def add(ch, j):
                        dve.wait_ge(exp_done, NJ * ch + j + 1)
                        if j == 0:
                            return
                        if j == 1:
                            if ch >= 2:
                                dve.wait_ge(tot_done, ch - 1)
                            in0 = ec[:, ch % 2, 0, :]
                        else:
                            dve.wait_ge(added, (NJ - 1) * ch + j - 1)
                            in0 = tot[:, ch % 2, :]
                        v.tensor_tensor(tot[:, ch % 2, :], in0, ec[:, ch % 2, j, :], ALU.add).then_inc(added, 1)

                    for j in range(NJ):
                        add(0, j)
                    for ch in range(NCH):
                        dve.wait_ge(tot_done, ch + 1)
                        if ch >= 2:
                            dve.wait_ge(scaled, NJ * (ch - 1))
                        v.reciprocal(rt[:, ch % 2, :], psum[:, 4, :]).then_inc(rt_ready, 1)
                        dve.wait_ge(rt_ready, ch + 1)
                        for j in range(NJ):
                            v.tensor_tensor(ec[:, ch % 2, j, :], ec[:, ch % 2, j, :], rt[:, ch % 2, :], ALU.mult).then_inc(scaled, 1)
                            if ch + 1 < NCH:
                                add(ch + 1, j)
                    for t in range(NT):
                        if t % 4 == 0:
                            dve.wait_ge(nat_done, t // 4 + 1)
                        ln.tile_stats(t, tile(t))
                    ln.finish(dve)
                    scale_on_dve(ln, lambda t: y[:, t, :], tile)
                    add_dve_tiles(dve, ln, x, lambda t: y[:, t, :], o_ready)

                @block.gpsimd
                def _(g):
                    add_act_tiles(g, ln, x, lambda t: y[:, t, :], o_late)

                @block.sync
                def _(sp):
                    for q in range(4):
                        sp.wait_ge(o_ready if q < 2 else o_late, 4 * (q % 2) + 4)
                        sp.dma_start(out.rearrange("(t p) c -> p t c", p=P)[:, 4 * q:4 * q + 4, :], x[:, 4 * q:4 * q + 4, :]).then_inc(stored, 16)
                    sp.wait_ge(stored, 64)


def sandwich(nc, args, out):
    with ExitStack() as ctx:
        a = Alloc(nc, ctx, "all")
        x = a.sb("x", [P, 16, P])
        consts = dict(ident=a.sb("ident", [P, P]), identb=a.sb("ident_bf16", [P, P], BF16))
        with ExitStack() as ctx0:
            b = Alloc(nc, ctx0, "band")
            consts["mask"] = b.sb("mask", [P, 2, 256], BF16)
            consts["sel"] = b.sb("select", [P, 16, P], BF16)
            attention(nc, x, consts, args)
        kmoe(nc, x, consts, args)
        ssm(nc, x, consts, args)
        soft_moe(nc, x, consts, args, out)


def kernel(**inputs):
    import numpy as np
    from concourse import bacc
    from concourse.bass_utils import run_bass_kernel_spmd

    first = {name[len("L0_attn_"):]: np.asarray(v) for name, v in inputs.items() if name.startswith("L0_attn_")}
    moe = {name[len("L0_ffn_"):]: np.asarray(v) for name, v in inputs.items() if name.startswith("L0_ffn_")}
    mix = {name[len("L1_attn_"):]: np.asarray(v) for name, v in inputs.items() if name.startswith("L1_attn_")}
    soft = {name[len("L1_ffn_"):]: np.asarray(v) for name, v in inputs.items() if name.startswith("L1_ffn_")}
    laid = {
        "x": first["x"].reshape(2048, 128),
        "ident": np.eye(128, dtype=np.float32),
        "wqkv": first["Wqkv"], "bqkv": first["bqkv"], "wout": first["Wout"], "bout": first["bout"],
        "expert_ids": np.arange(64, dtype=np.float32).reshape(1, 64),
        "w_up": moe["W_up"].reshape(64, 8, 128).transpose(2, 1, 0),
        "b_up": moe["B_up"],
        "a_up": moe["A_up"],
        "w_down": moe["W_down"].reshape(64, 64, 64).transpose(2, 1, 0),
        "b_down": moe["B_down"],
        "a_down": moe["A_down"],
        "bias_up": moe["bias_up"].reshape(64, 64).T,
        "bias_down": moe["bias_down"].reshape(32, 32).T,
        "scale_up": moe["scale_up"].reshape(1, 1),
        "scale_down": moe["scale_down"].reshape(1, 1),
        "w_in": mix["W_in"].T,
        "conv_w": mix["conv_w"].reshape(2, 128, 4).transpose(1, 0, 2),
        "conv_b": mix["conv_b"].reshape(2, 128).T,
        "w_b": mix["W_B"].reshape(64, 2, 128).transpose(2, 1, 0),
        "w_c": mix["W_C"].T,
        "d_param": mix["D_param"].reshape(2, 128).T,
        "w_out": mix["W_out"].reshape(128, 2, 128).transpose(2, 1, 0),
        "gamma": mix["ln_gamma"].reshape(1, 128),
        "beta": mix["ln_beta"].reshape(1, 128),
        "phi": soft["phi_w"].T,
        "phi_b": soft["phi_b"].reshape(1, 2048),
        "phi_b_col": soft["phi_b"].reshape(16, 128).T,
        "expert_w": soft["expert_w"].transpose(1, 0, 2),
        "expert_b": soft["expert_b"],
    }
    nc = bacc.Bacc("TRN2", target_bir_lowering=False, num_devices=1)
    arrays, args = {}, {}
    for name, v in laid.items():
        arrays["in_" + name] = np.ascontiguousarray(v)
        args[name] = nc.dram_tensor("in_" + name, v.shape, F32, kind="ExternalInput").ap()
    out = nc.dram_tensor("out_rows", [2048, 128], F32, kind="ExternalOutput").ap()
    sandwich(nc, args, out)
    result = run_bass_kernel_spmd(nc, [arrays], core_ids=[0])
    return result.results[0]["out_rows"].reshape(1, 2048, 128)
```
